# Optimizing a Trainium2 kernel written in Bass

```python
import numpy as np
import jax
import jax.numpy as jnp

def _softmax(x, axis=-1):
    return jax.nn.softmax(x, axis=axis)

def _gelu(x):
    return jax.nn.gelu(x, approximate=True)

def _silu(x):
    return jax.nn.silu(x)

def _sigmoid(x):
    return jax.nn.sigmoid(x)

def _layernorm(x, axis=-1, eps=1e-05):
    m = jnp.mean(x, axis=axis, keepdims=True)
    v = jnp.var(x, axis=axis, keepdims=True)
    return (x - m) / jnp.sqrt(v + eps)

def _scatter_add(tgt, idx, src, axis=0):
    return tgt.at[idx].add(src)

def _segment_sum(src, seg, n):
    return jax.ops.segment_sum(src, seg, n)
kernel_name = 'mk_flamingo_gated_d4_seqx_r4_cb7a61'

def setup_inputs(seed: int=0):
    np.random.seed(seed)
    _w = jnp.asarray

    def _rec_inputs():
        import jax
        import jax.numpy as jnp
        _rk = jax.random.key(seed)
        x = -0.0003929 + 0.9999 * jax.random.normal(jax.random.fold_in(_rk, 1), (2, 1024, 256), jnp.float32)
        _lenS = 1024 - jax.random.randint(jax.random.fold_in(_rk, 7), (2,), 0, max(1, 1024 // 4) + 1, jnp.int32)
        _lenS2 = 77 - jax.random.randint(jax.random.fold_in(_rk, 8), (2,), 0, max(1, 77 // 4) + 1, jnp.int32)
        _ctx_1024P = jax.random.normal(jax.random.fold_in(_rk, 11), (2, 16, 256), jnp.float32)
        _ctx_1024c = jax.random.dirichlet(jax.random.fold_in(_rk, 511), 0.3 * jnp.ones((16,), jnp.float32), (2, 77))
        _ctx_1024t = jnp.einsum('bsk,bkd->bsd', _ctx_1024c, _ctx_1024P)
        _ctx_1024t = _ctx_1024t * jax.lax.rsqrt(jnp.mean(jnp.square(_ctx_1024t)) + 1e-12) * 0.953939
        ctx_1024 = 2.81802e-05 + 1.00001 * (_ctx_1024t + 0.3 * jax.random.normal(jax.random.fold_in(_rk, 611), (2, 77, 256), jnp.float32))
        _validS = jnp.arange(1024)[None, :] < _lenS[:, None]
        _validS2 = jnp.arange(77)[None, :] < _lenS2[:, None]
        _causal = jnp.tril(jnp.ones((1024, 1024), dtype=bool))
        mask_BxS2x1_ff1 = jnp.where(jnp.ones((2, 77, 1), dtype=bool), 1.0, 0.0).astype(jnp.float32)
        mask_Bx1x1xS2_fk0 = jnp.where(jnp.broadcast_to(_validS2[:, None, None, :], (2, 1, 1, 77)), 0.0, 1.0).astype(jnp.float32)
        mask_BxS2_ik0 = jnp.where(jnp.broadcast_to(_validS2[:, :], (2, 77)), 0, 1).astype(jnp.int32)
        _g = jax.random.normal(jax.random.fold_in(_rk, 9001), (2, 4), jnp.float32)
        _g = jnp.sign(_g) * jnp.maximum(jnp.abs(_g), 1.0) + (_g == 0) * 1.0
        g_xattn = _g[0]
        g_ffn = _g[1]
        return (x, ctx_1024, mask_BxS2x1_ff1, mask_Bx1x1xS2_fk0, mask_BxS2_ik0, g_xattn, g_ffn)
    x, ctx_1024, mask_BxS2x1_ff1, mask_Bx1x1xS2_fk0, mask_BxS2_ik0, g_xattn, g_ffn = _rec_inputs()

    def _L0_xattn_setup():
        import jax, jax.numpy as jnp
        import numpy as np
        B, S, U = (4, 1024, 256)
        key = jax.random.key(seed)
        ks = jax.random.split(key, 8)
        scale = 1.0 / np.sqrt(U)
        return {'query': jax.random.normal(ks[0], (B, S, U), dtype=jnp.float32), 'key': jax.random.normal(ks[1], (B, S, U), dtype=jnp.float32), 'value': jax.random.normal(ks[2], (B, S, U), dtype=jnp.float32), 'mask': jnp.ones((B, S, 1), dtype=jnp.float32), 'Wk': jax.random.normal(ks[3], (U, U), dtype=jnp.float32) * scale, 'Wv': jax.random.normal(ks[4], (U, U), dtype=jnp.float32) * scale, 'Wq': jax.random.normal(ks[5], (U, U), dtype=jnp.float32) * scale, 'Wo': jax.random.normal(ks[6], (U, U), dtype=jnp.float32) * scale}
    _L0_xattn_all = _L0_xattn_setup()
    _L0_xattn_in = {k: v for k, v in _L0_xattn_all.items() if k in ('Wk', 'Wv', 'Wq', 'Wo')}
    del _L0_xattn_all

    def _L0_ffn_setup():
        import jax, jax.numpy as jnp
        import numpy as np
        import math
        D_IN = 256
        FEATURES = (1024, 1024, 256)
        BATCH, SEQ = (8, 512)

        def _conn_dense(kernel_bool, x):
            w = jnp.where(kernel_bool, jnp.float32(1.0), jnp.float32(-1.0))
            return x @ w
        key = jax.random.key(seed)
        kx, kk0, kk1, kk2 = jax.random.split(key, 4)
        x = jax.random.normal(kx, (BATCH, SEQ, D_IN), dtype=jnp.float32)
        k0 = jax.random.randint(kk0, (2 * D_IN, FEATURES[0]), 0, 2).astype(jnp.bool_)
        k1 = jax.random.randint(kk1, (FEATURES[0], FEATURES[1]), 0, 2).astype(jnp.bool_)
        k2 = jax.random.randint(kk2, (FEATURES[1], FEATURES[2]), 0, 2).astype(jnp.bool_)
        s0 = jnp.asarray(1.0 / math.sqrt(2 * D_IN), dtype=jnp.float32)
        s1 = jnp.asarray(1.0 / math.sqrt(FEATURES[0]), dtype=jnp.float32)
        s2 = jnp.asarray(1.0 / math.sqrt(FEATURES[1]), dtype=jnp.float32)
        return {'x': x, 'k0': k0, 'k1': k1, 'k2': k2, 's0': s0, 's1': s1, 's2': s2}
    _L0_ffn_all = _L0_ffn_setup()
    _L0_ffn_in = {k: v for k, v in _L0_ffn_all.items() if k in ('k0', 'k1', 'k2', 's0', 's1', 's2')}
    del _L0_ffn_all

    def _L1_xattn_setup():
        import jax, jax.numpy as jnp
        import numpy as np
        B, S, D, H = (2, 512, 256, 16)
        DH = D // H

        def _split_heads(x):
            b, s, _ = x.shape
            return x.reshape(b, s, H, DH).transpose(0, 2, 1, 3)
        key = jax.random.key(seed)
        ks = jax.random.split(key, 8)
        scale = 0.02
        return {'query': jax.random.normal(ks[0], (B, S, D), jnp.float32), 'key': jax.random.normal(ks[1], (B, S, D), jnp.float32), 'value': jax.random.normal(ks[2], (B, S, D), jnp.float32), 'mask': jax.random.randint(ks[3], (B, 1, 1, S), 0, 2).astype(jnp.float32), 'Wq': jax.random.normal(ks[4], (D, D), jnp.float32) * scale, 'bq': jnp.zeros((D,), jnp.float32), 'Wk': jax.random.normal(ks[5], (D, D), jnp.float32) * scale, 'bk': jnp.zeros((D,), jnp.float32), 'Wv': jax.random.normal(ks[6], (D, D), jnp.float32) * scale, 'bv': jnp.zeros((D,), jnp.float32), 'Wo': jax.random.normal(ks[7], (D, D), jnp.float32) * scale, 'bo': jnp.zeros((D,), jnp.float32)}
    _L1_xattn_all = _L1_xattn_setup()
    _L1_xattn_in = {k: v for k, v in _L1_xattn_all.items() if k in ('Wq', 'bq', 'Wk', 'bk', 'Wv', 'bv', 'Wo', 'bo')}
    del _L1_xattn_all

    def _L1_ffn_setup():
        import jax, jax.numpy as jnp
        import numpy as np
        D, F, E, K = (256, 688, 8, 2)
        key = jax.random.key(seed)
        k0, k1, k2, k3, k4 = jax.random.split(key, 5)
        s = 0.02
        x = jax.random.normal(k0, (2, 128, D), jnp.float32)
        Ws = jax.random.normal(k1, (D, E), jnp.float32) * s
        bs = jnp.zeros((E,), jnp.float32)
        Wg = jax.random.normal(k2, (E, D, F), jnp.float32) * s
        Wu = jax.random.normal(k3, (E, D, F), jnp.float32) * s
        Wd = jax.random.normal(k4, (E, F, D), jnp.float32) * s
        return {'x': x, 'Ws': Ws, 'bs': bs, 'Wg': Wg, 'Wu': Wu, 'Wd': Wd}
    _L1_ffn_all = _L1_ffn_setup()
    _L1_ffn_in = {k: v for k, v in _L1_ffn_all.items() if k in ('Ws', 'bs', 'Wg', 'Wu', 'Wd')}
    del _L1_ffn_all

    def _L2_xattn_setup():
        import jax, jax.numpy as jnp
        import numpy as np
        H = 256
        NH = 16
        HD = H // NH
        key = jax.random.key(seed)
        ks = jax.random.split(key, 12)
        inp = {'query': jax.random.normal(ks[0], (4, 256, H), dtype=jnp.float32), 'key': jax.random.normal(ks[1], (4, 512, H), dtype=jnp.float32), 'value': jax.random.normal(ks[2], (4, 512, H), dtype=jnp.float32), 'key_padding_mask': jax.random.randint(ks[3], (4, 512), 0, 2, dtype=jnp.int32), 'Wq': jax.random.normal(ks[4], (H, H), dtype=jnp.float32) * (1.0 / np.sqrt(H)), 'bq': jnp.zeros((H,), dtype=jnp.float32), 'Wk': jax.random.normal(ks[5], (H, H), dtype=jnp.float32) * (1.0 / np.sqrt(H)), 'bk': jnp.zeros((H,), dtype=jnp.float32), 'Wv': jax.random.normal(ks[6], (H, H), dtype=jnp.float32) * (1.0 / np.sqrt(H)), 'bv': jnp.zeros((H,), dtype=jnp.float32), 'Wo': jax.random.normal(ks[7], (H, H), dtype=jnp.float32) * (1.0 / np.sqrt(H)), 'bo': jnp.zeros((H,), dtype=jnp.float32)}
        return inp
    _L2_xattn_all = _L2_xattn_setup()
    _L2_xattn_in = {k: v for k, v in _L2_xattn_all.items() if k in ('Wq', 'bq', 'Wk', 'bk', 'Wv', 'bv', 'Wo', 'bo')}
    del _L2_xattn_all

    def _L2_ffn_setup():
        import jax, jax.numpy as jnp
        import numpy as np
        EPS = 1e-05
        HEADS = 8
        DIM_KEY = 128
        K = 16
        NUM_KEYS = 64
        key = jax.random.key(seed)
        ks = jax.random.split(key, 5)
        B, T, D = (1, 256, 256)
        x = jax.random.normal(ks[0], (B, T, D), dtype=jnp.float32)
        norm_w = jnp.ones((D,), dtype=jnp.float32)
        wq = jax.random.normal(ks[1], (D, DIM_KEY * HEADS * 2), dtype=jnp.float32) * 0.02
        keys = jax.random.normal(ks[2], (HEADS, NUM_KEYS, 2, DIM_KEY), dtype=jnp.float32) * 0.02
        expert_down = jax.random.normal(ks[3], (NUM_KEYS * NUM_KEYS, D), dtype=jnp.float32) * 0.02
        expert_up = jax.random.normal(ks[4], (NUM_KEYS * NUM_KEYS, D), dtype=jnp.float32) * 0.02
        return {'x': x, 'norm_w': norm_w, 'wq': wq, 'keys': keys, 'expert_down': expert_down, 'expert_up': expert_up}
    _L2_ffn_all = _L2_ffn_setup()
    _L2_ffn_in = {k: v for k, v in _L2_ffn_all.items() if k in ('norm_w', 'wq', 'keys', 'expert_down', 'expert_up')}
    del _L2_ffn_all

    def _L3_xattn_setup():
        import jax, jax.numpy as jnp
        import numpy as np
        DIM = 256
        NUM_HEADS = 16
        DIM_HEAD = 64
        INNER = NUM_HEADS * DIM_HEAD
        SCALE = DIM_HEAD ** (-0.5)

        def _layernorm(x, gamma, beta, eps=1e-05):
            mu = jnp.mean(x, axis=-1, keepdims=True)
            var = jnp.mean(jnp.square(x - mu), axis=-1, keepdims=True)
            return (x - mu) * jax.lax.rsqrt(var + eps) * gamma + beta
        key = jax.random.key(seed)
        ks = jax.random.split(key, 8)
        B, SQ, SK = (2, 512, 1024)
        x = jax.random.normal(ks[0], (B, SQ, DIM), dtype=jnp.float32)
        context = jax.random.normal(ks[1], (B, SK, DIM), dtype=jnp.float32)
        ln_gamma = jnp.ones((DIM,), jnp.float32)
        ln_beta = jnp.zeros((DIM,), jnp.float32)
        w_q = jax.random.normal(ks[2], (DIM, INNER), dtype=jnp.float32) / np.sqrt(DIM)
        w_kv = jax.random.normal(ks[3], (DIM, 2 * INNER), dtype=jnp.float32) / np.sqrt(DIM)
        w_out = jax.random.normal(ks[4], (INNER, DIM), dtype=jnp.float32) / np.sqrt(INNER)
        b_out = jnp.zeros((DIM,), jnp.float32)
        gate = jnp.array([0.5], jnp.float32)
        return {'x': x, 'context': context, 'ln_gamma': ln_gamma, 'ln_beta': ln_beta, 'w_q': w_q, 'w_kv': w_kv, 'w_out': w_out, 'b_out': b_out, 'gate': gate}
    _L3_xattn_all = _L3_xattn_setup()
    _L3_xattn_in = {k: v for k, v in _L3_xattn_all.items() if k in ('ln_gamma', 'ln_beta', 'w_q', 'w_kv', 'w_out', 'b_out', 'gate')}
    del _L3_xattn_all

    def _L3_ffn_setup():
        import jax, jax.numpy as jnp
        import numpy as np
        HID = 256
        NH = 16
        NKV = 4
        HD = HID // NH
        E = 8
        TOPK = 2
        FFN = 512
        EPS = 1e-05
        THETA = 10000.0

        def _rmsnorm(x, w):
            var = jnp.mean(x * x, axis=-1, keepdims=True)
            return x * jax.lax.rsqrt(var + EPS) * w

        def _rope_tables(S):
            inv_freq = 1.0 / THETA ** (jnp.arange(0, HD, 2, dtype=jnp.float32) / HD)
            freqs = jnp.arange(S, dtype=jnp.float32)[:, None] * inv_freq[None, :]
            emb = jnp.concatenate([freqs, freqs], axis=-1)
            return (jnp.cos(emb), jnp.sin(emb))

        def _apply_rope(t, cos, sin):
            t1, t2 = jnp.split(t, 2, axis=-1)
            rot = jnp.concatenate([-t2, t1], axis=-1)
            return t * cos[None, :, None, :] + rot * sin[None, :, None, :]
        key = jax.random.key(seed)
        ks = jax.random.split(key, 6)
        B, S = (1, 512)
        x = jax.random.normal(ks[0], (B, S, HID), dtype=jnp.float32)
        wqkv = jax.random.normal(ks[1], ((NH + 2 * NKV) * HD, HID), dtype=jnp.float32) * 0.02
        wo = jax.random.normal(ks[2], (HID, NH * HD), dtype=jnp.float32) * 0.02
        gate_w = jax.random.normal(ks[3], (E, HID), dtype=jnp.float32) * 0.02
        w13 = jax.random.normal(ks[4], (E, 2 * FFN, HID), dtype=jnp.float32) * 0.02
        w2 = jax.random.normal(ks[5], (E, HID, FFN), dtype=jnp.float32) * 0.02
        return {'x': x, 'ln1_w': jnp.ones((HID,), jnp.float32), 'ln2_w': jnp.ones((HID,), jnp.float32), 'wqkv': wqkv, 'wo': wo, 'gate_w': gate_w, 'w13': w13, 'w2': w2}
    _L3_ffn_all = _L3_ffn_setup()
    _L3_ffn_in = {k: v for k, v in _L3_ffn_all.items() if k in ('ln1_w', 'ln2_w', 'wqkv', 'wo', 'gate_w', 'w13', 'w2')}
    del _L3_ffn_all
    return {'x': x, 'ctx_1024': ctx_1024, 'mask_BxS2x1_ff1': mask_BxS2x1_ff1, 'mask_Bx1x1xS2_fk0': mask_Bx1x1xS2_fk0, 'mask_BxS2_ik0': mask_BxS2_ik0, 'g_xattn': g_xattn, 'g_ffn': g_ffn, 'L0_xattn_Wk': _L0_xattn_in['Wk'], 'L0_xattn_Wv': _L0_xattn_in['Wv'], 'L0_xattn_Wq': _L0_xattn_in['Wq'], 'L0_xattn_Wo': _L0_xattn_in['Wo'], 'L0_ffn_k0': _L0_ffn_in['k0'], 'L0_ffn_k1': _L0_ffn_in['k1'], 'L0_ffn_k2': _L0_ffn_in['k2'], 'L0_ffn_s0': _L0_ffn_in['s0'], 'L0_ffn_s1': _L0_ffn_in['s1'], 'L0_ffn_s2': _L0_ffn_in['s2'], 'L1_xattn_Wq': _L1_xattn_in['Wq'], 'L1_xattn_bq': _L1_xattn_in['bq'], 'L1_xattn_Wk': _L1_xattn_in['Wk'], 'L1_xattn_bk': _L1_xattn_in['bk'], 'L1_xattn_Wv': _L1_xattn_in['Wv'], 'L1_xattn_bv': _L1_xattn_in['bv'], 'L1_xattn_Wo': _L1_xattn_in['Wo'], 'L1_xattn_bo': _L1_xattn_in['bo'], 'L1_ffn_Ws': _L1_ffn_in['Ws'], 'L1_ffn_bs': _L1_ffn_in['bs'], 'L1_ffn_Wg': _L1_ffn_in['Wg'], 'L1_ffn_Wu': _L1_ffn_in['Wu'], 'L1_ffn_Wd': _L1_ffn_in['Wd'], 'L2_xattn_Wq': _L2_xattn_in['Wq'], 'L2_xattn_bq': _L2_xattn_in['bq'], 'L2_xattn_Wk': _L2_xattn_in['Wk'], 'L2_xattn_bk': _L2_xattn_in['bk'], 'L2_xattn_Wv': _L2_xattn_in['Wv'], 'L2_xattn_bv': _L2_xattn_in['bv'], 'L2_xattn_Wo': _L2_xattn_in['Wo'], 'L2_xattn_bo': _L2_xattn_in['bo'], 'L2_ffn_norm_w': _L2_ffn_in['norm_w'], 'L2_ffn_wq': _L2_ffn_in['wq'], 'L2_ffn_keys': _L2_ffn_in['keys'], 'L2_ffn_expert_down': _L2_ffn_in['expert_down'], 'L2_ffn_expert_up': _L2_ffn_in['expert_up'], 'L3_xattn_ln_gamma': _L3_xattn_in['ln_gamma'], 'L3_xattn_ln_beta': _L3_xattn_in['ln_beta'], 'L3_xattn_w_q': _L3_xattn_in['w_q'], 'L3_xattn_w_kv': _L3_xattn_in['w_kv'], 'L3_xattn_w_out': _L3_xattn_in['w_out'], 'L3_xattn_b_out': _L3_xattn_in['b_out'], 'L3_xattn_gate': _L3_xattn_in['gate'], 'L3_ffn_ln1_w': _L3_ffn_in['ln1_w'], 'L3_ffn_ln2_w': _L3_ffn_in['ln2_w'], 'L3_ffn_wqkv': _L3_ffn_in['wqkv'], 'L3_ffn_wo': _L3_ffn_in['wo'], 'L3_ffn_gate_w': _L3_ffn_in['gate_w'], 'L3_ffn_w13': _L3_ffn_in['w13'], 'L3_ffn_w2': _L3_ffn_in['w2']}

def reference(x, ctx_1024, mask_BxS2x1_ff1, mask_Bx1x1xS2_fk0, mask_BxS2_ik0, g_xattn, g_ffn, L0_xattn_Wk, L0_xattn_Wv, L0_xattn_Wq, L0_xattn_Wo, L0_ffn_k0, L0_ffn_k1, L0_ffn_k2, L0_ffn_s0, L0_ffn_s1, L0_ffn_s2, L1_xattn_Wq, L1_xattn_bq, L1_xattn_Wk, L1_xattn_bk, L1_xattn_Wv, L1_xattn_bv, L1_xattn_Wo, L1_xattn_bo, L1_ffn_Ws, L1_ffn_bs, L1_ffn_Wg, L1_ffn_Wu, L1_ffn_Wd, L2_xattn_Wq, L2_xattn_bq, L2_xattn_Wk, L2_xattn_bk, L2_xattn_Wv, L2_xattn_bv, L2_xattn_Wo, L2_xattn_bo, L2_ffn_norm_w, L2_ffn_wq, L2_ffn_keys, L2_ffn_expert_down, L2_ffn_expert_up, L3_xattn_ln_gamma, L3_xattn_ln_beta, L3_xattn_w_q, L3_xattn_w_kv, L3_xattn_w_out, L3_xattn_b_out, L3_xattn_gate, L3_ffn_ln1_w, L3_ffn_ln2_w, L3_ffn_wqkv, L3_ffn_wo, L3_ffn_gate_w, L3_ffn_w13, L3_ffn_w2):
    import jax
    import jax.numpy as jnp

    def _L0_xattn_ref(query, key, value, mask, Wk, Wv, Wq, Wo):
        import jax, jax.numpy as jnp
        import numpy as np
        B, S, U = (4, 1024, 256)
        pk = jnp.einsum('bsu,uv->bsv', key, Wk)
        pv = jnp.einsum('bsu,uv->bsv', value, Wv)
        pq = jnp.einsum('bsu,uv->bsv', query, Wq)
        pk = pk * mask
        pv = pv * mask
        pk = jax.nn.swish(pk)
        kv = jnp.einsum('bsu,bsv->buv', pk, pv)
        out = jnp.einsum('bsu,buv->bsv', pq, kv)
        return jnp.einsum('bsu,uv->bsv', out, Wo)

    def _L0_ffn_ref(x, k0, k1, k2, s0, s1, s2):
        import jax, jax.numpy as jnp
        import numpy as np
        import math
        D_IN = 256
        FEATURES = (1024, 1024, 256)
        BATCH, SEQ = (8, 512)

        def _conn_dense(kernel_bool, x):
            w = jnp.where(kernel_bool, jnp.float32(1.0), jnp.float32(-1.0))
            return x @ w
        h = jnp.concatenate([x, -x], axis=-1)
        h = s0 * _conn_dense(k0, h)
        h = jax.nn.relu(h) * 2
        h = s1 * _conn_dense(k1, h)
        h = jax.nn.relu(h) * 2
        h = s2 * _conn_dense(k2, h)
        return h

    def _L1_xattn_ref(query, key, value, mask, Wq, bq, Wk, bk, Wv, bv, Wo, bo):
        import jax, jax.numpy as jnp
        import numpy as np
        B, S, D, H = (2, 512, 256, 16)
        DH = D // H

        def _split_heads(x):
            b, s, _ = x.shape
            return x.reshape(b, s, H, DH).transpose(0, 2, 1, 3)
        q = _split_heads(query @ Wq + bq)
        k = _split_heads(key @ Wk + bk)
        v = _split_heads(value @ Wv + bv)
        logits = jnp.einsum('bhqd,bhkd->bhqk', q, k) / jnp.sqrt(jnp.float32(DH))
        logits = logits + mask * -1000000000.0
        attn = jax.nn.softmax(logits, axis=-1)
        out = jnp.einsum('bhqk,bhkd->bhqd', attn, v)
        out = out.transpose(0, 2, 1, 3).reshape(query.shape[0], -1, D)
        return out @ Wo + bo

    def _L1_ffn_ref(x, Ws, bs, Wg, Wu, Wd):
        import jax, jax.numpy as jnp
        import numpy as np
        D, F, E, K = (256, 688, 8, 2)
        b, n, d = x.shape
        xt = x.reshape(-1, d)
        logits = xt @ Ws + bs
        topk_w, topk_idx = jax.lax.top_k(logits, K)
        topk_w = jax.nn.softmax(topk_w, axis=-1)
        combine = jnp.sum(jax.nn.one_hot(topk_idx, E, dtype=xt.dtype) * topk_w[..., None], axis=1)
        g = jnp.einsum('td,edf->tef', xt, Wg)
        u = jnp.einsum('td,edf->tef', xt, Wu)
        h = jax.nn.silu(g) * u
        y = jnp.einsum('tef,efd->ted', h, Wd)
        out = jnp.einsum('ted,te->td', y, combine)
        return out.reshape(b, n, d)

    def _L2_xattn_ref(query, key, value, key_padding_mask, Wq, bq, Wk, bk, Wv, bv, Wo, bo):
        import jax, jax.numpy as jnp
        import numpy as np
        H = 256
        NH = 16
        HD = H // NH
        B, Sq, _ = query.shape
        Sk = key.shape[1]
        scaling = HD ** (-0.5)
        q = (query @ Wq + bq).reshape(B, Sq, NH, HD).transpose(0, 2, 1, 3)
        k = (key @ Wk + bk).reshape(B, Sk, NH, HD).transpose(0, 2, 1, 3)
        v = (value @ Wv + bv).reshape(B, Sk, NH, HD).transpose(0, 2, 1, 3)
        scores = jnp.einsum('bhqd,bhkd->bhqk', q, k) * scaling
        scores = jnp.where((key_padding_mask == 0)[:, None, None, :], -jnp.inf, scores)
        attn = jax.nn.softmax(scores, axis=-1)
        out = jnp.einsum('bhqk,bhkd->bhqd', attn, v)
        out = out.transpose(0, 2, 1, 3).reshape(B, Sq, H)
        return out @ Wo + bo

    def _L2_ffn_ref(x, norm_w, wq, keys, expert_down, expert_up):
        import jax, jax.numpy as jnp
        import numpy as np
        EPS = 1e-05
        HEADS = 8
        DIM_KEY = 128
        K = 16
        NUM_KEYS = 64
        B, T, D = x.shape
        inv = jax.lax.rsqrt(jnp.mean(x * x, axis=-1, keepdims=True) + EPS)
        x_norm = x * inv * norm_w
        q = (x_norm @ wq).reshape(B, T, HEADS, 2, DIM_KEY)
        sim = jnp.einsum('bthpd,hkpd->pbthk', q, keys)
        s1, i1 = jax.lax.top_k(sim[0], K)
        s2, i2 = jax.lax.top_k(sim[1], K)
        all_idx = (i1[..., :, None] * NUM_KEYS + i2[..., None, :]).reshape(B, T, HEADS, K * K)
        all_scores = (s1[..., :, None] + s2[..., None, :]).reshape(B, T, HEADS, K * K)
        final_scores, pk = jax.lax.top_k(all_scores, K)
        final_idx = jnp.take_along_axis(all_idx, pk, axis=-1)
        wd = expert_down[final_idx]
        wu = expert_up[final_idx]
        hidden = jnp.einsum('btd,bthkd->bthk', x_norm, wd)
        hidden = jax.nn.gelu(hidden, approximate=False)
        hidden = hidden * jax.nn.relu(final_scores)
        out = jnp.einsum('bthk,bthkd->btd', hidden, wu)
        return out

    def _L3_xattn_ref(x, context, ln_gamma, ln_beta, w_q, w_kv, w_out, b_out, gate):
        import jax, jax.numpy as jnp
        import numpy as np
        DIM = 256
        NUM_HEADS = 16
        DIM_HEAD = 64
        INNER = NUM_HEADS * DIM_HEAD
        SCALE = DIM_HEAD ** (-0.5)

        def _layernorm(x, gamma, beta, eps=1e-05):
            mu = jnp.mean(x, axis=-1, keepdims=True)
            var = jnp.mean(jnp.square(x - mu), axis=-1, keepdims=True)
            return (x - mu) * jax.lax.rsqrt(var + eps) * gamma + beta
        B, SQ, _ = x.shape
        SK = context.shape[1]
        xn = _layernorm(x, ln_gamma, ln_beta)
        q = (xn @ w_q).reshape(B, SQ, NUM_HEADS, DIM_HEAD)
        kv = context @ w_kv
        k, v = jnp.split(kv, 2, axis=-1)
        k = k.reshape(B, SK, NUM_HEADS, DIM_HEAD)
        v = v.reshape(B, SK, NUM_HEADS, DIM_HEAD)
        scores = jnp.einsum('bqhd,bkhd->bhqk', q * SCALE, k)
        attn = jax.nn.softmax(scores, axis=-1)
        out = jnp.einsum('bhqk,bkhd->bqhd', attn, v).reshape(B, SQ, INNER)
        out = out @ w_out + b_out
        return out * jnp.tanh(gate[0])

    def _L3_ffn_ref(x, ln1_w, ln2_w, wqkv, wo, gate_w, w13, w2):
        import jax, jax.numpy as jnp
        import numpy as np
        HID = 256
        NH = 16
        NKV = 4
        HD = HID // NH
        E = 8
        TOPK = 2
        FFN = 512
        EPS = 1e-05
        THETA = 10000.0

        def _rmsnorm(x, w):
            var = jnp.mean(x * x, axis=-1, keepdims=True)
            return x * jax.lax.rsqrt(var + EPS) * w

        def _rope_tables(S):
            inv_freq = 1.0 / THETA ** (jnp.arange(0, HD, 2, dtype=jnp.float32) / HD)
            freqs = jnp.arange(S, dtype=jnp.float32)[:, None] * inv_freq[None, :]
            emb = jnp.concatenate([freqs, freqs], axis=-1)
            return (jnp.cos(emb), jnp.sin(emb))

        def _apply_rope(t, cos, sin):
            t1, t2 = jnp.split(t, 2, axis=-1)
            rot = jnp.concatenate([-t2, t1], axis=-1)
            return t * cos[None, :, None, :] + rot * sin[None, :, None, :]
        B, S, _ = x.shape
        h = _rmsnorm(x, ln1_w)
        qkv = jnp.einsum('bsh,oh->bso', h, wqkv)
        q = qkv[..., :NH * HD].reshape(B, S, NH, HD)
        k = qkv[..., NH * HD:(NH + NKV) * HD].reshape(B, S, NKV, HD)
        v = qkv[..., (NH + NKV) * HD:].reshape(B, S, NKV, HD)
        cos, sin = _rope_tables(S)
        q = _apply_rope(q, cos, sin)
        k = _apply_rope(k, cos, sin)
        groups = NH // NKV
        k = jnp.repeat(k, groups, axis=2)
        v = jnp.repeat(v, groups, axis=2)
        scale = HD ** (-0.5)
        scores = jnp.einsum('bqhd,bkhd->bhqk', q, k) * scale
        causal = jnp.tril(jnp.ones((S, S), dtype=bool))
        scores = jnp.where(causal[None, None], scores, jnp.finfo(scores.dtype).min)
        probs = jax.nn.softmax(scores, axis=-1)
        attn = jnp.einsum('bhqk,bkhd->bqhd', probs, v).reshape(B, S, NH * HD)
        x = x + jnp.einsum('bso,ho->bsh', attn, wo)
        h = _rmsnorm(x, ln2_w).reshape(-1, HID)
        T = h.shape[0]
        logits = jnp.einsum('th,eh->te', h, gate_w)
        rprobs = jax.nn.softmax(logits.astype(jnp.float32), axis=-1)
        topw, topi = jax.lax.top_k(rprobs, TOPK)
        topw = topw / jnp.sum(topw, axis=-1, keepdims=True)
        wfull = jnp.zeros((T, E), jnp.float32).at[jnp.arange(T)[:, None], topi].set(topw)
        wfull = wfull.astype(h.dtype)
        out = jnp.zeros((T, HID), h.dtype)
        for e in range(E):
            w1 = w13[e, :FFN]
            w3 = w13[e, FFN:]
            g = jax.nn.silu(h @ w1.T) * (h @ w3.T)
            out = out + jnp.einsum('tf,hf->th', g, w2[e]) * wfull[:, e:e + 1]
        return x + out.reshape(B, S, HID)
    x = x + jnp.tanh(g_xattn[0]) * _L0_xattn_ref(_layernorm(x, axis=-1), ctx_1024, ctx_1024, mask_BxS2x1_ff1, L0_xattn_Wk, L0_xattn_Wv, L0_xattn_Wq, L0_xattn_Wo)
    x = x + jnp.tanh(g_ffn[0]) * _L0_ffn_ref(_layernorm(x, axis=-1), L0_ffn_k0, L0_ffn_k1, L0_ffn_k2, L0_ffn_s0, L0_ffn_s1, L0_ffn_s2)
    x = x + jnp.tanh(g_xattn[1]) * _L1_xattn_ref(_layernorm(x, axis=-1), ctx_1024, ctx_1024, mask_Bx1x1xS2_fk0, L1_xattn_Wq, L1_xattn_bq, L1_xattn_Wk, L1_xattn_bk, L1_xattn_Wv, L1_xattn_bv, L1_xattn_Wo, L1_xattn_bo)
    x = x + jnp.tanh(g_ffn[1]) * _L1_ffn_ref(_layernorm(x, axis=-1), L1_ffn_Ws, L1_ffn_bs, L1_ffn_Wg, L1_ffn_Wu, L1_ffn_Wd)
    x = x + jnp.tanh(g_xattn[2]) * _L2_xattn_ref(_layernorm(x, axis=-1), ctx_1024, ctx_1024, mask_BxS2_ik0, L2_xattn_Wq, L2_xattn_bq, L2_xattn_Wk, L2_xattn_bk, L2_xattn_Wv, L2_xattn_bv, L2_xattn_Wo, L2_xattn_bo)
    x = x + jnp.tanh(g_ffn[2]) * _L2_ffn_ref(_layernorm(x, axis=-1), L2_ffn_norm_w, L2_ffn_wq, L2_ffn_keys, L2_ffn_expert_down, L2_ffn_expert_up)
    x = x + jnp.tanh(g_xattn[3]) * _L3_xattn_ref(_layernorm(x, axis=-1), ctx_1024, L3_xattn_ln_gamma, L3_xattn_ln_beta, L3_xattn_w_q, L3_xattn_w_kv, L3_xattn_w_out, L3_xattn_b_out, L3_xattn_gate)
    x = x + jnp.tanh(g_ffn[3]) * _L3_ffn_ref(_layernorm(x, axis=-1), L3_ffn_ln1_w, L3_ffn_ln2_w, L3_ffn_wqkv, L3_ffn_wo, L3_ffn_gate_w, L3_ffn_w13, L3_ffn_w2)
    return x

_drawn_inputs = setup_inputs


def setup_inputs(seed=0):
    import zlib

    import numpy as np

    out = dict(_drawn_inputs(seed))
    spreads = {'L1_xattn_bq': (0.0, 0.8),
     'L1_xattn_bk': (0.0, 0.8),
     'L1_xattn_bv': (0.0, 0.8),
     'L1_xattn_bo': (0.0, 0.8),
     'L1_ffn_bs': (0.0, 0.8),
     'L2_xattn_bq': (0.0, 0.8),
     'L2_xattn_bk': (0.0, 0.8),
     'L2_xattn_bv': (0.0, 0.8),
     'L2_xattn_bo': (0.0, 0.8),
     'L2_ffn_norm_w': (1.0, 0.6),
     'L3_xattn_ln_gamma': (1.0, 0.6),
     'L3_xattn_ln_beta': (0.0, 0.8),
     'L3_xattn_b_out': (0.0, 0.8),
     'L3_ffn_ln1_w': (1.0, 0.6),
     'L3_ffn_ln2_w': (1.0, 0.6)}
    factors = {'g_ffn': 8.0,
     'L1_xattn_Wq': 8.0,
     'L1_xattn_Wk': 8.0,
     'L1_xattn_Wv': 8.0,
     'L1_xattn_Wo': 8.0,
     'L1_ffn_Ws': 8.0,
     'L1_ffn_Wg': 8.0,
     'L1_ffn_Wu': 8.0,
     'L1_ffn_Wd': 8.0,
     'L2_xattn_Wq': 8.0,
     'L2_xattn_Wk': 8.0,
     'L2_xattn_Wv': 8.0,
     'L2_xattn_Wo': 8.0,
     'L2_ffn_wq': 8.0,
     'L2_ffn_keys': 8.0,
     'L2_ffn_expert_down': 8.0,
     'L2_ffn_expert_up': 8.0,
     'L3_xattn_w_q': 8.0,
     'L3_xattn_w_kv': 8.0,
     'L3_xattn_w_out': 8.0,
     'L3_ffn_wqkv': 8.0,
     'L3_ffn_wo': 8.0,
     'L3_ffn_gate_w': 8.0,
     'L3_ffn_w13': 8.0,
     'L3_ffn_w2': 8.0}
    for name, (base, spread) in spreads.items():
        noise = np.random.default_rng([zlib.crc32(name.encode()), seed]).standard_normal(out[name].shape)
        drawn = base * np.exp(spread * noise) if base else spread * noise
        out[name] = jnp.asarray(drawn.astype(out[name].dtype))
    for name, factor in factors.items():
        out[name] = (out[name] * factor).astype(out[name].dtype)
    return out
```

```python
from contextlib import ExitStack

import numpy as np

import concourse.bass as bass
from concourse import mybir

F32 = mybir.dt.float32
BF16 = mybir.dt.bfloat16
I32 = mybir.dt.int32
U32 = mybir.dt.uint32
U8 = mybir.dt.uint8
ALU = mybir.AluOpType
ACT = mybir.ActivationFunctionType
AX_X = mybir.AxisListType.X

P = 128
B, S, D = 2, 1024, 256
TILES = B * S // P
TB = S // P
DC = D // P
NKEY = 77
NH = 16
HK = NH * NKEY
HKC = -(-HK // P)
HK_LAST = HK - (HKC - 1) * P
HPB = 512 // NKEY
GROUP = 512
NG = B * S // GROUP
TPG = GROUP // P
EPS = 1e-5
MASKED = -3.0e38
GATE_XATTN, GATE_FFN, GATE_L3 = 0, 4, 8

HEAD_BANKS = [(j, h0, min(HPB, NH - h0)) for j, h0 in enumerate(range(0, NH, HPB))]


class Steps:

    def __init__(self, eng, sem, base=0):
        self.eng, self.sem, self.base, self.n = eng, sem, base, 0

    def mark(self, ins):
        ins.then_inc(self.sem, 1)
        self.n += 1

    def link(self, ins, alone=None):
        self.mark(ins)
        self.eng.wait_ge(self.sem, self.base + self.n)
        if alone is not None:
            self.eng.sem_inc(alone, 1)


def flat(ap):
    return ap.rearrange("p a n -> p (a n)")


def tile_of(t3, t):
    return flat(t3[:, bass.ds(t, 1), :])


NORM_LINKS = {"layer": 2, "rms": 3}


class Norm:

    def __init__(self, nc, g, st, name=""):
        self.nc, self.minus_half = nc, g.minus_half
        self.small = st.sb(f"moments{name}", [P, 10])
        self.waits_alone = st.sem(f"waits_alone{name}")
        self.var_ready, self.rstd_ready = st.sem(f"var_ready{name}"), st.sem(f"rstd_ready{name}")

    def vector(self, dve, steps, n, src, dst, kind):
        nc, small = self.nc, self.small
        stats, agg, power, rstd = small[:, 0:6], small[:, 6:8], small[:, 8:9], small[:, 9:10]
        steps.link(nc.vector.bn_stats(stats, src), alone=self.waits_alone)
        steps.link(nc.vector.bn_aggr(agg, stats))
        if kind == "rms":
            steps.link(nc.vector.scalar_tensor_tensor(out=power, in0=agg[:, 0:1], scalar=agg[:, 0:1],
                                                      in1=agg[:, 1:2], op0=ALU.mult, op1=ALU.add))
        mean_square = power if kind == "rms" else agg[:, 1:2]
        nc.vector.tensor_scalar(power, mean_square, EPS, None, ALU.add).then_inc(self.var_ready, 1)
        dve.wait_ge(self.rstd_ready, n + 1)
        if kind == "rms":
            return nc.vector.tensor_scalar(dst, src, rstd, None, ALU.mult)
        return nc.vector.tensor_scalar(dst, src, agg[:, 0:1], rstd, ALU.subtract, ALU.mult)

    def gpsimd(self, pool, n):
        pool.wait_ge(self.var_ready, n + 1)
        self.nc.gpsimd.tensor_tensor(self.small[:, 9:10], self.small[:, 8:9], self.minus_half[:, 0:1], ALU.pow)\
            .then_inc(self.rstd_ready, 1)


class Stage:

    def __init__(self, nc, ctx, name):
        self.nc, self.ctx, self.name, self.sems = nc, ctx, name, []
        ctx.callback(self.clear)

    def clear(self):
        if self.sems:
            self.nc.clear_and_free_semaphores(self.sems)
            self.nc.all_engine_barrier()

    def sb(self, name, shape, dt=F32):
        return self.ctx.enter_context(self.nc.sbuf_tensor(f"{self.name}_{name}", shape, dt))

    def sem(self, name):
        self.sems.append(self.nc.alloc_semaphore(f"{self.name}_{name}"))
        return self.sems[-1]

    def block(self):
        return self.ctx.enter_context(self.nc.Block())


def load_stream(nc, g, dram):
    with ExitStack() as ctx:
        st = Stage(nc, ctx, "in")
        loaded, gates_loaded = st.sem("loaded"), st.sem("gates_loaded")
        zeroed, made, gates_done = st.sem("zeroed"), st.sem("made"), st.sem("gates_done")
        block = st.block()

        @block.sync
        def _(sp):
            sp.dma_start(g.x[:], dram["x"].rearrange("b (t p) d -> p (b t) d", p=P)).then_inc(loaded, 16)
            for src, at, n in (("g_xattn", GATE_XATTN, 4), ("g_ffn", GATE_FFN, 4), ("L3_xattn_gate", GATE_L3, 1)):
                sp.dma_start(g.gates[:, at:at + n], dram[src].partition_broadcast(P)).then_inc(gates_loaded, 16)
            sp.wait_ge(loaded, 16)

        @block.scalar
        def _(act):
            act.wait_ge(gates_loaded, 48)
            nc.scalar.activation(g.gates[:, 0:9], g.gates[:, 0:9], ACT.Tanh).then_inc(gates_done, 1)
            act.wait_ge(gates_done, 1)

        @block.gpsimd
        def _(pool):
            nc.gpsimd.memset(g.ident[:], 0.0).then_inc(zeroed, 1)
            nc.gpsimd.memset(g.identb[:], 0.0).then_inc(zeroed, 1)
            nc.gpsimd.memset(g.ones[:], 1.0).then_inc(made, 1)
            nc.gpsimd.memset(g.minus_half[:], -0.5).then_inc(made, 1)
            nc.gpsimd.memset(g.causal[:], 0.0).then_inc(zeroed, 1)
            pool.wait_ge(zeroed, 3)
            for m in (g.ident, g.identb):
                nc.gpsimd.affine_select(out=m[:], in_=m[:], compare_op=ALU.not_equal, fill=1.0, base=0,
                                        pattern=[[-1, P]], channel_multiplier=1).then_inc(made, 1)
            nc.gpsimd.affine_select(out=g.causal[:], in_=g.causal[:], compare_op=ALU.is_ge, fill=MASKED / 4, base=0,
                                    pattern=[[-1, P]], channel_multiplier=1).then_inc(made, 1)
            pool.wait_ge(made, 5)


def store_stream(nc, g, out):
    with ExitStack() as ctx:
        st = Stage(nc, ctx, "out")
        stored = st.sem("stored")
        block = st.block()

        @block.sync
        def _(sp):
            sp.dma_start(out.rearrange("b (t p) d -> p (b t) d", p=P), g.x[:]).then_inc(stored, 16)
            sp.wait_ge(stored, 16)


def linear_attention(nc, g, dram):
    with ExitStack() as ctx:
        st = Stage(nc, ctx, "la")
        ctxT = st.sb("ctxT", [P, B, DC, NKEY])
        wk, wv, wo, wqT = (st.sb(n, [P, DC, D]) for n in ("wk", "wv", "wo", "wqT"))
        mask = st.sb("mask", [P, B])
        pk, pv, sig = (st.sb(n, [P, B, D]) for n in ("pk", "pv", "sig"))
        kvT, kvo, mat = (st.sb(n, [P, B, DC, D]) for n in ("kvT", "kvo", "mat"))
        norm = Norm(nc, g, st)
        xn = st.sb("xn", [P, D])
        xT = st.sb("xT", [P, DC, P])
        loaded, steps_done = st.sem("loaded"), st.sem("steps_done")
        keys_ready, masked, sig_done, kv_in_ready = st.sem("keys_ready"), st.sem("masked"), st.sem("sig_done"), st.sem("kv_in_ready")
        prod_ready, prod_used = st.sem("prod_ready"), st.sem("prod_used")
        xn_ready, xT_psum_ready, xT_ready, y_ready, tile_done = (
            st.sem(n) for n in ("xn_ready", "xT_psum_ready", "xT_ready", "y_ready", "tile_done"))
        ps = g.ps
        block = st.block()

        @block.sync
        def _(sp):
            sp.dma_start(ctxT[:], dram["ctxT"].rearrange("b (c p) k -> p b c k", p=P)).then_inc(loaded, 16)
            for t, n in ((wk, "L0_xattn_Wk"), (wv, "L0_xattn_Wv"), (wo, "L0_xattn_Wo"), (wqT, "L0_xattn_WqT")):
                sp.dma_start(t[:], dram[n].rearrange("(c p) n -> p c n", p=P)).then_inc(loaded, 16)
            sp.dma_start(mask[0:NKEY, :], dram["maskT_ff1"]).then_inc(loaded, 16)

        @block.tensor
        def _(pe):
            pe.wait_ge(loaded, 96)
            for b in range(B):
                for w, bank in ((wk, 0), (wv, 1)):
                    for c in range(DC):
                        last = nc.tensor.matmul(ps[0:NKEY, 2 * b + bank, 0:D], ctxT[:, b, c, :], w[:, c, :],
                                                start=(c == 0), stop=(c == DC - 1))
            last.then_inc(keys_ready, 1)
            pe.wait_ge(kv_in_ready, 2 * B)
            for b in range(B):
                for c in range(DC):
                    last = nc.tensor.matmul(ps[:, 4 + b, c * D:(c + 1) * D], pv[0:NKEY, b, c * P:(c + 1) * P],
                                            pk[0:NKEY, b, :], start=True, stop=True)
            last.then_inc(prod_ready, 1)
            for n, (lhs, rhs) in enumerate(((kvT, wo), (wqT, kvo))):
                pe.wait_ge(prod_used, n + 1)
                for b in range(B):
                    for m in range(DC):
                        for c in range(DC):
                            left = (lhs[:, b, c] if n == 0 else lhs[:, c])[:, m * P:(m + 1) * P]
                            right = rhs[:, c, :] if n == 0 else rhs[:, b, c, :]
                            last = nc.tensor.matmul(ps[:, 4 + b, m * D:(m + 1) * D], left, right,
                                                    start=(c == 0), stop=(c == DC - 1))
                last.then_inc(prod_ready, 1)
            pe.wait_ge(prod_used, 3)
            for b in range(B):
                with pe.Fori(0, TB) as t:
                    n = b * TB + t
                    pe.wait_ge(xn_ready, n + 1)
                    for c in range(DC):
                        last = nc.tensor.transpose(ps[:, 0, c * P:(c + 1) * P], xn[:, c * P:(c + 1) * P], g.ident[:])
                    last.then_inc(xT_psum_ready, 1)
                    pe.wait_ge(xT_ready, n + 1)
                    for c in range(DC):
                        last = nc.tensor.matmul(ps[:, 1, 0:D], xT[:, c, :], mat[:, b, c, :],
                                                start=(c == 0), stop=(c == DC - 1))
                    last.then_inc(y_ready, 1)

        @block.scalar
        def _(act):
            act.wait_ge(masked, 2 * B)
            nc.scalar.activation(sig[0:NKEY], pk[0:NKEY], ACT.Sigmoid).then_inc(sig_done, 1)

        @block.gpsimd
        def _(pool):
            with pool.Fori(0, TILES) as n:
                norm.gpsimd(pool, n)

        @block.vector
        def _(dve):
            dve.wait_ge(keys_ready, 1)
            for b in range(B):
                for dst, bank, done in ((pk, 0, masked), (pv, 1, masked)):
                    nc.vector.tensor_scalar(dst[0:NKEY, b, :], ps[0:NKEY, 2 * b + bank, 0:D], mask[0:NKEY, b:b + 1],
                                            None, ALU.mult).then_inc(done, 1)
            dve.wait_ge(sig_done, 1)
            for b in range(B):
                nc.vector.tensor_tensor(pk[0:NKEY, b, :], pk[0:NKEY, b, :], sig[0:NKEY, b, :], ALU.mult)\
                    .then_inc(kv_in_ready, 2)
            for n, dst in enumerate((kvT, kvo, mat)):
                dve.wait_ge(prod_ready, n + 1)
                for b in range(B):
                    src = ps[:, 4 + b, :].rearrange("p (c n) -> p c n", c=DC)
                    if n < 2:
                        last = nc.vector.tensor_copy(dst[:, b], src)
                    else:
                        last = nc.vector.tensor_scalar(dst[:, b], src, g.gates[:, GATE_XATTN:GATE_XATTN + 1], None, ALU.mult)
                last.then_inc(prod_used, 1)
            with dve.Fori(0, TILES) as n:
                s = Steps(dve, steps_done, n * NORM_LINKS["layer"])
                norm.vector(dve, s, n, tile_of(g.x, n), xn[:], "layer").then_inc(xn_ready, 1)
                dve.wait_ge(xT_psum_ready, n + 1)
                nc.vector.tensor_copy(xT[:], ps[:, 0, 0:D].rearrange("p (c n) -> p c n", c=DC)).then_inc(xT_ready, 1)
                dve.wait_ge(y_ready, n + 1)
                nc.vector.tensor_tensor(tile_of(g.x, n), tile_of(g.x, n), ps[:, 1, 0:D], ALU.add).then_inc(tile_done, 1)
                dve.wait_ge(tile_done, n + 1)


def cross_attention(nc, g, dram, layer, b):
    dh = dram[f"L{layer}_xattn_WqT"].shape[0]
    inner = NH * dh
    scale = dh ** -0.5
    full = layer == 3
    ps = g.ps
    with ExitStack() as ctx:
        st = Stage(nc, ctx, f"xa{layer}{b}")
        scores_w = st.sb("scores_w", [P, DC, HK])
        scores_b = st.sb("scores_b", [1, HK])
        values_w = st.sb("values_w", [P, HKC, D])
        bo = st.sb("bo", [1, D])
        affine = st.sb("affine", [P, 2, DC])
        scratch = nc.dram_tensor(f"xa{layer}{b}_values", (HKC * P, D), F32).ap()
        fold_context(nc, g, dram, layer, b, scores_w, scores_b, values_w, bo, affine, scratch)

        norm = Norm(nc, g, st)
        norm2 = Norm(nc, g, st, "2") if full else None
        xn, xT = st.sb("xn", [P, D]), st.sb("xT", [P, DC, P])
        probs = st.sb("probs", [P, NH, NKEY])
        probs_flat = probs[:].rearrange("p h k -> p (h k)")
        probsT = st.sb("probsT", [P, HKC, P])
        row_max, row_sum = st.sb("row_max", [P, NH]), st.sb("row_sum", [P, NH])
        steps_done = st.sem("steps_done")
        xn_ready, xT_psum_ready, xT_ready, scores_ready, centred, exp_done, probs_ready, pT_psum_ready, pT_ready, \
            y_ready, tile_done = (st.sem(n) for n in (
                "xn_ready", "xT_psum_ready", "xT_ready", "scores_ready", "centred", "exp_done", "probs_ready",
                "pT_psum_ready", "pT_ready", "y_ready", "tile_done"))
        SC, PT, XT, Y = 0, 3, 6, 7
        block = st.block()

        @block.tensor
        def _(pe):
            with pe.Fori(0, TB) as t:
                pe.wait_ge(xn_ready, t + 1)
                for c in range(DC):
                    last = nc.tensor.transpose(ps[:, XT, c * P:(c + 1) * P], xn[:, c * P:(c + 1) * P], g.ident[:])
                last.then_inc(xT_psum_ready, 1)
                pe.wait_ge(xT_ready, t + 1)
                for j, h0, n in HEAD_BANKS:
                    cols = slice(h0 * NKEY, (h0 + n) * NKEY)
                    for c in range(DC):
                        last = nc.tensor.matmul(ps[:, SC + j, 0:n * NKEY], xT[:, c, :], scores_w[:, c, cols],
                                                start=(c == 0), stop=(full and c == DC - 1))
                    if not full:
                        last = nc.tensor.matmul(ps[:, SC + j, 0:n * NKEY], g.ones[0:1, :], scores_b[0:1, cols],
                                                start=False, stop=True)
                last.then_inc(scores_ready, 1)
                pe.wait_ge(probs_ready, t + 1)
                for c in range(HKC):
                    w = P if c < HKC - 1 else HK_LAST
                    last = nc.tensor.transpose(ps[0:w, PT + c // 4, (c % 4) * P:(c % 4 + 1) * P],
                                               probs_flat[:, c * P:c * P + w], g.ident[:])
                last.then_inc(pT_psum_ready, 1)
                pe.wait_ge(pT_ready, 4 * t + 4)
                for c in range(HKC):
                    w = P if c < HKC - 1 else HK_LAST
                    nc.tensor.matmul(ps[:, Y, 0:D], probsT[0:w, c, :], values_w[0:w, c, :], start=(c == 0), stop=False)
                nc.tensor.matmul(ps[:, Y, 0:D], g.ones[0:1, :], bo[0:1, :], start=False, stop=True).then_inc(y_ready, 1)

        @block.gpsimd
        def _(pool):
            with pool.Fori(0, TB) as t:
                norm.gpsimd(pool, t)
                if full:
                    norm2.gpsimd(pool, t)

        @block.scalar
        def _(act):
            with act.Fori(0, TB) as t:
                act.wait_ge(centred, t + 1)
                nc.scalar.activation(probs_flat, probs_flat, ACT.Exp).then_inc(exp_done, 1)
                act.wait_ge(pT_psum_ready, t + 1)
                for k in range(2):
                    nc.scalar.activation(probsT[:, 4 * k:4 * k + 4, :].rearrange("p c n -> p (c n)"), ps[:, PT + k, :],
                                         ACT.Copy).then_inc(pT_ready, 1)
                nc.scalar.activation(probsT[:, 8, :], ps[:, PT + 2, 0:P], ACT.Copy).then_inc(pT_ready, 1)
                nc.scalar.activation(probsT[0:HK_LAST, 9, :], ps[0:HK_LAST, PT + 2, P:2 * P], ACT.Copy)\
                    .then_inc(pT_ready, 1)

        @block.vector
        def _(dve):
            per = NORM_LINKS["layer"] * (2 if full else 1) + (1 if full else 0) + 3
            with dve.Fori(0, TB) as t:
                s = Steps(dve, steps_done, t * per)
                x = tile_of(g.x, b * TB + t)
                if full:
                    s.link(norm.vector(dve, s, t, x, xn[:], "layer"))
                    norm2.vector(dve, s, t, xn[:], xn[:], "layer").then_inc(xn_ready, 1)
                else:
                    norm.vector(dve, s, t, x, xn[:], "layer").then_inc(xn_ready, 1)
                dve.wait_ge(xT_psum_ready, t + 1)
                if full:
                    for c in range(DC):
                        last = nc.vector.tensor_scalar(xT[:, c, :], ps[:, XT, c * P:(c + 1) * P], affine[:, 0, c:c + 1],
                                                       affine[:, 1, c:c + 1], ALU.mult, ALU.add)
                else:
                    last = nc.vector.tensor_copy(xT[:], ps[:, XT, 0:D].rearrange("p (c n) -> p c n", c=DC))
                last.then_inc(xT_ready, 1)
                dve.wait_ge(scores_ready, t + 1)
                sc = [(j, slice(h0, h0 + n), n, ps[:, SC + j, 0:n * NKEY].rearrange("p (h k) -> p h k", h=n))
                      for j, h0, n in HEAD_BANKS]
                for j, heads, n, bank in sc:
                    last = nc.vector.tensor_reduce(row_max[:, heads], bank, AX_X, ALU.max)
                s.link(last)
                for j, heads, n, bank in sc:
                    last = nc.vector.tensor_tensor(probs[:, heads, :], bank,
                                                   row_max[:, heads].unsqueeze(2).broadcast_to([P, n, NKEY]), ALU.subtract)
                last.then_inc(centred, 1)
                dve.wait_ge(exp_done, t + 1)
                s.link(nc.vector.tensor_reduce(row_sum[:], probs[:], AX_X, ALU.add))
                s.link(nc.vector.reciprocal(row_sum[:], row_sum[:]))
                nc.vector.tensor_tensor(probs[:], probs[:], row_sum[:].unsqueeze(2).broadcast_to([P, NH, NKEY]), ALU.mult)\
                    .then_inc(probs_ready, 1)
                dve.wait_ge(y_ready, t + 1)
                nc.vector.tensor_tensor(x, x, ps[:, Y, 0:D], ALU.add).then_inc(tile_done, 1)
                dve.wait_ge(tile_done, t + 1)
                assert s.n == per


def fold_context(nc, g, dram, layer, b, scores_w, scores_b, values_w, bo, affine, scratch):
    dh = dram[f"L{layer}_xattn_WqT"].shape[0]
    inner = NH * dh
    scale = dh ** -0.5
    full = layer == 3
    ps = g.ps
    with ExitStack() as ctx:
        st = Stage(nc, ctx, f"fc{layer}{b}")
        ctxT = st.sb("ctxT", [P, DC, NKEY])
        wk, wv = st.sb("wk", [P, DC, inner]), st.sb("wv", [P, DC, inner])
        wqT, wo = st.sb("wqT", [dh, NH, D]), st.sb("wo", [dh, NH, D])
        bias = st.sb("bias", [dh, 3, NH])
        mask_in = st.sb("mask_in", [P, NKEY], I32 if layer == 2 else F32)
        mask = st.sb("mask", [P, NKEY])
        gate = st.sb("gate", [P, 2])
        kT, vT = st.sb("kT", [dh, NH, NKEY]), st.sb("vT", [dh, NH, NKEY])
        vwo = st.sb("vwo", [NKEY, NH, D])
        loaded, stored, reloaded = st.sem("loaded"), st.sem("stored"), st.sem("reloaded")
        steps_done, gate_ready = st.sem("steps_done"), st.sem("gate_ready")
        kT_psum_ready, kT_ready, vT_psum_ready, vT_ready = (
            st.sem(n) for n in ("kT_psum_ready", "kT_ready", "vT_psum_ready", "vT_ready"))
        a_psum_ready, a_ready, row_psum_ready, row_ready = (
            st.sem(n) for n in ("a_psum_ready", "a_ready", "row_psum_ready", "row_ready"))
        vwo_psum_ready, vwo_ready = st.sem("vwo_psum_ready"), st.sem("vwo_ready")
        block = st.block()
        K_BANK, V_BANK, W_BANK = 0, 3, 6

        @block.sync
        def _(sp):
            sp.dma_start(ctxT[:], dram["ctxT"][b].rearrange("(c p) k -> p c k", p=P)).then_inc(loaded, 16)
            for t, n in ((wk, "Wk"), (wv, "Wv")):
                sp.dma_start(t[:], dram[f"L{layer}_xattn_{n}"].rearrange("(c p) n -> p c n", p=P)).then_inc(loaded, 16)
            sp.dma_start(wqT[:], dram[f"L{layer}_xattn_WqT"]).then_inc(loaded, 16)
            sp.dma_start(wo[:], dram[f"L{layer}_xattn_Wo"].rearrange("(h p) n -> p h n", p=dh)).then_inc(loaded, 16)
            sp.dma_start(bo[:], dram[f"L{layer}_xattn_bo"].rearrange("(a n) -> a n", a=1)).then_inc(loaded, 16)
            if full:
                sp.dma_start(affine[:], dram["L3_xattn_affine"]).then_inc(loaded, 16)
            else:
                sp.dma_start(bias[:], dram[f"L{layer}_xattn_bias"]).then_inc(loaded, 16)
                src = dram[f"L{layer}_xattn_mask"][b]
                sp.dma_start(mask_in[:], src.partition_broadcast(P)).then_inc(loaded, 16)
            sp.wait_ge(vwo_ready, NH // 2)
            sp.dma_start(scratch[0:HK, :].rearrange("(h k) n -> k h n", h=NH), vwo[:]).then_inc(stored, 16)
            sp.wait_ge(stored, 16)
            sp.dma_start(values_w[:, 0:HKC - 1, :], scratch[0:(HKC - 1) * P, :].rearrange("(c p) n -> p c n", p=P))\
                .then_inc(reloaded, 16)
            sp.dma_start(values_w[0:HK_LAST, HKC - 1, :], scratch[(HKC - 1) * P:HK, :]).then_inc(reloaded, 16)
            sp.wait_ge(reloaded, 32)

        @block.tensor
        def _(pe):
            pe.wait_ge(loaded, 16 * (7 if full else 8))
            for w, bank, ready in ((wk, K_BANK, kT_psum_ready), (wv, V_BANK, vT_psum_ready)):
                for h in range(NH):
                    for c in range(DC):
                        last = nc.tensor.matmul(ps[0:dh, bank + h // HPB, (h % HPB) * NKEY:(h % HPB + 1) * NKEY],
                                                w[:, c, h * dh:(h + 1) * dh], ctxT[:, c, :],
                                                start=(c == 0), stop=(c == DC - 1))
                last.then_inc(ready, 1)
            for m, bank, free in ((0, K_BANK, kT_ready), (1, V_BANK, vT_ready)):
                pe.wait_ge(free, 1)
                for h in range(NH):
                    last = nc.tensor.matmul(ps[:, bank + h // HPB, (h % HPB) * NKEY:(h % HPB + 1) * NKEY],
                                            wqT[:, h, m * P:(m + 1) * P], kT[:, h, :], start=True, stop=True)
                last.then_inc(a_psum_ready, 1)
            if not full:
                pe.wait_ge(a_ready, 1)
                for h in range(NH):
                    last = nc.tensor.matmul(ps[0:1, K_BANK + h // HPB, (h % HPB) * NKEY:(h % HPB + 1) * NKEY],
                                            bias[:, 0, h:h + 1], kT[:, h, :], start=True, stop=True)
                last.then_inc(row_psum_ready, 1)
            for pair in range(NH // 2):
                if pair >= 2:
                    pe.wait_ge(vwo_ready, pair - 1)
                for h in (2 * pair, 2 * pair + 1):
                    last = nc.tensor.matmul(ps[0:NKEY, W_BANK + pair % 2, (h % 2) * D:(h % 2 + 1) * D],
                                            vT[:, h, :], wo[:, h, :], start=True, stop=True)
                last.then_inc(vwo_psum_ready, 1)

        @block.vector
        def _(dve):
            s = Steps(dve, steps_done)
            dve.wait_ge(loaded, 16 * (7 if full else 8))
            at = GATE_XATTN + layer
            if full:
                s.link(nc.vector.tensor_tensor(gate[:, 0:1], g.gates[:, at:at + 1], g.gates[:, GATE_L3:GATE_L3 + 1], ALU.mult))
            elif layer == 1:
                s.link(nc.vector.tensor_copy(gate[:, 0:1], g.gates[:, at:at + 1]))
                s.link(nc.vector.tensor_scalar(mask[:], mask_in[:], -1e9, None, ALU.mult))
            else:
                s.link(nc.vector.tensor_scalar(mask[:], mask_in[:], 0.0, None, ALU.not_equal))
                s.link(nc.vector.tensor_reduce(gate[:, 1:2], mask[:], AX_X, ALU.max))
                s.link(nc.vector.reciprocal(gate[:, 1:2], gate[:, 1:2]))
                s.link(nc.vector.scalar_tensor_tensor(out=gate[:, 0:1], in0=gate[:, 1:2], scalar=0.0,
                                                      in1=g.gates[:, at:at + 1], op0=ALU.mult, op1=ALU.add))
                s.link(nc.vector.tensor_scalar(mask[:], mask_in[:], 0.0, MASKED, ALU.is_equal, ALU.mult))
            s.link(nc.vector.tensor_scalar(bo[:], bo[:], gate[0:1, 0:1], None, ALU.mult))
            for dst, bank, which, psum_ready, ready in ((kT, K_BANK, 1, kT_psum_ready, kT_ready),
                                                        (vT, V_BANK, 2, vT_psum_ready, vT_ready)):
                dve.wait_ge(psum_ready, 1)
                for j, h0, n in HEAD_BANKS:
                    src = ps[0:dh, bank + j, 0:n * NKEY].rearrange("p (h k) -> p h k", h=n)
                    if full:
                        last = nc.vector.tensor_copy(dst[:, h0:h0 + n, :], src)
                    else:
                        last = nc.vector.tensor_tensor(dst[:, h0:h0 + n, :], src, bias[:, which, h0:h0 + n].unsqueeze(2)
                                                       .broadcast_to([dh, n, NKEY]), ALU.add)
                last.then_inc(ready, 1)
            for m, bank in ((0, K_BANK), (1, V_BANK)):
                dve.wait_ge(a_psum_ready, m + 1)
                for j, h0, n in HEAD_BANKS:
                    last = nc.vector.tensor_scalar(scores_w[:, m, h0 * NKEY:(h0 + n) * NKEY], ps[:, bank + j, 0:n * NKEY],
                                                   scale, None, ALU.mult)
                last.then_inc(a_ready, 1)
            if not full:
                dve.wait_ge(row_psum_ready, 1)
                for j, h0, n in HEAD_BANKS:
                    last = nc.vector.scalar_tensor_tensor(
                        out=scores_b[0:1, h0 * NKEY:(h0 + n) * NKEY].rearrange("p (h k) -> p h k", h=n),
                        in0=ps[0:1, K_BANK + j, 0:n * NKEY].rearrange("p (h k) -> p h k", h=n), scalar=scale,
                        in1=mask[0:1, :].unsqueeze(1).broadcast_to([1, n, NKEY]), op0=ALU.mult, op1=ALU.add)
                last.then_inc(row_ready, 1)
            for pair in range(NH // 2):
                dve.wait_ge(vwo_psum_ready, pair + 1)
                nc.vector.tensor_scalar(vwo[:, 2 * pair:2 * pair + 2, :],
                                        ps[0:NKEY, W_BANK + pair % 2, :].rearrange("p (h n) -> p h n", h=2),
                                        gate[0:NKEY, 0:1], None, ALU.mult).then_inc(vwo_ready, 1)


def sign_network(nc, g, dram):
    F = dram["L0_ffn_k1"].shape[0]
    FC = F // P
    ps = g.ps
    with ExitStack() as ctx:
        st = Stage(nc, ctx, "sn")
        w0, w1, w2 = st.sb("w0", [P, DC, F]), st.sb("w1", [P, FC, F]), st.sb("w2", [P, FC, D])
        scales = st.sb("scales", [P, 4])
        prep_sign_weights(nc, g, dram, w0, w1, w2, scales)
        norm = Norm(nc, g, st)
        xn, xT = st.sb("xn", [P, D]), st.sb("xT", [P, DC, GROUP])
        h1, h2 = st.sb("h1", [P, FC, GROUP]), st.sb("h2", [P, FC, GROUP])
        steps_done = st.sem("steps_done")
        xn_ready, xT_psum_ready, xT_ready, h_psum_ready, h_ready, y_ready, y_used = (st.sem(n) for n in (
            "xn_ready", "xT_psum_ready", "xT_ready", "h_psum_ready", "h_ready", "y_ready", "y_used"))
        H_BANKS, XT, Y = 4, 4, 6
        block = st.block()

        @block.tensor
        def _(pe):
            with pe.Fori(0, NG) as gr:
                for j in range(TPG):
                    pe.wait_ge(xn_ready, gr * TPG + j + 1)
                    if j > 0:
                        pe.wait_ge(xT_ready, gr * TPG + j)
                    for c in range(DC):
                        last = nc.tensor.transpose(ps[:, XT, c * P:(c + 1) * P], xn[:, c * P:(c + 1) * P], g.ident[:])
                    last.then_inc(xT_psum_ready, 1)
                pe.wait_ge(xT_ready, gr * TPG + TPG)
                for m in range(2 * FC):
                    if m >= H_BANKS:
                        pe.wait_ge(h_ready, gr * (2 * FC) + m - H_BANKS + 1)
                    if m == FC:
                        pe.wait_ge(h_ready, gr * (2 * FC) + FC)
                    w, src, n = (w0, xT, DC) if m < FC else (w1, h1, FC)
                    for c in range(n):
                        last = nc.tensor.matmul(ps[:, m % H_BANKS, :], w[:, c, (m % FC) * P:(m % FC + 1) * P],
                                                src[:, c, :], start=(c == 0), stop=(c == n - 1))
                    last.then_inc(h_psum_ready, 1)
                pe.wait_ge(h_ready, gr * (2 * FC) + 2 * FC)
                for j in range(TPG):
                    if j >= 2:
                        pe.wait_ge(y_used, gr * TPG + j - 1)
                    for c in range(FC):
                        last = nc.tensor.matmul(ps[:, Y + j % 2, 0:D], h2[:, c, j * P:(j + 1) * P], w2[:, c, :],
                                                start=(c == 0), stop=(c == FC - 1))
                    last.then_inc(y_ready, 1)

        @block.gpsimd
        def _(pool):
            with pool.Fori(0, TILES) as n:
                norm.gpsimd(pool, n)

        @block.scalar
        def _(act):
            with act.Fori(0, NG) as gr:
                for m in range(2 * FC):
                    act.wait_ge(h_psum_ready, gr * (2 * FC) + m + 1)
                    dst, scale = (h1, scales[:, 0:1]) if m < FC else (h2, scales[:, 1:2])
                    nc.scalar.activation(dst[:, m % FC, :], ps[:, m % H_BANKS, :], ACT.Relu, scale=scale)\
                        .then_inc(h_ready, 1)

        @block.vector
        def _(dve):
            per = NORM_LINKS["layer"]
            with dve.Fori(0, NG) as gr:
                for j in range(TPG):
                    n = gr * TPG + j
                    s = Steps(dve, steps_done, n * per)
                    norm.vector(dve, s, n, tile_of(g.x, n), xn[:], "layer").then_inc(xn_ready, 1)
                    dve.wait_ge(xT_psum_ready, n + 1)
                    nc.vector.tensor_copy(xT[:, :, j * P:(j + 1) * P], ps[:, XT, 0:D].rearrange("p (c n) -> p c n", c=DC))\
                        .then_inc(xT_ready, 1)
                for j in range(TPG):
                    n = gr * TPG + j
                    dve.wait_ge(y_ready, n + 1)
                    nc.vector.scalar_tensor_tensor(out=tile_of(g.x, n), in0=ps[:, Y + j % 2, 0:D], scalar=scales[:, 2:3],
                                                   in1=tile_of(g.x, n), op0=ALU.mult, op1=ALU.add).then_inc(y_used, 1)
                    dve.wait_ge(y_used, n + 1)


def prep_sign_weights(nc, g, dram, w0, w1, w2, scales):
    F = dram["L0_ffn_k1"].shape[0]
    FC = F // P
    with ExitStack() as ctx:
        st = Stage(nc, ctx, "sp")
        b0, b1, b2 = st.sb("b0", [P, 2 * DC, F], U8), st.sb("b1", [P, FC, F], U8), st.sb("b2", [P, FC, D], U8)
        loaded, made = st.sem("loaded"), st.sem("made")
        diff_ready = st.sem("diff_ready")
        block = st.block()

        @block.sync
        def _(sp):
            for n, (t, name) in enumerate(((b0, "L0_ffn_k0"), (b2, "L0_ffn_k2"), (b1, "L0_ffn_k1"))):
                sp.dma_start(t[:], dram[name].rearrange("(c p) n -> p c n", p=P)).then_inc(loaded, 16)
            for n in range(3):
                sp.dma_start(scales[:, n:n + 1], dram[f"L0_ffn_s{n}"].partition_broadcast(P)).then_inc(loaded, 16)

        @block.vector
        def _(dve):
            dve.wait_ge(loaded, 96)
            nc.vector.tensor_tensor(w0[:], b0[:, 0:DC, :], b0[:, DC:2 * DC, :], ALU.subtract).then_inc(diff_ready, 1)
            nc.vector.tensor_scalar(w2[:], b2[:], 4.0, -2.0, ALU.mult, ALU.add)
            nc.vector.tensor_scalar(w1[:], b1[:], 8.0, -4.0, ALU.mult, ALU.add)
            nc.vector.tensor_tensor(scales[:, 2:3], scales[:, 2:3], g.gates[:, GATE_FFN:GATE_FFN + 1], ALU.mult)\
                .then_inc(made, 1)


def mixture(nc, g, dram, layer, src, acc, xT_all):
    E = 8
    K3 = 3 * E
    weights = dram[f"L{layer}_moe_w"]
    selector = dram[f"L{layer}_moe_sel"]
    chunks = weights.shape[0]
    inner_norm = layer == 3
    ps = g.ps
    with ExitStack() as outer:
        combT = Stage(nc, outer, f"mx{layer}").sb("combT", [K3, B * S], BF16)
        with ExitStack() as ctx:
            st = Stage(nc, ctx, f"rt{layer}")
            norm = Norm(nc, g, st)
            xn, xT = st.sb("xn", [P, D]), st.sb("xT", [P, DC, P])
            router, gain = st.sb("router", [P, DC, E]), st.sb("gain", [P, DC])
            bias, iota = st.sb("bias", [P, E]), st.sb("iota", [P, E])
            logits, top, expd, w2, where = (st.sb(n, [P, E]) for n in ("logits", "top", "expd", "w2", "where"))
            index, total = st.sb("index", [P, E], U32), st.sb("total", [P, 4])
            comb, other, rest = (st.sb(n, [P, E]) for n in ("comb", "other", "rest"))
            parts = st.sb("parts", [P, K3], BF16)
            loaded, steps_done, alone = st.sem("loaded"), st.sem("steps_done"), st.sem("alone")
            xn_ready, xT_psum_ready, xT_ready, xT_kept, logits_ready, shifted, exp_done, parts_ready, \
                combT_psum_ready, combT_ready, cleared = (st.sem(n) for n in (
                    "xn_ready", "xT_psum_ready", "xT_ready", "xT_kept", "logits_ready", "shifted", "exp_done",
                    "parts_ready", "combT_psum_ready", "combT_ready", "cleared"))
            XT, LG, CT = 0, 1, 2
            combT_psum = ps[0:K3, CT, 0:P // 2].bitcast(BF16)
            loads = 4 if layer == 1 else 3
            block = st.block()

            @block.sync
            def _(sp):
                sp.dma_start(router[:], dram[f"L{layer}_moe_router"].rearrange("(c p) e -> p c e", p=P)).then_inc(loaded, 16)
                sp.dma_start(iota[:], dram["iota8"].partition_broadcast(P)).then_inc(loaded, 16)
                if layer == 1:
                    sp.dma_start(bias[:], dram["L1_ffn_bs"].partition_broadcast(P)).then_inc(loaded, 16)
                sp.dma_start(gain[:], dram["L3_ffn_ln2"]).then_inc(loaded, 16)

            @block.tensor
            def _(pe):
                pe.wait_ge(loaded, 16 * loads)
                with pe.Fori(0, TILES) as t:
                    pe.wait_ge(xn_ready, t + 1)
                    for c in range(DC):
                        last = nc.tensor.transpose(ps[:, XT, c * P:(c + 1) * P], xn[:, c * P:(c + 1) * P], g.ident[:])
                    last.then_inc(xT_psum_ready, 1)
                    pe.wait_ge(xT_ready, t + 1)
                    for c in range(DC):
                        last = nc.tensor.matmul(ps[:, LG, 0:E], xT[:, c, :], router[:, c, :], start=(c == 0), stop=(c == DC - 1))
                    last.then_inc(logits_ready, 1)
                    pe.wait_ge(parts_ready, t + 1)
                    nc.tensor.transpose(combT_psum, parts[:], g.identb[:]).then_inc(combT_psum_ready, 1)

            @block.gpsimd
            def _(pool):
                if not inner_norm:
                    nc.gpsimd.memset(acc[:], 0.0).then_inc(cleared, 1)
                with pool.Fori(0, TILES) as t:
                    norm.gpsimd(pool, t)
                    pool.wait_ge(xT_ready, t + 1)
                    nc.gpsimd.tensor_copy(xT_all[:, :, bass.ds(t * P, P)], xT[:]).then_inc(xT_kept, 1)

            @block.scalar
            def _(act):
                with act.Fori(0, TILES) as t:
                    act.wait_ge(shifted, t + 1)
                    n = 2 if layer == 1 else E
                    nc.scalar.activation(expd[:, 0:n], w2[:, 0:n], ACT.Exp, accum_out=total[:, 0:1]).then_inc(exp_done, 1)

            @block.vector
            def _(dve):
                per = NORM_LINKS["rms" if inner_norm else "layer"] + (16 if inner_norm else 12)
                dve.wait_ge(loaded, 16 * loads)
                with dve.Fori(0, TILES) as t:
                    s = Steps(dve, steps_done, t * per)
                    kind = "rms" if inner_norm else "layer"
                    norm.vector(dve, s, t, tile_of(src, t), xn[:], kind).then_inc(xn_ready, 1)
                    dve.wait_ge(xT_psum_ready, t + 1)
                    for c in range(DC):
                        bank = ps[:, XT, c * P:(c + 1) * P]
                        if inner_norm:
                            last = nc.vector.tensor_scalar(xT[:, c, :], bank, gain[:, c:c + 1], None, ALU.mult)
                        else:
                            last = nc.vector.tensor_copy(xT[:, c, :], bank)
                    last.then_inc(xT_ready, 1)
                    dve.wait_ge(logits_ready, t + 1)
                    if layer == 1:
                        s.link(nc.vector.tensor_tensor(logits[:], ps[:, LG, 0:E], bias[:], ALU.add), alone)
                        s.link(nc.vector.max(top[:], logits[:]), alone)
                        s.link(nc.vector.max_index(index[:], top[:], logits[:]))
                        nc.vector.tensor_scalar(w2[:, 0:2], top[:, 0:2], top[:, 0:1], None, ALU.subtract).then_inc(shifted, 1)
                        dve.wait_ge(exp_done, t + 1)
                        s.link(nc.vector.reciprocal(total[:, 1:2], total[:, 0:1]))
                        s.link(nc.vector.tensor_scalar(w2[:, 0:2], expd[:, 0:2], total[:, 1:2], None, ALU.mult))
                    else:
                        s.link(nc.vector.tensor_copy(logits[:], ps[:, LG, 0:E]))
                        s.link(nc.vector.tensor_reduce(total[:, 2:3], logits[:], AX_X, ALU.max))
                        nc.vector.tensor_scalar(w2[:], logits[:], total[:, 2:3], None, ALU.subtract).then_inc(shifted, 1)
                        dve.wait_ge(exp_done, t + 1)
                        s.link(nc.vector.reciprocal(total[:, 1:2], total[:, 0:1]))
                        s.link(nc.vector.tensor_scalar(logits[:], expd[:], total[:, 1:2], None, ALU.mult), alone)
                        s.link(nc.vector.max(top[:], logits[:]), alone)
                        s.link(nc.vector.max_index(index[:], top[:], logits[:]))
                        s.link(nc.vector.tensor_tensor(total[:, 3:4], top[:, 0:1], top[:, 1:2], ALU.add))
                        s.link(nc.vector.reciprocal(total[:, 3:4], total[:, 3:4]))
                        s.link(nc.vector.tensor_scalar(w2[:, 0:2], top[:, 0:2], total[:, 3:4], None, ALU.mult))
                    s.link(nc.vector.tensor_copy(where[:, 0:2], index[:, 0:2]))
                    s.link(nc.vector.tensor_scalar(comb[:], iota[:], where[:, 0:1], w2[:, 0:1], ALU.is_equal, ALU.mult))
                    s.link(nc.vector.tensor_scalar(other[:], iota[:], where[:, 1:2], w2[:, 1:2], ALU.is_equal, ALU.mult))
                    s.link(nc.vector.tensor_tensor(comb[:], comb[:], other[:], ALU.add))
                    s.link(nc.vector.tensor_copy(parts[:, 0:E], comb[:]))
                    s.link(nc.vector.tensor_tensor(rest[:], comb[:], parts[:, 0:E], ALU.subtract))
                    s.link(nc.vector.tensor_copy(parts[:, E:2 * E], rest[:]))
                    nc.vector.tensor_tensor(parts[:, 2 * E:K3], rest[:], parts[:, E:2 * E], ALU.subtract).then_inc(parts_ready, 1)
                    dve.wait_ge(combT_psum_ready, t + 1)
                    nc.vector.tensor_copy(combT[:, bass.ds(t * P, P)], combT_psum).then_inc(combT_ready, 1)
                    dve.wait_ge(xT_kept, t + 1)
                    assert s.n == per, s.n

        with ExitStack() as ctx:
            st = Stage(nc, ctx, f"ex{layer}")
            slots = st.sb("slots", [P, 2, 3 * D])
            sels = st.sb("sels", [K3, 2, P], BF16)
            act_out, h = st.sb("act_out", [P, 2, GROUP]), st.sb("h", [P, 2, GROUP])
            slot_loaded = [st.sem(f"slot_loaded{n}") for n in range(2)]
            chunk_used, gate_up_ready, silu_done, gated, h_ready, y_ready, y_used = (st.sem(n) for n in (
                "chunk_used", "gate_up_ready", "silu_done", "gated", "h_ready", "y_ready", "y_used"))
            GATE, UP, SPREAD, Y = 0, 2, 4, 6
            tail = 1 if chunks % 2 else 2
            pairs = (chunks - tail) // 2
            block = st.block()

            def load(sp, c, slot):
                sp.dma_start(slots[:, slot, :], weights[bass.ds(c, 1)].rearrange("a p n -> p (a n)"))\
                    .then_inc(slot_loaded[slot], 16)
                sp.dma_start(sels[:, slot, :], selector[:, bass.ds(c * P, P)]).then_inc(slot_loaded[slot], 16)

            @block.sync
            def _(sp):
                for slot in range(2):
                    load(sp, slot, slot)
                with sp.Fori(1, pairs) as p:
                    for slot in range(2):
                        sp.wait_ge(chunk_used, 2 * p + slot - 1)
                        load(sp, 2 * p + slot, slot)
                for c in range(2 * pairs, chunks):
                    sp.wait_ge(chunk_used, c - 1)
                    load(sp, c, c % 2)

            @block.tensor
            def _(pe):
                def gate_up(c, slot, gr):
                    i = gr % 2
                    if gr == 0:
                        pe.wait_ge(slot_loaded[slot], 32 * (c // 2) + 32)
                    tokens = slice(gr * GROUP, (gr + 1) * GROUP)
                    for bank, w in ((GATE + i, 0), (UP + i, 1)):
                        for k in range(DC):
                            nc.tensor.matmul(ps[:, bank, :], slots[:, slot, (DC * w + k) * P:(DC * w + k + 1) * P],
                                             xT_all[:, k, tokens], start=(k == 0), stop=(k == DC - 1))
                    nc.tensor.matmul(ps[:, SPREAD + i, :], sels[:, slot, :], combT[:, tokens], start=True, stop=True)\
                        .then_inc(gate_up_ready, 1)

                def down(c, slot, gr, first=False):
                    unit = 4 * c + gr
                    pe.wait_ge(h_ready, unit + 1)
                    if not first:
                        pe.wait_ge(y_used, unit)
                    for j in range(TPG):
                        last = nc.tensor.matmul(ps[:, Y + j // 2, (j % 2) * D:(j % 2 + 1) * D],
                                                h[:, gr % 2, j * P:(j + 1) * P], slots[:, slot, 2 * DC * P:],
                                                start=True, stop=True)
                    last.then_inc(y_ready, 1)

                def chunk(c, slot, more, first=False):
                    for gr in range(NG):
                        if gr < NG - 1:
                            gate_up(c, slot, gr + 1)
                        elif more:
                            gate_up(c + 1, 1 - slot, 0)
                        down(c, slot, gr, first and gr == 0)

                gate_up(0, 0, 0)
                chunk(0, 0, True, first=True)
                chunk(1, 1, True)
                with pe.Fori(1, pairs) as p:
                    chunk(2 * p, 0, True)
                    chunk(2 * p + 1, 1, True)
                for c in range(2 * pairs, chunks):
                    chunk(c, c % 2, c < chunks - 1)

            @block.scalar
            def _(act):
                def unit_of(u, i):
                    act.wait_ge(gate_up_ready, u + 1)
                    nc.scalar.activation(act_out[:, i, :], ps[:, GATE + i, :], ACT.Silu).then_inc(silu_done, 1)

                with act.Fori(0, chunks * NG // 2) as k:
                    for i in range(2):
                        unit_of(2 * k + i, i)

            @block.vector
            def _(dve):
                def hidden(u, i):
                    dve.wait_ge(silu_done, u + 1)
                    nc.vector.tensor_tensor(act_out[:, i, :], act_out[:, i, :], ps[:, UP + i, :], ALU.mult).then_inc(gated, 1)
                    dve.wait_ge(gated, u + 1)
                    nc.vector.tensor_tensor(h[:, i, :], act_out[:, i, :], ps[:, SPREAD + i, :], ALU.mult).then_inc(h_ready, 1)

                def add_up(u, gr):
                    dve.wait_ge(y_ready, u + 1)
                    part = acc[:, gr * TPG:(gr + 1) * TPG, :].rearrange("p t n -> p (t n)")
                    nc.vector.tensor_tensor(part, part, ps[:, Y:Y + 2, :].rearrange("p b n -> p (b n)"), ALU.add)\
                        .then_inc(y_used, 1)
                    if gr == NG - 1:
                        dve.sem_inc(chunk_used, 1)

                hidden(0, 0)
                with dve.Fori(0, chunks - 1) as c:
                    for gr in range(NG):
                        hidden(NG * c + gr + 1, (gr + 1) % 2)
                        add_up(NG * c + gr, gr)
                last = NG * (chunks - 1)
                for gr in range(NG):
                    if gr < NG - 1:
                        hidden(last + gr + 1, (gr + 1) % 2)
                    add_up(last + gr, gr)
                dve.wait_ge(y_used, chunks * NG)


def expert_layer_1(nc, g, dram):
    with ExitStack() as ctx:
        st = Stage(nc, ctx, "m1")
        acc, xT_all = st.sb("acc", [P, TILES, D]), st.sb("xT_all", [P, DC, B * S])
        mixture(nc, g, dram, 1, g.x, acc, xT_all)
        add_gated(nc, g, acc, 1)


def add_gated(nc, g, acc, layer):
    with ExitStack() as ctx:
        st = Stage(nc, ctx, f"ag{layer}")
        added = st.sem("added")
        block = st.block()

        @block.vector
        def _(dve):
            at = GATE_FFN + layer
            nc.vector.scalar_tensor_tensor(out=g.x[:], in0=acc[:], scalar=g.gates[:, at:at + 1], in1=g.x[:],
                                           op0=ALU.mult, op1=ALU.add).then_inc(added, 1)
            dve.wait_ge(added, 1)


def product_key_experts(nc, g, dram):
    HEADS, KEYS, TOP = 8, 64, 16
    EXPERTS = KEYS * KEYS
    EC = EXPERTS // P
    SIDES = 2 * HEADS
    BLK = 1024
    IB = BLK // KEYS
    ps = g.ps
    with ExitStack() as ctx:
        st = Stage(nc, ctx, "pk")
        sim_w = st.sb("sim_w", [P, DC, SIDES * KEYS])
        fold_product_keys(nc, g, dram, sim_w)
        downT, up = st.sb("downT", [P, DC, EXPERTS]), st.sb("up", [P, EC, D])
        gain = st.sb("gain", [P, DC])
        norm, norm2 = Norm(nc, g, st), Norm(nc, g, st, "2")
        xn, xT = st.sb("xn", [P, D]), st.sb("xT", [P, DC, P])
        sims, rest = st.sb("sims", [P, SIDES, KEYS]), st.sb("rest", [P, SIDES, KEYS])
        best = st.sb("best", [P, SIDES, TOP])
        pairs = st.sb("pairs", [P, HEADS, TOP * TOP])
        top = st.sb("top", [P, HEADS, TOP])
        least = st.sb("least", [P, HEADS])
        sums, kept = st.sb("sums", [P, 2, BLK]), st.sb("kept", [P, BLK])
        weight, hidden = st.sb("weight", [P, EXPERTS]), st.sb("hidden", [P, EXPERTS])
        hT = st.sb("hT", [P, 2, 4 * P])
        loaded, steps_done, alone = st.sem("loaded"), st.sem("steps_done"), st.sem("alone")
        xn_ready, xT_psum_ready, xT_ready, sims_psum_ready, sims_ready, least_ready, sums_ready, sums_used, \
            weight_ready, hid_psum_ready, gelu_done, hidden_ready, hT_psum_ready, hT_ready, y_ready, tile_done = (
                st.sem(n) for n in (
                    "xn_ready", "xT_psum_ready", "xT_ready", "sims_psum_ready", "sims_ready", "least_ready",
                    "sums_ready", "sums_used", "weight_ready", "hid_psum_ready", "gelu_done", "hidden_ready",
                    "hT_psum_ready", "hT_ready", "y_ready", "tile_done"))
        SIM, XT, HID, HT, Y = 0, 2, 3, 5, 7
        HB = EXPERTS // 512
        UNITS = (EXPERTS // BLK) * HEADS
        block = st.block()

        @block.sync
        def _(sp):
            sp.dma_start(gain[:], dram["L2_ffn_norm"]).then_inc(loaded, 16)
            sp.dma_start(downT[:], dram["L2_ffn_downT"].rearrange("(c p) e -> p c e", p=P)).then_inc(loaded, 16)
            sp.dma_start(up[:], dram["L2_ffn_expert_up"].rearrange("(c p) n -> p c n", p=P)).then_inc(loaded, 16)

        @block.tensor
        def _(pe):
            pe.wait_ge(loaded, 48)
            with pe.Fori(0, TILES) as t:
                pe.wait_ge(xn_ready, t + 1)
                for c in range(DC):
                    last = nc.tensor.transpose(ps[:, XT, c * P:(c + 1) * P], xn[:, c * P:(c + 1) * P], g.ident[:])
                last.then_inc(xT_psum_ready, 1)
                pe.wait_ge(xT_ready, t + 1)
                for j in range(2):
                    for c in range(DC):
                        last = nc.tensor.matmul(ps[:, SIM + j, :], xT[:, c, :], sim_w[:, c, j * 512:(j + 1) * 512],
                                                start=(c == 0), stop=(c == DC - 1))
                last.then_inc(sims_psum_ready, 1)
                for k in range(HB):
                    if k >= 2:
                        pe.wait_ge(gelu_done, HB * t + k - 1)
                    for c in range(DC):
                        last = nc.tensor.matmul(ps[:, HID + k % 2, :], xT[:, c, :], downT[:, c, k * 512:(k + 1) * 512],
                                                start=(c == 0), stop=(c == DC - 1))
                    last.then_inc(hid_psum_ready, 1)

                def turn(k):
                    pe.wait_ge(hidden_ready, HB * t + k + 1)
                    if k >= 2:
                        pe.wait_ge(hT_ready, HB * t + k - 1)
                    for i in range(4):
                        last = nc.tensor.transpose(ps[:, HT + k % 2, i * P:(i + 1) * P],
                                                   hidden[:, (4 * k + i) * P:(4 * k + i + 1) * P], g.ident[:])
                    last.then_inc(hT_psum_ready, 1)

                turn(0)
                for k in range(HB):
                    if k < HB - 1:
                        turn(k + 1)
                    pe.wait_ge(hT_ready, HB * t + k + 1)
                    for i in range(4):
                        last = nc.tensor.matmul(ps[:, Y, 0:D], hT[:, k % 2, i * P:(i + 1) * P], up[:, 4 * k + i, :],
                                                start=(k == 0 and i == 0), stop=(k == HB - 1 and i == 3))
                last.then_inc(y_ready, 1)

        @block.gpsimd
        def _(pool):
            with pool.Fori(0, TILES) as t:
                norm.gpsimd(pool, t)
                norm2.gpsimd(pool, t)
                pool.wait_ge(sims_ready, t + 1)
                for u in range(UNITS):
                    q, head = u // HEADS, u % HEADS
                    if u >= 2:
                        pool.wait_ge(sums_used, UNITS * t + u - 1)
                    first = sims[:, 2 * head, q * IB:(q + 1) * IB].unsqueeze(2).broadcast_to([P, IB, KEYS])
                    second = sims[:, 2 * head + 1, :].unsqueeze(1).broadcast_to([P, IB, KEYS])
                    nc.gpsimd.tensor_tensor(sums[:, u % 2, :].rearrange("p (i j) -> p i j", i=IB), first, second, ALU.add)\
                        .then_inc(sums_ready, 1)

        @block.scalar
        def _(act):
            with act.Fori(0, TILES) as t:
                for k in range(HB):
                    act.wait_ge(hid_psum_ready, HB * t + k + 1)
                    nc.scalar.activation(hidden[:, k * 512:(k + 1) * 512], ps[:, HID + k % 2, :], ACT.Gelu).then_inc(gelu_done, 1)
                for k in range(HB):
                    act.wait_ge(hT_psum_ready, HB * t + k + 1)
                    nc.scalar.activation(hT[:, k % 2, :], ps[:, HT + k % 2, :], ACT.Copy).then_inc(hT_ready, 1)

        @block.vector
        def _(dve):
            per = NORM_LINKS["layer"] + NORM_LINKS["rms"] + 9 + UNITS - EXPERTS // BLK
            dve.wait_ge(loaded, 48)
            with dve.Fori(0, TILES) as t:
                s = Steps(dve, steps_done, t * per)
                x = tile_of(g.x, t)
                s.link(norm.vector(dve, s, t, x, xn[:], "layer"))
                norm2.vector(dve, s, t, xn[:], xn[:], "rms").then_inc(xn_ready, 1)
                dve.wait_ge(xT_psum_ready, t + 1)
                for c in range(DC):
                    last = nc.vector.tensor_scalar(xT[:, c, :], ps[:, XT, c * P:(c + 1) * P], gain[:, c:c + 1], None, ALU.mult)
                last.then_inc(xT_ready, 1)
                dve.wait_ge(sims_psum_ready, t + 1)
                nc.vector.tensor_copy(sims[:].rearrange("p s k -> p (s k)"),
                                      ps[:, SIM:SIM + 2, :].rearrange("p b n -> p (b n)")).then_inc(sims_ready, 1)
                dve.wait_ge(sims_ready, t + 1)
                dve.sem_inc(alone, 1)
                for k in range(SIDES):
                    last = nc.vector.max(best[:, k, 0:8], sims[:, k, :])
                s.link(last, alone)
                for k in range(SIDES):
                    last = nc.vector.match_replace(rest[:, k, :], best[:, k, 0:8], sims[:, k, :], MASKED)
                s.link(last, alone)
                for k in range(SIDES):
                    last = nc.vector.max(best[:, k, 8:16], rest[:, k, :])
                s.link(last)
                for head in range(HEADS):
                    last = nc.vector.tensor_tensor(pairs[:, head, :].rearrange("p (i j) -> p i j", i=TOP),
                                                   best[:, 2 * head, :].unsqueeze(2).broadcast_to([P, TOP, TOP]),
                                                   best[:, 2 * head + 1, :].unsqueeze(1).broadcast_to([P, TOP, TOP]), ALU.add)
                s.link(last, alone)
                for head in range(HEADS):
                    last = nc.vector.max(top[:, head, 0:8], pairs[:, head, :])
                s.link(last, alone)
                for head in range(HEADS):
                    last = nc.vector.match_replace(pairs[:, head, :], top[:, head, 0:8], pairs[:, head, :], MASKED)
                s.link(last, alone)
                for head in range(HEADS):
                    last = nc.vector.max(top[:, head, 8:16], pairs[:, head, :])
                s.link(last)
                s.link(nc.vector.tensor_scalar(least[:], top[:, :, TOP - 1], 0.0, None, ALU.max))
                for u in range(UNITS):
                    q, head = u // HEADS, u % HEADS
                    dve.wait_ge(sums_ready, UNITS * t + u + 1)
                    part = weight[:, q * BLK:(q + 1) * BLK]
                    dst = part if head == 0 else kept[:]
                    ins = nc.vector.scalar_tensor_tensor(out=dst, in0=sums[:, u % 2, :], scalar=least[:, head:head + 1],
                                                         in1=sums[:, u % 2, :], op0=ALU.is_ge, op1=ALU.mult)
                    ins.then_inc(sums_used, 1)
                    dve.wait_ge(sums_used, UNITS * t + u + 1)
                    if head > 0:
                        s.link(nc.vector.tensor_tensor(part, part, kept[:], ALU.add))
                for k in range(HB):
                    dve.wait_ge(gelu_done, HB * t + k + 1)
                    part = slice(k * 512, (k + 1) * 512)
                    nc.vector.tensor_tensor(hidden[:, part], hidden[:, part], weight[:, part], ALU.mult).then_inc(hidden_ready, 1)
                dve.wait_ge(y_ready, t + 1)
                nc.vector.scalar_tensor_tensor(out=x, in0=ps[:, Y, 0:D], scalar=g.gates[:, GATE_FFN + 2:GATE_FFN + 3], in1=x,
                                               op0=ALU.mult, op1=ALU.add).then_inc(tile_done, 1)
                dve.wait_ge(tile_done, t + 1)
                assert s.n == per, (s.n, per)


def fold_product_keys(nc, g, dram, sim_w):
    SIDES, KEYS = dram["L2_ffn_keysT"].shape[1:]
    ps = g.ps
    with ExitStack() as ctx:
        st = Stage(nc, ctx, "fk")
        wqT, keysT = st.sb("wqT", [P, SIDES, D]), st.sb("keysT", [P, SIDES, KEYS])
        loaded, psum_ready, made = st.sem("loaded"), st.sem("psum_ready"), st.sem("made")
        block = st.block()

        @block.sync
        def _(sp):
            sp.dma_start(wqT[:], dram["L2_ffn_wqT"]).then_inc(loaded, 16)
            sp.dma_start(keysT[:], dram["L2_ffn_keysT"]).then_inc(loaded, 16)

        @block.tensor
        def _(pe):
            pe.wait_ge(loaded, 32)
            for c in range(DC):
                for k in range(SIDES):
                    last = nc.tensor.matmul(ps[:, 2 * c + k // 8, (k % 8) * KEYS:(k % 8 + 1) * KEYS],
                                            wqT[:, k, c * P:(c + 1) * P], keysT[:, k, :], start=True, stop=True)
                last.then_inc(psum_ready, 1)

        @block.vector
        def _(dve):
            for c in range(DC):
                dve.wait_ge(psum_ready, c + 1)
                nc.vector.tensor_copy(sim_w[:, c, :], ps[:, 2 * c:2 * c + 2, :].rearrange("p b n -> p (b n)"))\
                    .then_inc(made, 1)


def causal_attention_block(nc, g, dram, inner):
    for b in range(B):
        project_heads(nc, g, dram, b, inner)
        attend_heads(nc, g, dram, b, inner)


HEAD, NKV = 16, 4
QKV = (NH + 2 * NKV) * HEAD
QK = (NH + NKV) * HEAD


def project_heads(nc, g, dram, b, inner):
    HALF = HEAD // 2
    heads = NH + NKV
    ps = g.ps
    g.qkT = nc.dram_tensor(f"qkT{b}", (QK, S), F32).ap()
    g.values = nc.dram_tensor(f"values{b}", (NKV, P, TB, HEAD), F32).ap()
    with ExitStack() as ctx:
        st = Stage(nc, ctx, f"ph{b}")
        wqkv, gain = st.sb("wqkv", [P, DC, QKV]), st.sb("gain", [P, DC])
        cos, sin = st.sb("cos", [P, TB, HALF]), st.sb("sin", [P, TB, HALF])
        norm, norm2 = Norm(nc, g, st), Norm(nc, g, st, "2")
        xn, xT = st.sb("xn", [P, D]), st.sb("xT", [P, DC, P])
        qkv, turned = st.sb("qkv", [P, QKV]), st.sb("turned", [P, QK])
        prods = [st.sb(f"prod{n}", [P, heads, HALF]) for n in range(4)]
        qkT = st.sb("qkT", [P, 3, P])
        loaded, steps_done, prods_ready = st.sem("loaded"), st.sem("steps_done"), st.sem("prods_ready")
        xn_ready, xT_psum_ready, xT_ready, qkv_psum_ready, qkv_ready, turned_ready, qkT_psum_ready, qkT_ready, stored, \
            values_stored = (st.sem(n) for n in (
                "xn_ready", "xT_psum_ready", "xT_ready", "qkv_psum_ready", "qkv_ready", "turned_ready",
                "qkT_psum_ready", "qkT_ready", "stored", "values_stored"))
        XT, QP, TP = 0, 1, 2
        block = st.block()

        @block.sync
        def _(sp):
            sp.dma_start(wqkv[:], dram["L3_ffn_wqkvT"].rearrange("(c p) n -> p c n", p=P)).then_inc(loaded, 16)
            sp.dma_start(gain[:], dram["L3_ffn_ln1"]).then_inc(loaded, 16)
            sp.dma_start(cos[:], dram["rope_cos"].rearrange("(t p) n -> p t n", p=P)).then_inc(loaded, 16)
            sp.dma_start(sin[:], dram["rope_sin"].rearrange("(t p) n -> p t n", p=P)).then_inc(loaded, 16)
            with sp.Fori(0, TB) as t:
                sp.wait_ge(qkv_ready, t + 1)
                sp.dma_start(g.values[:, :, bass.ds(t, 1), :].rearrange("h p a n -> p h (a n)"),
                             qkv[:, QK:].rearrange("p (h n) -> p h n", h=NKV)).then_inc(values_stored, 16)
                sp.wait_ge(qkT_ready, t + 1)
                for c in range(3):
                    rows = min(P, QK - c * P)
                    sp.dma_start(g.qkT[c * P:c * P + rows, bass.ds(t * P, P)], qkT[0:rows, c, :]).then_inc(stored, 16)
            sp.wait_ge(stored, 48 * TB)
            sp.wait_ge(values_stored, 16 * TB)

        @block.tensor
        def _(pe):
            pe.wait_ge(loaded, 64)
            with pe.Fori(0, TB) as t:
                pe.wait_ge(xn_ready, t + 1)
                for c in range(DC):
                    last = nc.tensor.transpose(ps[:, XT, c * P:(c + 1) * P], xn[:, c * P:(c + 1) * P], g.ident[:])
                last.then_inc(xT_psum_ready, 1)
                pe.wait_ge(xT_ready, t + 1)
                for c in range(DC):
                    last = nc.tensor.matmul(ps[:, QP, 0:QKV], xT[:, c, :], wqkv[:, c, :], start=(c == 0), stop=(c == DC - 1))
                last.then_inc(qkv_psum_ready, 1)
                pe.wait_ge(turned_ready, t + 1)
                for c in range(3):
                    rows = min(P, QK - c * P)
                    last = nc.tensor.transpose(ps[0:rows, TP, c * P:(c + 1) * P], turned[:, c * P:c * P + rows], g.ident[:])
                last.then_inc(qkT_psum_ready, 1)

        @block.gpsimd
        def _(pool):
            with pool.Fori(0, TB) as t:
                norm.gpsimd(pool, t)
                norm2.gpsimd(pool, t)

        @block.vector
        def _(dve):
            per = NORM_LINKS["layer"] + NORM_LINKS["rms"] + 1
            dve.wait_ge(loaded, 64)
            with dve.Fori(0, TB) as t:
                s = Steps(dve, steps_done, t * per)
                own = tile_of(inner, b * TB + t)
                s.link(norm.vector(dve, s, t, tile_of(g.x, b * TB + t), own, "layer"), norm.waits_alone)
                norm2.vector(dve, s, t, own, xn[:], "rms").then_inc(xn_ready, 1)
                dve.wait_ge(xT_psum_ready, t + 1)
                for c in range(DC):
                    last = nc.vector.tensor_scalar(xT[:, c, :], ps[:, XT, c * P:(c + 1) * P], gain[:, c:c + 1], None, ALU.mult)
                last.then_inc(xT_ready, 1)
                dve.wait_ge(qkv_psum_ready, t + 1)
                nc.vector.tensor_copy(qkv[:], ps[:, QP, 0:QKV]).then_inc(qkv_ready, 1)
                dve.wait_ge(qkv_ready, t + 1)
                pair = qkv[:, 0:QK].rearrange("p (h s n) -> p s h n", s=2, n=HALF)
                out = turned[:].rearrange("p (h s n) -> p s h n", s=2, n=HALF)
                tables = [tab[:, bass.ds(t, 1), :].broadcast_to([P, heads, HALF]) for tab in (cos, sin)]
                for k, (half, table) in enumerate(((0, 0), (1, 1), (1, 0), (0, 1))):
                    last = nc.vector.tensor_tensor(prods[k][:], pair[:, half], tables[table], ALU.mult)
                last.then_inc(prods_ready, 1)
                dve.wait_ge(prods_ready, t + 1)
                nc.vector.tensor_tensor(out[:, 0], prods[0][:], prods[1][:], ALU.subtract)
                nc.vector.tensor_tensor(out[:, 1], prods[2][:], prods[3][:], ALU.add).then_inc(turned_ready, 1)
                dve.wait_ge(qkT_psum_ready, t + 1)
                nc.vector.tensor_scalar(qkT[:, 0:2, :], ps[:, TP, 0:2 * P].rearrange("p (c n) -> p c n", c=2),
                                        HEAD ** -0.5, None, ALU.mult)
                nc.vector.tensor_copy(qkT[0:QK - 2 * P, 2, :], ps[0:QK - 2 * P, TP, 2 * P:3 * P]).then_inc(qkT_ready, 1)
                dve.wait_ge(values_stored, 16 * t + 16)
                dve.wait_ge(stored, 48 * t + 48)


def attend_heads(nc, g, dram, b, inner):
    ps = g.ps
    with ExitStack() as ctx:
        st = Stage(nc, ctx, f"ah{b}")
        q, k, v = st.sb("q", [HEAD, 2, S]), st.sb("k", [HEAD, 2, S]), st.sb("v", [P, 2, TB, HEAD])
        probs, probsT = st.sb("probs", [P, 2, S]), st.sb("probsT", [P, 2, S])
        lowest, total, share = st.sb("lowest", [P, 2]), st.sb("total", [P, 2]), st.sb("share", [P, 2])
        attended = st.sb("attended", [P, TB, NH * HEAD])
        wo = st.sb("wo", [P, DC, D])
        row, rowT = st.sb("row", [P, D]), st.sb("rowT", [P, DC, P])
        head_loaded = [st.sem(f"head_loaded{n}") for n in range(2)]
        wo_loaded = st.sem("wo_loaded")
        scores_ready, masked, max_ready, exp_done, pT_psum_ready, pT_ready, o_ready, share_ready, unit_done, \
            row_ready, rowT_psum_ready, rowT_ready, y_ready, tile_done = (st.sem(n) for n in (
                "scores_ready", "masked", "max_ready", "exp_done", "pT_psum_ready", "pT_ready", "o_ready", "share_ready",
                "unit_done", "row_ready", "rowT_psum_ready", "rowT_ready", "y_ready", "tile_done"))
        SC, PT, O = 0, 4, 6
        UNITS = TB
        block = st.block()

        def banks(first, n):
            return ps[:, first:first + 2, :].rearrange("p b n -> p (b n)")[:, 0:n]

        @block.sync
        def _(sp):
            sp.dma_start(wo[:], dram["L3_ffn_woT"].rearrange("(c p) n -> p c n", p=P)).then_inc(wo_loaded, 16)

            def load(h, slot):
                for dst, src in ((q, g.qkT[bass.ds(h * HEAD, HEAD), :]),
                                 (k, g.qkT[bass.ds(NH * HEAD + (h // (NH // NKV)) * HEAD, HEAD), :])):
                    sp.dma_start(dst[:, slot, :], src).then_inc(head_loaded[slot], 16)
                sp.dma_start(v[:, slot], g.values[bass.ds(h // (NH // NKV), 1)].rearrange("a p t n -> p (a t) n"))\
                    .then_inc(head_loaded[slot], 16)

            load(0, 0)
            load(1, 1)
            with sp.Fori(1, NH // 2) as pair:
                for slot in range(2):
                    sp.wait_ge(unit_done, UNITS * (2 * pair + slot - 1))
                    load(2 * pair + slot, slot)

        @block.tensor
        def _(pe):
            def scores(u, slot, i):
                for j in range(0, i + 1, 4):
                    n = min(4, i + 1 - j) * P
                    last = nc.tensor.matmul(ps[:, SC + 2 * (i % 2) + j // 4, 0:n], q[:, slot, i * P:(i + 1) * P],
                                            k[:, slot, j * P:j * P + n], start=True, stop=True)
                last.then_inc(scores_ready, 1)

            with pe.Fori(0, NH // 2) as pair:
                for slot in range(2):
                    head = 2 * pair + slot
                    pe.wait_ge(head_loaded[slot], 48 * pair + 48)
                    for i in range(TB + 1):
                        if i < TB:
                            scores(UNITS * head + i, slot, i)
                        if i == 0:
                            continue
                        n, u = i, UNITS * head + i - 1
                        pe.wait_ge(exp_done, u + 1)
                        for j in range(n):
                            last = nc.tensor.transpose(ps[:, PT + j // 4, (j % 4) * P:(j % 4 + 1) * P],
                                                       probs[:, (n - 1) % 2, j * P:(j + 1) * P], g.ident[:])
                        last.then_inc(pT_psum_ready, 1)
                        pe.wait_ge(pT_ready, u + 1)
                        for j in range(n):
                            last = nc.tensor.matmul(ps[:, O + (n - 1) % 2, 0:HEAD], probsT[:, (n - 1) % 2, j * P:(j + 1) * P],
                                                    v[:, slot, j, :], start=(j == 0), stop=(j == n - 1))
                        last.then_inc(o_ready, 1)
            pe.wait_ge(wo_loaded, 16)
            with pe.Fori(0, TB) as t:
                pe.wait_ge(row_ready, t + 1)
                for c in range(DC):
                    last = nc.tensor.transpose(ps[:, PT, c * P:(c + 1) * P], row[:, c * P:(c + 1) * P], g.ident[:])
                last.then_inc(rowT_psum_ready, 1)
                pe.wait_ge(rowT_ready, t + 1)
                for c in range(DC):
                    last = nc.tensor.matmul(ps[:, SC, 0:D], rowT[:, c, :], wo[:, c, :], start=(c == 0), stop=(c == DC - 1))
                last.then_inc(y_ready, 1)

        @block.scalar
        def _(act):
            with act.Fori(0, NH // 2) as pair:
                for slot in range(2):
                    for i in range(TB):
                        u = UNITS * (2 * pair + slot) + i
                        act.wait_ge(max_ready, u + 1)
                        n = (i + 1) * P
                        nc.scalar.activation(probs[:, i % 2, 0:n], banks(SC + 2 * (i % 2), n), ACT.Exp,
                                             bias=lowest[:, i % 2:i % 2 + 1], accum_out=total[:, i % 2:i % 2 + 1])\
                            .then_inc(exp_done, 1)

        @block.vector
        def _(dve):
            def finish(u, slot, i, head):
                n = (i + 1) * P
                dve.wait_ge(pT_psum_ready, u + 1)
                nc.vector.tensor_copy(probsT[:, i % 2, 0:n], banks(PT, n)).then_inc(pT_ready, 1)
                dve.wait_ge(exp_done, u + 1)
                nc.vector.reciprocal(share[:, i % 2:i % 2 + 1], total[:, i % 2:i % 2 + 1]).then_inc(share_ready, 1)
                dve.wait_ge(share_ready, u + 1)
                dve.wait_ge(o_ready, u + 1)
                nc.vector.tensor_scalar(attended[:, i, bass.ds(head * HEAD, HEAD)], ps[:, O + i % 2, 0:HEAD],
                                        share[:, i % 2:i % 2 + 1], None, ALU.mult).then_inc(unit_done, 1)

            with dve.Fori(0, NH // 2) as pair:
                for slot in range(2):
                    head = 2 * pair + slot
                    for i in range(TB):
                        u = UNITS * head + i
                        n = (i + 1) * P
                        bank = banks(SC + 2 * (i % 2), n)
                        dve.wait_ge(scores_ready, u + 1)
                        nc.vector.tensor_tensor(bank[:, n - P:n], bank[:, n - P:n], g.causal[:], ALU.add).then_inc(masked, 1)
                        dve.wait_ge(masked, u + 1)
                        nc.vector.tensor_reduce(lowest[:, i % 2:i % 2 + 1], bank, AX_X, ALU.max, negate=True)\
                            .then_inc(max_ready, 1)
                        if i > 0:
                            finish(u - 1, slot, i - 1, head)
                    finish(UNITS * head + TB - 1, slot, TB - 1, head)
            with dve.Fori(0, TB) as t:
                nc.vector.tensor_copy(row[:], tile_of(attended, t)).then_inc(row_ready, 1)
                dve.wait_ge(rowT_psum_ready, t + 1)
                nc.vector.tensor_copy(rowT[:], ps[:, PT, 0:D].rearrange("p (c n) -> p c n", c=DC)).then_inc(rowT_ready, 1)
                dve.wait_ge(y_ready, t + 1)
                own = tile_of(inner, b * TB + t)
                nc.vector.tensor_tensor(own, own, ps[:, SC, 0:D], ALU.add).then_inc(tile_done, 1)
                dve.wait_ge(tile_done, t + 1)


def transformer_layer_3(nc, g, dram):
    with ExitStack() as ctx:
        st = Stage(nc, ctx, "m3")
        inner = st.sb("inner", [P, TILES, D])
        causal_attention_block(nc, g, dram, inner)
        xT_all = st.sb("xT_all", [P, DC, B * S])
        mixture(nc, g, dram, 3, inner, inner, xT_all)
        add_gated(nc, g, inner, 3)


class Shared:
    pass


def attention_layer(layer):
    def stage(nc, g, dram):
        for b in range(B):
            cross_attention(nc, g, dram, layer, b)
    return stage


STAGES = [(1, linear_attention), (2, sign_network), (3, attention_layer(1)), (4, expert_layer_1), (5, attention_layer(2)), (6, product_key_experts), (7, attention_layer(3)),
          (8, transformer_layer_3)]


def build(nc, dram, out, upto=99):
    with ExitStack() as ctx:
        g = Shared()
        st = Stage(nc, ctx, "g")
        g.x = st.sb("x", [P, TILES, D])
        g.gates = st.sb("gates", [P, 16])
        g.ident = st.sb("ident", [P, P])
        g.identb = st.sb("identb", [P, P], BF16)
        g.minus_half = st.sb("minus_half", [P, 2])
        g.ones = st.sb("ones", [P, P])
        g.causal = st.sb("causal", [P, P])
        g.ps = ctx.enter_context(nc.psum_tensor("ps", [P, 8, 512], F32))
        load_stream(nc, g, dram)
        for n, stage in STAGES:
            if n <= upto:
                stage(nc, g, dram)
        store_stream(nc, g, out)


def expert_chunks(gate, up, down):
    n = gate.shape[1] // P
    left = [w.reshape(DC, P, n, P).transpose(2, 1, 0, 3).reshape(n, P, DC * P) for w in (gate, up)]
    return np.concatenate([*left, down.reshape(n, P, D)], axis=2)


def expert_selector(experts, hidden):
    return np.tile(np.kron(np.eye(experts), np.ones((1, hidden))), (3, 1)).astype(mybir.dt.np(BF16))


def lay_out(v):
    a = {k: np.asarray(x) for k, x in v.items()}
    a["ctxT"] = a["ctx_1024"].transpose(0, 2, 1)
    a["L0_xattn_WqT"] = a["L0_xattn_Wq"].T
    a["maskT_ff1"] = a["mask_BxS2x1_ff1"][:, :, 0].T
    for n in (1, 2):
        a[f"L{n}_xattn_WqT"] = a[f"L{n}_xattn_Wq"].reshape(D, NH, D // NH).transpose(2, 1, 0)
        a[f"L{n}_xattn_bias"] = np.stack([a[f"L{n}_xattn_b{w}"].reshape(NH, D // NH) for w in "qkv"]).transpose(2, 0, 1)
    a["L3_xattn_WqT"] = a["L3_xattn_w_q"].reshape(D, NH, -1).transpose(2, 1, 0)
    a["L3_xattn_Wk"], a["L3_xattn_Wv"] = np.split(a["L3_xattn_w_kv"], 2, axis=1)
    a["L3_xattn_Wo"], a["L3_xattn_bo"] = a["L3_xattn_w_out"], a["L3_xattn_b_out"]
    a["L3_xattn_affine"] = np.stack([a["L3_xattn_ln_gamma"], a["L3_xattn_ln_beta"]]).reshape(2, DC, P).transpose(2, 0, 1)
    a["L1_xattn_mask"], a["L2_xattn_mask"] = a["mask_Bx1x1xS2_fk0"][:, 0, 0], a["mask_BxS2_ik0"]
    used = [f"L{n}_xattn_{w}" for n in (1, 2, 3) for w in ("WqT", "Wk", "Wv", "Wo", "bo")]
    used += ["L1_xattn_bias", "L2_xattn_bias", "L1_xattn_mask", "L2_xattn_mask", "L3_xattn_affine"]
    for n in range(3):
        a[f"L0_ffn_s{n}"] = a[f"L0_ffn_s{n}"].reshape(1)
        used += [f"L0_ffn_k{n}", f"L0_ffn_s{n}"]
    e, _, f = a["L1_ffn_Wg"].shape
    a["L1_moe_w"] = expert_chunks(a["L1_ffn_Wg"].transpose(1, 0, 2).reshape(D, e * f),
                                  a["L1_ffn_Wu"].transpose(1, 0, 2).reshape(D, e * f), a["L1_ffn_Wd"].reshape(e * f, D))
    a["L1_moe_sel"], a["L1_moe_router"] = expert_selector(e, f), a["L1_ffn_Ws"]
    f = a["L3_ffn_w2"].shape[2]
    gate, up = a["L3_ffn_w13"][:, :f], a["L3_ffn_w13"][:, f:]
    a["L3_moe_w"] = expert_chunks(gate.reshape(e * f, D).T, up.reshape(e * f, D).T,
                                  a["L3_ffn_w2"].transpose(0, 2, 1).reshape(e * f, D))
    a["L3_moe_sel"], a["L3_moe_router"] = expert_selector(e, f), a["L3_ffn_gate_w"].T
    a["L3_ffn_ln2"] = a["L3_ffn_ln2_w"].reshape(DC, P).T
    a["iota8"] = np.arange(8, dtype=np.float32)
    used += ["L1_moe_w", "L1_moe_sel", "L1_moe_router", "L1_ffn_bs", "L3_moe_w", "L3_moe_sel", "L3_moe_router",
             "L3_ffn_ln2", "iota8"]
    a["L2_ffn_wqT"] = a["L2_ffn_wq"].reshape(D, 16, P).transpose(2, 1, 0)
    a["L2_ffn_keysT"] = a["L2_ffn_keys"].transpose(3, 0, 2, 1).reshape(P, 16, 64)
    a["L2_ffn_downT"] = a["L2_ffn_expert_down"].T
    a["L2_ffn_norm"] = a["L2_ffn_norm_w"].reshape(DC, P).T
    used += ["L2_ffn_wqT", "L2_ffn_keysT", "L2_ffn_downT", "L2_ffn_norm", "L2_ffn_expert_up"]
    a["L3_ffn_wqkvT"], a["L3_ffn_woT"] = a["L3_ffn_wqkv"].T, a["L3_ffn_wo"].T
    a["L3_ffn_ln1"] = a["L3_ffn_ln1_w"].reshape(DC, P).T
    freq = np.float32(1.0) / np.float32(10000.0) ** (np.arange(0, HEAD, 2, dtype=np.float32) / np.float32(HEAD))
    angle = np.arange(S, dtype=np.float32)[:, None] * freq[None, :]
    a["rope_cos"], a["rope_sin"] = np.cos(angle), np.sin(angle)
    used += ["L3_ffn_wqkvT", "L3_ffn_woT", "L3_ffn_ln1", "rope_cos", "rope_sin"]
    used += ["x", "g_xattn", "g_ffn", "L3_xattn_gate", "ctxT", "maskT_ff1",
            "L0_xattn_Wk", "L0_xattn_Wv", "L0_xattn_Wo", "L0_xattn_WqT"]
    return {k: np.ascontiguousarray(a[k]) for k in used}


def kernel(**inputs):
    import concourse.bacc as bacc
    from concourse.bass_utils import run_bass_kernel_spmd

    nc = bacc.Bacc("TRN2", target_bir_lowering=False, num_devices=1)
    arrays = lay_out(inputs)
    dram = {k: nc.dram_tensor(f"in_{k}", a.shape, mybir.dt.from_np(a.dtype), kind="ExternalInput").ap()
            for k, a in arrays.items()}
    out = nc.dram_tensor("out_x", (B, S, D), F32, kind="ExternalOutput").ap()
    build(nc, dram, out)
    r = run_bass_kernel_spmd(nc, [{f"in_{k}": a for k, a in arrays.items()}], core_ids=[0])
    return r.results[0]["out_x"]
```

```python
from contextlib import ExitStack

import numpy as np

import concourse.bass as bass
from concourse import mybir

F32 = mybir.dt.float32
F32R = mybir.dt.float32r
BF16 = mybir.dt.bfloat16
I32 = mybir.dt.int32
U32 = mybir.dt.uint32
U8 = mybir.dt.uint8
ALU = mybir.AluOpType
ACT = mybir.ActivationFunctionType
AX_X = mybir.AxisListType.X

P = 128
B, S, D = 2, 1024, 256
TILES = B * S // P
TB = S // P
DC = D // P
NKEY = 77
NH = 16
HK = NH * NKEY
HKC = -(-HK // P)
HK_LAST = HK - (HKC - 1) * P
HPB = 512 // NKEY
GROUP = 512
NG = B * S // GROUP
TPG = GROUP // P
EPS = 1e-5
MASKED = -3.0e38
GATE_XATTN, GATE_FFN, GATE_L3 = 0, 4, 8

HEAD_BANKS = [(j, h0, min(HPB, NH - h0)) for j, h0 in enumerate(range(0, NH, HPB))]


class Steps:

    def __init__(self, eng, sem, base=0):
        self.eng, self.sem, self.base, self.n = eng, sem, base, 0

    def mark(self, ins):
        ins.then_inc(self.sem, 1)
        self.n += 1

    def link(self, ins, alone=None):
        self.mark(ins)
        self.eng.wait_ge(self.sem, self.base + self.n)
        if alone is not None:
            self.eng.sem_inc(alone, 1)


def flat(ap):
    return ap.rearrange("p a n -> p (a n)")


def tile_of(t3, t):
    return flat(t3[:, bass.ds(t, 1), :])


NORM_LINKS = {"layer": 2, "rms": 3}


class Norm:

    def __init__(self, nc, g, st, name=""):
        self.nc, self.minus_half = nc, g.minus_half
        self.small = st.sb(f"moments{name}", [P, 10])
        self.waits_alone = st.sem(f"waits_alone{name}")
        self.var_ready, self.rstd_ready = st.sem(f"var_ready{name}"), st.sem(f"rstd_ready{name}")

    def vector(self, dve, steps, n, src, dst, kind):
        nc, small = self.nc, self.small
        stats, agg, power, rstd = small[:, 0:6], small[:, 6:8], small[:, 8:9], small[:, 9:10]
        steps.link(nc.vector.bn_stats(stats, src), alone=self.waits_alone)
        steps.link(nc.vector.bn_aggr(agg, stats))
        if kind == "rms":
            steps.link(nc.vector.scalar_tensor_tensor(out=power, in0=agg[:, 0:1], scalar=agg[:, 0:1],
                                                      in1=agg[:, 1:2], op0=ALU.mult, op1=ALU.add))
        mean_square = power if kind == "rms" else agg[:, 1:2]
        nc.vector.tensor_scalar(power, mean_square, EPS, None, ALU.add).then_inc(self.var_ready, 1)
        dve.wait_ge(self.rstd_ready, n + 1)
        if kind == "rms":
            return nc.vector.tensor_scalar(dst, src, rstd, None, ALU.mult)
        return nc.vector.tensor_scalar(dst, src, agg[:, 0:1], rstd, ALU.subtract, ALU.mult)

    def gpsimd(self, pool, n):
        pool.wait_ge(self.var_ready, n + 1)
        self.nc.gpsimd.tensor_tensor(self.small[:, 9:10], self.small[:, 8:9], self.minus_half[:, 0:1], ALU.pow)\
            .then_inc(self.rstd_ready, 1)


class Stage:

    def __init__(self, nc, ctx, name):
        self.nc, self.ctx, self.name, self.sems = nc, ctx, name, []
        ctx.callback(self.clear)

    def clear(self):
        if self.sems:
            self.nc.clear_and_free_semaphores(self.sems)
            self.nc.all_engine_barrier()

    def sb(self, name, shape, dt=F32):
        return self.ctx.enter_context(self.nc.sbuf_tensor(f"{self.name}_{name}", shape, dt))

    def sem(self, name):
        self.sems.append(self.nc.alloc_semaphore(f"{self.name}_{name}"))
        return self.sems[-1]

    def block(self):
        return self.ctx.enter_context(self.nc.Block())


def load_stream(nc, g, dram):
    with ExitStack() as ctx:
        st = Stage(nc, ctx, "in")
        loaded, gates_loaded = st.sem("loaded"), st.sem("gates_loaded")
        zeroed, made, gates_done = st.sem("zeroed"), st.sem("made"), st.sem("gates_done")
        block = st.block()

        @block.sync
        def _(sp):
            sp.dma_start(g.x[:], dram["x"].rearrange("b (t p) d -> p (b t) d", p=P)).then_inc(loaded, 16)
            for src, at, n in (("g_xattn", GATE_XATTN, 4), ("g_ffn", GATE_FFN, 4), ("L3_xattn_gate", GATE_L3, 1)):
                sp.dma_start(g.gates[:, at:at + n], dram[src].partition_broadcast(P)).then_inc(gates_loaded, 16)
            sp.wait_ge(loaded, 16)

        @block.scalar
        def _(act):
            act.wait_ge(gates_loaded, 48)
            nc.scalar.activation(g.gates[:, 0:9], g.gates[:, 0:9], ACT.Tanh).then_inc(gates_done, 1)
            act.wait_ge(gates_done, 1)

        @block.gpsimd
        def _(pool):
            nc.gpsimd.memset(g.ident[:], 0.0).then_inc(zeroed, 1)
            nc.gpsimd.memset(g.identb[:], 0.0).then_inc(zeroed, 1)
            nc.gpsimd.memset(g.ones[:], 1.0).then_inc(made, 1)
            nc.gpsimd.memset(g.minus_half[:], -0.5).then_inc(made, 1)
            nc.gpsimd.memset(g.causal[:], 0.0).then_inc(zeroed, 1)
            pool.wait_ge(zeroed, 3)
            for m in (g.ident, g.identb):
                nc.gpsimd.affine_select(out=m[:], in_=m[:], compare_op=ALU.not_equal, fill=1.0, base=0,
                                        pattern=[[-1, P]], channel_multiplier=1).then_inc(made, 1)
            nc.gpsimd.affine_select(out=g.causal[:], in_=g.causal[:], compare_op=ALU.is_ge, fill=MASKED / 4, base=0,
                                    pattern=[[-1, P]], channel_multiplier=1).then_inc(made, 1)
            pool.wait_ge(made, 5)


def store_stream(nc, g, out):
    with ExitStack() as ctx:
        st = Stage(nc, ctx, "out")
        stored = st.sem("stored")
        block = st.block()

        @block.sync
        def _(sp):
            sp.dma_start(out.rearrange("b (t p) d -> p (b t) d", p=P), g.x[:]).then_inc(stored, 16)
            sp.wait_ge(stored, 16)


def linear_attention(nc, g, dram):
    with ExitStack() as ctx:
        st = Stage(nc, ctx, "la")
        ctxT = st.sb("ctxT", [P, DC, B * NKEY])
        wk, wv, wo, wqT = (st.sb(n, [P, DC, D]) for n in ("wk", "wv", "wo", "wqT"))
        mask = st.sb("mask", [P, B])
        pk, pv, sig = (st.sb(n, [P, B, D]) for n in ("pk", "pv", "sig"))
        kvT, kvo, mat = (st.sb(n, [P, B, DC, D]) for n in ("kvT", "kvo", "mat"))
        norm = Norm(nc, g, st)
        xn = st.sb("xn", [P, D])
        xT = st.sb("xT", [P, DC, P])
        loaded, steps_done = st.sem("loaded"), st.sem("steps_done")
        keys_ready, masked, sig_done, kv_in_ready = st.sem("keys_ready"), st.sem("masked"), st.sem("sig_done"), st.sem("kv_in_ready")
        prod_ready, prod_used = st.sem("prod_ready"), st.sem("prod_used")
        xn_ready, xT_psum_ready, xT_ready, y_ready, tile_done = (
            st.sem(n) for n in ("xn_ready", "xT_psum_ready", "xT_ready", "y_ready", "tile_done"))
        ps = g.ps
        block = st.block()

        @block.sync
        def _(sp):
            sp.dma_start(ctxT[:], dram["ctxT"].rearrange("(c p) k -> p c k", p=P)).then_inc(loaded, 16)
            for t, n in ((wk, "L0_xattn_Wk"), (wv, "L0_xattn_Wv"), (wo, "L0_xattn_Wo"), (wqT, "L0_xattn_WqT")):
                sp.dma_start(t[:], dram[n].rearrange("(c p) n -> p c n", p=P)).then_inc(loaded, 16)
            sp.dma_start(mask[0:NKEY, :], dram["maskT_ff1"]).then_inc(loaded, 16)

        @block.tensor
        def _(pe):
            pe.wait_ge(loaded, 96)
            for b in range(B):
                for w, bank in ((wk, 0), (wv, 1)):
                    for c in range(DC):
                        last = nc.tensor.matmul(ps[0:NKEY, 2 * b + bank, 0:D], ctxT[:, c, b * NKEY:(b + 1) * NKEY], w[:, c, :],
                                                start=(c == 0), stop=(c == DC - 1))
            last.then_inc(keys_ready, 1)
            pe.wait_ge(kv_in_ready, 2 * B)
            for b in range(B):
                for c in range(DC):
                    last = nc.tensor.matmul(ps[:, 4 + b, c * D:(c + 1) * D], pv[0:NKEY, b, c * P:(c + 1) * P],
                                            pk[0:NKEY, b, :], start=True, stop=True)
            last.then_inc(prod_ready, 1)
            for n, (lhs, rhs) in enumerate(((kvT, wo), (wqT, kvo))):
                pe.wait_ge(prod_used, n + 1)
                for b in range(B):
                    for m in range(DC):
                        for c in range(DC):
                            left = (lhs[:, b, c] if n == 0 else lhs[:, c])[:, m * P:(m + 1) * P]
                            right = rhs[:, c, :] if n == 0 else rhs[:, b, c, :]
                            last = nc.tensor.matmul(ps[:, 4 + b, m * D:(m + 1) * D], left, right,
                                                    start=(c == 0), stop=(c == DC - 1))
                last.then_inc(prod_ready, 1)
            pe.wait_ge(prod_used, 3)
            for b in range(B):
                with pe.Fori(0, TB) as t:
                    n = b * TB + t
                    pe.wait_ge(xn_ready, n + 1)
                    for c in range(DC):
                        last = nc.tensor.transpose(ps[:, 0, c * P:(c + 1) * P], xn[:, c * P:(c + 1) * P], g.ident[:])
                    last.then_inc(xT_psum_ready, 1)
                    pe.wait_ge(xT_ready, n + 1)
                    for c in range(DC):
                        last = nc.tensor.matmul(ps[:, 1, 0:D], xT[:, c, :], mat[:, b, c, :],
                                                start=(c == 0), stop=(c == DC - 1))
                    last.then_inc(y_ready, 1)

        @block.scalar
        def _(act):
            act.wait_ge(masked, 2 * B)
            nc.scalar.activation(sig[0:NKEY], pk[0:NKEY], ACT.Sigmoid).then_inc(sig_done, 1)

        @block.gpsimd
        def _(pool):
            with pool.Fori(0, TILES) as n:
                norm.gpsimd(pool, n)

        @block.vector
        def _(dve):
            dve.wait_ge(keys_ready, 1)
            for b in range(B):
                for dst, bank, done in ((pk, 0, masked), (pv, 1, masked)):
                    nc.vector.tensor_scalar(dst[0:NKEY, b, :], ps[0:NKEY, 2 * b + bank, 0:D], mask[0:NKEY, b:b + 1],
                                            None, ALU.mult).then_inc(done, 1)
            dve.wait_ge(sig_done, 1)
            for b in range(B):
                nc.vector.tensor_tensor(pk[0:NKEY, b, :], pk[0:NKEY, b, :], sig[0:NKEY, b, :], ALU.mult)\
                    .then_inc(kv_in_ready, 2)
            for n, dst in enumerate((kvT, kvo, mat)):
                dve.wait_ge(prod_ready, n + 1)
                for b in range(B):
                    src = ps[:, 4 + b, :].rearrange("p (c n) -> p c n", c=DC)
                    if n < 2:
                        last = nc.vector.tensor_copy(dst[:, b], src)
                    else:
                        last = nc.vector.tensor_scalar(dst[:, b], src, g.gates[:, GATE_XATTN:GATE_XATTN + 1], None, ALU.mult)
                last.then_inc(prod_used, 1)
            with dve.Fori(0, TILES) as n:
                s = Steps(dve, steps_done, n * NORM_LINKS["layer"])
                norm.vector(dve, s, n, tile_of(g.x, n), xn[:], "layer").then_inc(xn_ready, 1)
                dve.wait_ge(xT_psum_ready, n + 1)
                nc.vector.tensor_copy(xT[:], ps[:, 0, 0:D].rearrange("p (c n) -> p c n", c=DC)).then_inc(xT_ready, 1)
                dve.wait_ge(y_ready, n + 1)
                nc.vector.tensor_tensor(tile_of(g.x, n), tile_of(g.x, n), ps[:, 1, 0:D], ALU.add).then_inc(tile_done, 1)
                dve.wait_ge(tile_done, n + 1)


def split(nc, hi, lo, src):
    return nc.vector.tensor_copy(hi, src), lambda: nc.vector.tensor_tensor(lo, src, hi.bitcast(F32), ALU.subtract)


PASSES = ((0, 0), (1, 0), (0, 1))


def cross_attention(nc, g, dram, layer):
    full = layer == 3
    ps = g.ps
    with ExitStack() as ctx:
        st = Stage(nc, ctx, f"xa{layer}")
        scores_w = st.sb("scores_w", [P, 2, B, DC, HK], F32R)
        scores_b = st.sb("scores_b", [1, 2, B, 2 if full else HK], F32R)
        values_w = st.sb("values_w", [P, B, HKC, D])
        bo = st.sb("bo", [1, B, D])
        affine = st.sb("affine", [P, 2, DC])
        fold_context(nc, g, dram, layer, scores_w, scores_b, values_w, bo, affine)

        norm = Norm(nc, g, st)
        norm2 = Norm(nc, g, st, "2") if full else None
        xn, xT = st.sb("xn", [P, D]), st.sb("xT", [P, 2, DC, P], F32R)
        xT_whole = st.sb("xT_whole", [P, DC, P])
        probs = st.sb("probs", [P, NH, NKEY])
        probs_flat = probs[:].rearrange("p h k -> p (h k)")
        probsT = st.sb("probsT", [P, HKC, P])
        row_max, row_sum = st.sb("row_max", [P, NH]), st.sb("row_sum", [P, NH])
        ones = st.sb("ones", [1, P], F32R)
        steps_done, ones_ready = st.sem("steps_done"), st.sem("ones_ready")
        xn_ready, xT_psum_ready, xT_ready, scores_ready, centred, exp_done, probs_ready, pT_psum_ready, pT_ready, \
            y_ready, tile_done = (st.sem(n) for n in (
                "xn_ready", "xT_psum_ready", "xT_ready", "scores_ready", "centred", "exp_done", "probs_ready",
                "pT_psum_ready", "pT_ready", "y_ready", "tile_done"))
        SC, PT, XT, Y = 0, 3, 6, 7
        block = st.block()

        @block.tensor
        def _(pe):
            def turn_x(n):
                pe.wait_ge(xn_ready, n + 1)
                for c in range(DC):
                    last = nc.tensor.transpose(ps[:, XT, c * P:(c + 1) * P], xn[:, c * P:(c + 1) * P], g.ident[:])
                last.then_inc(xT_psum_ready, 1)

            def scores(n, b):
                for j, h0, heads in HEAD_BANKS:
                    cols = slice(h0 * NKEY, (h0 + heads) * NKEY)
                    out = ps[:, SC + j, 0:heads * NKEY]
                    for c in range(DC):
                        for left, right in PASSES:
                            last = nc.tensor.matmul(out, xT[:, left, c, :], scores_w[:, right, b, c, cols],
                                                    start=(c + left + right == 0),
                                                    stop=(full and (c, left, right) == (DC - 1, 0, 1)))
                    if not full:
                        for part in range(2):
                            last = nc.tensor.matmul(out, ones[0:1, :], scores_b[0:1, part, b, cols], start=False, stop=(part == 1))
                last.then_inc(scores_ready, 1)

            def step(n, b, b_next=None, turn=True, first=False):
                if b_next is not None:
                    pe.wait_ge(centred, n + 1)
                    pe.wait_ge(xT_ready, n + 2)
                    scores(n + 1, b_next)
                if turn:
                    turn_x(n + 2)
                pe.wait_ge(probs_ready, n + 1)
                for c in range(HKC):
                    w = P if c < HKC - 1 else HK_LAST
                    last = nc.tensor.transpose(ps[0:w, PT + c // 4, (c % 4) * P:(c % 4 + 1) * P],
                                               probs_flat[:, c * P:c * P + w], g.ident[:])
                last.then_inc(pT_psum_ready, 1)
                if not first:
                    pe.wait_ge(tile_done, n)
                pe.wait_ge(pT_ready, 4 * n + 4)
                for c in range(HKC):
                    w = P if c < HKC - 1 else HK_LAST
                    nc.tensor.matmul(ps[:, Y, 0:D], probsT[0:w, c, :], values_w[0:w, b, c, :], start=(c == 0), stop=False)
                nc.tensor.matmul(ps[:, Y, 0:D], g.ones[0:1, :], bo[0:1, b, :], start=False, stop=True).then_inc(y_ready, 1)

            turn_x(0)
            pe.wait_ge(ones_ready, 1)
            pe.wait_ge(xT_ready, 1)
            scores(0, 0)
            turn_x(1)
            step(0, 0, 0, first=True)
            with pe.Fori(1, TB - 1) as n:
                step(n, 0, 0)
            step(TB - 1, 0, 1)
            with pe.Fori(TB, TILES - 2) as n:
                step(n, 1, 1)
            step(TILES - 2, 1, 1, turn=False)
            step(TILES - 1, 1, turn=False)

        @block.gpsimd
        def _(pool):
            with pool.Fori(0, TILES) as t:
                norm.gpsimd(pool, t)
                if full:
                    norm2.gpsimd(pool, t)

        @block.scalar
        def _(act):
            with act.Fori(0, TILES) as t:
                act.wait_ge(centred, t + 1)
                nc.scalar.activation(probs_flat, probs_flat, ACT.Exp).then_inc(exp_done, 1)
                act.wait_ge(pT_psum_ready, t + 1)
                for k in range(2):
                    nc.scalar.activation(probsT[:, 4 * k:4 * k + 4, :].rearrange("p c n -> p (c n)"), ps[:, PT + k, :],
                                         ACT.Copy).then_inc(pT_ready, 1)
                nc.scalar.activation(probsT[:, 8, :], ps[:, PT + 2, 0:P], ACT.Copy).then_inc(pT_ready, 1)
                nc.scalar.activation(probsT[0:HK_LAST, 9, :], ps[0:HK_LAST, PT + 2, P:2 * P], ACT.Copy)\
                    .then_inc(pT_ready, 1)

        @block.vector
        def _(dve):
            per_norm = NORM_LINKS["layer"] * (2 if full else 1) + (1 if full else 0)
            per_turn = 2 if full else 1
            per = per_norm + per_turn + 3

            def normalised(n, s):
                x = tile_of(g.x, n)
                if full:
                    s.link(norm.vector(dve, s, n, x, xn[:], "layer"))
                    norm2.vector(dve, s, n, xn[:], xn[:], "layer").then_inc(xn_ready, 1)
                else:
                    norm.vector(dve, s, n, x, xn[:], "layer").then_inc(xn_ready, 1)

            def turned(n, s):
                dve.wait_ge(xT_psum_ready, n + 1)
                src = ps[:, XT, 0:D].rearrange("p (c n) -> p c n", c=DC)
                if full:
                    for c in range(DC):
                        last = nc.vector.tensor_scalar(xT_whole[:, c, :], src[:, c, :], affine[:, 0, c:c + 1],
                                                       affine[:, 1, c:c + 1], ALU.mult, ALU.add)
                    s.link(last)
                    src = xT_whole[:]
                high, low = split(nc, xT[:, 0], xT[:, 1], src)
                s.link(high)
                low().then_inc(xT_ready, 1)

            def add_up(n):
                x = tile_of(g.x, n)
                dve.wait_ge(y_ready, n + 1)
                nc.vector.tensor_tensor(x, x, ps[:, Y, 0:D], ALU.add).then_inc(tile_done, 1)

            def step(n, base, ahead=True, first=False):
                s = Steps(dve, steps_done, base)
                dve.wait_ge(scores_ready, n + 1)
                sc = [(j, slice(h0, h0 + k), k, ps[:, SC + j, 0:k * NKEY].rearrange("p (h k) -> p h k", h=k))
                      for j, h0, k in HEAD_BANKS]
                for j, heads, k, bank in sc:
                    last = nc.vector.tensor_reduce(row_max[:, heads], bank, AX_X, ALU.max)
                s.link(last)
                if not first:
                    dve.wait_ge(pT_psum_ready, n)
                for j, heads, k, bank in sc:
                    last = nc.vector.tensor_tensor(probs[:, heads, :], bank,
                                                   row_max[:, heads].unsqueeze(2).broadcast_to([P, k, NKEY]), ALU.subtract)
                last.then_inc(centred, 1)
                if not first:
                    add_up(n - 1)
                if ahead:
                    normalised(n + 2, s)
                dve.wait_ge(exp_done, n + 1)
                s.link(nc.vector.tensor_reduce(row_sum[:], probs[:], AX_X, ALU.add))
                s.link(nc.vector.reciprocal(row_sum[:], row_sum[:]))
                nc.vector.tensor_tensor(probs[:], probs[:], row_sum[:].unsqueeze(2).broadcast_to([P, NH, NKEY]), ALU.mult)\
                    .then_inc(probs_ready, 1)
                if ahead:
                    turned(n + 2, s)

            nc.vector.memset(xT_whole[0:1, 0, :], 1.0).then_inc(steps_done, 1)
            dve.wait_ge(steps_done, 1)
            nc.vector.tensor_copy(ones[:], xT_whole[0:1, 0, :]).then_inc(ones_ready, 1)
            dve.wait_ge(ones_ready, 1)
            start = 1 + 2 * (per_norm + per_turn)
            for n in range(2):
                s = Steps(dve, steps_done, 1 + n * (per_norm + per_turn))
                normalised(n, s)
                turned(n, s)
                assert s.n == per_norm + per_turn
            step(0, start, first=True)
            with dve.Fori(1, TILES - 2) as n:
                step(n, start + per * n)
            step(TILES - 2, start + per * (TILES - 2), ahead=False)
            step(TILES - 1, start + per * (TILES - 2) + 3, ahead=False)
            add_up(TILES - 1)
            dve.wait_ge(tile_done, TILES)


def fold_context(nc, g, dram, layer, scores_w, scores_b, values_w, bo, affine):
    dh = dram[f"L{layer}_xattn_WqT"].shape[0]
    inner = NH * dh
    scale = dh ** -0.5
    full = layer == 3
    BK = B * NKEY
    HPF = 512 // BK
    FILLS = [(h0, min(HPF, NH - h0)) for h0 in range(0, NH, HPF)]
    RING = 6
    VALUE_FILLS = B * NH // 2
    ps = g.ps
    scratch = nc.dram_tensor(f"values_w{layer}", (B, HK, D), F32).ap()
    with ExitStack() as ctx:
        st = Stage(nc, ctx, f"fc{layer}")
        ctxT = st.sb("ctxT", [P, DC, BK])
        wk, wv = st.sb("wk", [P, DC, inner]), st.sb("wv", [P, DC, inner])
        wqT, wo = st.sb("wqT", [dh, NH, D]), st.sb("wo", [dh, NH, D])
        bias = st.sb("bias", [dh, 3, NH])
        mask_in = st.sb("mask_in", [P, B, NKEY], I32 if layer == 2 else F32)
        mask = st.sb("mask", [P, B, NKEY])
        gate = st.sb("gate", [P, B, 2])
        bo_in = st.sb("bo_in", [1, D])
        row = st.sb("row", [1, B, 2 if full else HK])
        kT, vT = st.sb("kT", [dh, NH, BK]), st.sb("vT", [dh, NH, BK])
        vwo = st.sb("vwo", [NKEY, B, NH, D])
        small_loaded, k_loaded, v_loaded, q_loaded, o_loaded = (
            st.sem(n) for n in ("small_loaded", "k_loaded", "v_loaded", "q_loaded", "o_loaded"))
        stored, reloaded = st.sem("stored"), st.sem("reloaded")
        filled, emptied, steps_done, gate_done = st.sem("filled"), st.sem("emptied"), st.sem("steps_done"), st.sem("gate_done")
        smalls = 3 if full else 4
        block = st.block()

        @block.sync
        def _(sp):
            sp.dma_start(ctxT[:], dram["ctxT"].rearrange("(c p) k -> p c k", p=P)).then_inc(small_loaded, 16)
            sp.dma_start(wk[:], dram[f"L{layer}_xattn_Wk"].rearrange("(c p) n -> p c n", p=P)).then_inc(k_loaded, 16)
            sp.dma_start(bo_in[:], dram[f"L{layer}_xattn_bo"].rearrange("(a n) -> a n", a=1)).then_inc(small_loaded, 16)
            if full:
                sp.dma_start(affine[:], dram["L3_xattn_affine"]).then_inc(small_loaded, 16)
            else:
                sp.dma_start(bias[:], dram[f"L{layer}_xattn_bias"]).then_inc(small_loaded, 16)
                sp.dma_start(mask_in[:], dram[f"L{layer}_xattn_mask"].partition_broadcast(P)).then_inc(small_loaded, 16)
            sp.dma_start(wv[:], dram[f"L{layer}_xattn_Wv"].rearrange("(c p) n -> p c n", p=P)).then_inc(v_loaded, 16)
            sp.dma_start(wqT[:], dram[f"L{layer}_xattn_WqT"]).then_inc(q_loaded, 16)
            sp.dma_start(wo[:], dram[f"L{layer}_xattn_Wo"].rearrange("(h p) n -> p h n", p=dh)).then_inc(o_loaded, 16)
            before = len(FILLS) * (4 if full else 5)
            for b in range(B):
                sp.wait_ge(emptied, before + (b + 1) * NH // 2)
                sp.dma_start(scratch[b].rearrange("(h k) n -> k h n", h=NH), vwo[:, b]).then_inc(stored, 16)
                sp.wait_ge(stored, 16 * b + 16)
                sp.dma_start(values_w[:, b, 0:HKC - 1, :], scratch[b, 0:(HKC - 1) * P, :].rearrange("(c p) n -> p c n", p=P))\
                    .then_inc(reloaded, 16)
                sp.dma_start(values_w[0:HK_LAST, b, HKC - 1, :], scratch[b, (HKC - 1) * P:HK, :]).then_inc(reloaded, 16)
            sp.wait_ge(reloaded, 32 * B)

        @block.tensor
        def _(pe):
            count = 0

            def bank():
                nonlocal count
                if count >= RING:
                    pe.wait_ge(emptied, count - RING + 1)
                count += 1
                return ps[:, (count - 1) % RING, :]

            pe.wait_ge(small_loaded, 16 * smalls)
            for w, loaded in ((wk, k_loaded), (wv, v_loaded)):
                pe.wait_ge(loaded, 16)
                for h0, heads in FILLS:
                    out = bank()
                    for h in range(heads):
                        for c in range(DC):
                            last = nc.tensor.matmul(out[0:dh, h * BK:(h + 1) * BK], w[:, c, (h0 + h) * dh:(h0 + h + 1) * dh],
                                                    ctxT[:, c, :], start=(c == 0), stop=(c == DC - 1))
                    last.then_inc(filled, 1)
            pe.wait_ge(q_loaded, 16)
            pe.wait_ge(emptied, len(FILLS))
            for m in range(DC if full else DC + 1):
                for h0, heads in FILLS:
                    out = bank()
                    for h in range(heads):
                        left = wqT[:, h0 + h, m * P:(m + 1) * P] if m < DC else bias[:, 0, h0 + h:h0 + h + 1]
                        last = nc.tensor.matmul(out[0:left.shape[1], h * BK:(h + 1) * BK], left, kT[:, h0 + h, :],
                                                start=True, stop=True)
                    last.then_inc(filled, 1)
            pe.wait_ge(o_loaded, 16)
            pe.wait_ge(emptied, 2 * len(FILLS))
            for b in range(B):
                for h0 in range(0, NH, 2):
                    out = bank()
                    for h in range(2):
                        last = nc.tensor.matmul(out[0:NKEY, h * D:(h + 1) * D], vT[:, h0 + h, b * NKEY:(b + 1) * NKEY],
                                                wo[:, h0 + h, :], start=True, stop=True)
                    last.then_inc(filled, 1)

        @block.vector
        def _(dve):
            count = 0

            def bank(rows, cols):
                nonlocal count
                dve.wait_ge(filled, count + 1)
                count += 1
                return ps[0:rows, (count - 1) % RING, 0:cols]

            s = Steps(dve, steps_done)
            dve.wait_ge(small_loaded, 16 * smalls)
            at = GATE_XATTN + layer
            own_gate = g.gates[:, at:at + 1]
            for b in range(B):
                if full:
                    s.link(nc.vector.tensor_tensor(gate[:, b, 0:1], own_gate, g.gates[:, GATE_L3:GATE_L3 + 1], ALU.mult))
                elif layer == 1:
                    s.link(nc.vector.tensor_copy(gate[:, b, 0:1], own_gate))
                    s.link(nc.vector.tensor_scalar(mask[:, b, :], mask_in[:, b, :], -1e9, None, ALU.mult))
                else:
                    s.link(nc.vector.tensor_scalar(mask[:, b, :], mask_in[:, b, :], 0.0, None, ALU.not_equal))
                    s.link(nc.vector.tensor_reduce(gate[:, b, 1:2], mask[:, b, :], AX_X, ALU.max))
                    s.link(nc.vector.reciprocal(gate[:, b, 1:2], gate[:, b, 1:2]))
                    s.link(nc.vector.scalar_tensor_tensor(out=gate[:, b, 0:1], in0=gate[:, b, 1:2], scalar=0.0,
                                                          in1=own_gate, op0=ALU.mult, op1=ALU.add))
                    s.link(nc.vector.tensor_scalar(mask[:, b, :], mask_in[:, b, :], 0.0, MASKED, ALU.is_equal, ALU.mult))
                s.link(nc.vector.tensor_scalar(bo[0:1, b, :], bo_in[:], gate[0:1, b, 0:1], None, ALU.mult))
            for dst, which in ((kT, 1), (vT, 2)):
                for h0, heads in FILLS:
                    src = bank(dh, heads * BK).rearrange("p (h k) -> p h k", h=heads)
                    if full:
                        last = nc.vector.tensor_copy(dst[:, h0:h0 + heads, :], src)
                    else:
                        last = nc.vector.tensor_tensor(dst[:, h0:h0 + heads, :], src, bias[:, which, h0:h0 + heads].unsqueeze(2)
                                                       .broadcast_to([dh, heads, BK]), ALU.add)
                    last.then_inc(emptied, 1)
            for m in range(DC):
                for h0, heads in FILLS:
                    src = bank(P, heads * BK).rearrange("p (h b k) -> p b h k", h=heads, b=B)
                    cols = slice(h0 * NKEY, (h0 + heads) * NKEY)
                    high, low = ([scores_w[:, part, b, m, cols].rearrange("p (h k) -> p h k", h=heads) for b in range(B)]
                                 for part in range(2))
                    for b in range(B):
                        last = nc.vector.tensor_scalar(high[b], src[:, b], scale, None, ALU.mult)
                    s.link(last)
                    for b in range(B):
                        last = nc.vector.scalar_tensor_tensor(out=low[b], in0=src[:, b], scalar=scale, in1=high[b].bitcast(F32),
                                                              op0=ALU.mult, op1=ALU.subtract)
                    last.then_inc(emptied, 1)
            if not full:
                for h0, heads in FILLS:
                    src = bank(1, heads * BK).rearrange("p (h b k) -> p b h k", h=heads, b=B)
                    for b in range(B):
                        last = nc.vector.scalar_tensor_tensor(
                            out=row[0:1, b, h0 * NKEY:(h0 + heads) * NKEY].rearrange("p (h k) -> p h k", h=heads),
                            in0=src[:, b], scalar=scale, in1=mask[0:1, b, :].unsqueeze(1).broadcast_to([1, heads, NKEY]),
                            op0=ALU.mult, op1=ALU.add)
                    last.then_inc(emptied, 1)
            for b in range(B):
                for h0 in range(0, NH, 2):
                    nc.vector.tensor_scalar(vwo[:, b, h0:h0 + 2, :], bank(NKEY, 2 * D).rearrange("p (h n) -> p h n", h=2),
                                            gate[0:NKEY, b, 0:1], None, ALU.mult).then_inc(emptied, 1)
            if not full:
                dve.wait_ge(emptied, 5 * len(FILLS))
                high, low = split(nc, scores_b[0:1, 0], scores_b[0:1, 1], row[:])
                s.link(high)
                s.link(low())


def sign_network(nc, g, dram):
    F = dram["L0_ffn_k1"].shape[0]
    FC = F // P
    ps = g.ps
    with ExitStack() as ctx:
        st = Stage(nc, ctx, "sn")
        w0, w1, w2 = (st.sb(n, shape, F32R) for n, shape in (("w0", [P, DC, F]), ("w1", [P, FC, F]), ("w2", [P, FC, D])))
        scales = st.sb("scales", [P, 4])
        prep_sign_weights(nc, g, dram, w0, w1, w2, scales)
        norm = Norm(nc, g, st)
        xn, xT = st.sb("xn", [P, D]), st.sb("xT", [P, 2, DC, GROUP], F32R)
        h1, h2 = st.sb("h1", [P, 2, FC, GROUP], F32R), st.sb("h2", [P, 2, FC, GROUP], F32R)
        whole = st.sb("whole", [P, 2, GROUP])
        whole_ready, high_ready, high_x = st.sem("whole_ready"), st.sem("high_ready"), st.sem("high_x")
        steps_done = st.sem("steps_done")
        xn_ready, xT_psum_ready, xT_ready, h_psum_ready, h_ready, y_ready, y_used = (st.sem(n) for n in (
            "xn_ready", "xT_psum_ready", "xT_ready", "h_psum_ready", "h_ready", "y_ready", "y_used"))
        H_BANKS, XT, Y = 4, 4, 6
        block = st.block()

        @block.tensor
        def _(pe):
            with pe.Fori(0, NG) as gr:
                for j in range(TPG):
                    pe.wait_ge(xn_ready, gr * TPG + j + 1)
                    if j > 0:
                        pe.wait_ge(xT_ready, gr * TPG + j)
                    for c in range(DC):
                        last = nc.tensor.transpose(ps[:, XT, c * P:(c + 1) * P], xn[:, c * P:(c + 1) * P], g.ident[:])
                    last.then_inc(xT_psum_ready, 1)
                pe.wait_ge(xT_ready, gr * TPG + TPG)
                for m in range(2 * FC):
                    if m >= H_BANKS:
                        pe.wait_ge(h_ready, gr * (2 * FC) + m - H_BANKS + 1)
                    if m == FC:
                        pe.wait_ge(h_ready, gr * (2 * FC) + FC)
                    w, src, n = (w0, xT, DC) if m < FC else (w1, h1, FC)
                    for c in range(n):
                        for part in range(2):
                            last = nc.tensor.matmul(ps[:, m % H_BANKS, :], w[:, c, (m % FC) * P:(m % FC + 1) * P],
                                                    src[:, part, c, :], start=(c + part == 0), stop=(c + part == n))
                    last.then_inc(h_psum_ready, 1)
                pe.wait_ge(h_ready, gr * (2 * FC) + 2 * FC)
                for j in range(TPG):
                    if j >= 2:
                        pe.wait_ge(y_used, gr * TPG + j - 1)
                    for c in range(FC):
                        for part in range(2):
                            last = nc.tensor.matmul(ps[:, Y + j % 2, 0:D], h2[:, part, c, j * P:(j + 1) * P], w2[:, c, :],
                                                    start=(c + part == 0), stop=(c + part == FC))
                    last.then_inc(y_ready, 1)

        @block.gpsimd
        def _(pool):
            with pool.Fori(0, TILES) as n:
                norm.gpsimd(pool, n)

        @block.scalar
        def _(act):
            with act.Fori(0, NG) as gr:
                for m in range(2 * FC):
                    dst = h1 if m < FC else h2
                    act.wait_ge(whole_ready, gr * (2 * FC) + m + 1)
                    nc.scalar.activation(dst[:, 0, m % FC, :], whole[:, m % 2, :], ACT.Copy).then_inc(high_ready, 1)

        @block.vector
        def _(dve):
            per = NORM_LINKS["layer"]
            with dve.Fori(0, NG) as gr:
                for j in range(TPG):
                    n = gr * TPG + j
                    s = Steps(dve, steps_done, n * per)
                    norm.vector(dve, s, n, tile_of(g.x, n), xn[:], "layer").then_inc(xn_ready, 1)
                    dve.wait_ge(xT_psum_ready, n + 1)
                    src = ps[:, XT, 0:D].rearrange("p (c n) -> p c n", c=DC)
                    nc.vector.tensor_copy(xT[:, 0, :, j * P:(j + 1) * P], src).then_inc(high_x, 1)
                    dve.wait_ge(high_x, n + 1)
                    nc.vector.tensor_tensor(xT[:, 1, :, j * P:(j + 1) * P], src, xT[:, 0, :, j * P:(j + 1) * P].bitcast(F32),
                                            ALU.subtract).then_inc(xT_ready, 1)
                for m in range(2 * FC):
                    k = gr * (2 * FC) + m
                    dve.wait_ge(h_psum_ready, k + 1)
                    dst, scale = (h1, scales[:, 0:1]) if m < FC else (h2, scales[:, 1:2])
                    nc.vector.tensor_scalar(whole[:, m % 2, :], ps[:, m % H_BANKS, :], scale, 0.0, ALU.mult, ALU.max)\
                        .then_inc(whole_ready, 1)
                    dve.wait_ge(high_ready, k + 1)
                    nc.vector.tensor_tensor(dst[:, 1, m % FC, :], whole[:, m % 2, :], dst[:, 0, m % FC, :].bitcast(F32),
                                            ALU.subtract).then_inc(h_ready, 1)
                for j in range(TPG):
                    n = gr * TPG + j
                    dve.wait_ge(y_ready, n + 1)
                    nc.vector.scalar_tensor_tensor(out=tile_of(g.x, n), in0=ps[:, Y + j % 2, 0:D], scalar=scales[:, 2:3],
                                                   in1=tile_of(g.x, n), op0=ALU.mult, op1=ALU.add).then_inc(y_used, 1)
                    dve.wait_ge(y_used, n + 1)


def prep_sign_weights(nc, g, dram, w0, w1, w2, scales):
    F = dram["L0_ffn_k1"].shape[0]
    FC = F // P
    with ExitStack() as ctx:
        st = Stage(nc, ctx, "sp")
        b0, b1, b2 = st.sb("b0", [P, 2 * DC, F], U8), st.sb("b1", [P, FC, F], U8), st.sb("b2", [P, FC, D], U8)
        loaded, made = st.sem("loaded"), st.sem("made")
        diff_ready = st.sem("diff_ready")
        block = st.block()

        @block.sync
        def _(sp):
            for n, (t, name) in enumerate(((b0, "L0_ffn_k0"), (b2, "L0_ffn_k2"), (b1, "L0_ffn_k1"))):
                sp.dma_start(t[:], dram[name].rearrange("(c p) n -> p c n", p=P)).then_inc(loaded, 16)
            for n in range(3):
                sp.dma_start(scales[:, n:n + 1], dram[f"L0_ffn_s{n}"].partition_broadcast(P)).then_inc(loaded, 16)

        @block.vector
        def _(dve):
            dve.wait_ge(loaded, 96)
            nc.vector.tensor_tensor(w0[:], b0[:, 0:DC, :], b0[:, DC:2 * DC, :], ALU.subtract).then_inc(diff_ready, 1)
            nc.vector.tensor_scalar(w2[:], b2[:], 4.0, -2.0, ALU.mult, ALU.add)
            nc.vector.tensor_scalar(w1[:], b1[:], 8.0, -4.0, ALU.mult, ALU.add)
            nc.vector.tensor_tensor(scales[:, 2:3], scales[:, 2:3], g.gates[:, GATE_FFN:GATE_FFN + 1], ALU.mult)\
                .then_inc(made, 1)


def mixture(nc, g, dram, layer, src, acc):
    E = 8
    K3 = 3 * E
    weights = dram[f"L{layer}_moe_w"]
    selector = dram[f"L{layer}_moe_sel"]
    chunks = weights.shape[0]
    inner_norm = layer == 3
    ps = g.ps
    with ExitStack() as outer:
        combT = Stage(nc, outer, f"mx{layer}").sb("combT", [K3, B * S], BF16)
        xT_all = Stage(nc, outer, f"mx{layer}").sb("xT_all", [P, 2, DC, B * S], F32R)
        with ExitStack() as ctx:
            st = Stage(nc, ctx, f"rt{layer}")
            norm = Norm(nc, g, st)
            xn, xT = st.sb("xn", [P, D]), st.sb("xT", [P, DC, P])
            router, gain = st.sb("router", [P, DC, E]), st.sb("gain", [P, DC])
            bias, iota = st.sb("bias", [P, E]), st.sb("iota", [P, E])
            logits, top, expd, w2, where = (st.sb(n, [P, E]) for n in ("logits", "top", "expd", "w2", "where"))
            index, total = st.sb("index", [P, E], U32), st.sb("total", [P, 4])
            comb, other, rest = (st.sb(n, [P, E]) for n in ("comb", "other", "rest"))
            parts = st.sb("parts", [P, K3], BF16)
            loaded, steps_done, alone, high_kept = (st.sem(n) for n in ("loaded", "steps_done", "alone", "high_kept"))
            xn_ready, xT_psum_ready, xT_ready, xT_kept, logits_ready, shifted, exp_done, parts_ready, \
                combT_psum_ready, combT_ready, cleared = (st.sem(n) for n in (
                    "xn_ready", "xT_psum_ready", "xT_ready", "xT_kept", "logits_ready", "shifted", "exp_done",
                    "parts_ready", "combT_psum_ready", "combT_ready", "cleared"))
            XT, LG, CT = 0, 1, 2
            combT_psum = ps[0:K3, CT, 0:P // 2].bitcast(BF16)
            loads = 4 if layer == 1 else 3
            block = st.block()

            @block.sync
            def _(sp):
                sp.dma_start(router[:], dram[f"L{layer}_moe_router"].rearrange("(c p) e -> p c e", p=P)).then_inc(loaded, 16)
                sp.dma_start(iota[:], dram["iota8"].partition_broadcast(P)).then_inc(loaded, 16)
                if layer == 1:
                    sp.dma_start(bias[:], dram["L1_ffn_bs"].partition_broadcast(P)).then_inc(loaded, 16)
                sp.dma_start(gain[:], dram["L3_ffn_ln2"]).then_inc(loaded, 16)

            @block.tensor
            def _(pe):
                pe.wait_ge(loaded, 16 * loads)
                with pe.Fori(0, TILES) as t:
                    pe.wait_ge(xn_ready, t + 1)
                    for c in range(DC):
                        last = nc.tensor.transpose(ps[:, XT, c * P:(c + 1) * P], xn[:, c * P:(c + 1) * P], g.ident[:])
                    last.then_inc(xT_psum_ready, 1)
                    pe.wait_ge(xT_ready, t + 1)
                    for c in range(DC):
                        last = nc.tensor.matmul(ps[:, LG, 0:E], xT[:, c, :], router[:, c, :], start=(c == 0), stop=(c == DC - 1))
                    last.then_inc(logits_ready, 1)
                    pe.wait_ge(parts_ready, t + 1)
                    nc.tensor.transpose(combT_psum, parts[:], g.identb[:]).then_inc(combT_psum_ready, 1)

            @block.gpsimd
            def _(pool):
                if not inner_norm:
                    nc.gpsimd.memset(acc[:], 0.0).then_inc(cleared, 1)
                with pool.Fori(0, TILES) as t:
                    norm.gpsimd(pool, t)
                    pool.wait_ge(xT_ready, t + 1)
                    high, low = (xT_all[:, part, :, bass.ds(t * P, P)] for part in range(2))
                    nc.gpsimd.tensor_copy(high, xT[:]).then_inc(high_kept, 1)
                    pool.wait_ge(high_kept, t + 1)
                    nc.gpsimd.tensor_tensor(low, xT[:], high.bitcast(F32), ALU.subtract).then_inc(xT_kept, 1)

            @block.scalar
            def _(act):
                with act.Fori(0, TILES) as t:
                    act.wait_ge(shifted, t + 1)
                    n = 2 if layer == 1 else E
                    nc.scalar.activation(expd[:, 0:n], w2[:, 0:n], ACT.Exp, accum_out=total[:, 0:1]).then_inc(exp_done, 1)

            @block.vector
            def _(dve):
                per = NORM_LINKS["rms" if inner_norm else "layer"] + (16 if inner_norm else 12)
                dve.wait_ge(loaded, 16 * loads)
                with dve.Fori(0, TILES) as t:
                    s = Steps(dve, steps_done, t * per)
                    kind = "rms" if inner_norm else "layer"
                    norm.vector(dve, s, t, tile_of(src, t), xn[:], kind).then_inc(xn_ready, 1)
                    dve.wait_ge(xT_psum_ready, t + 1)
                    for c in range(DC):
                        bank = ps[:, XT, c * P:(c + 1) * P]
                        if inner_norm:
                            last = nc.vector.tensor_scalar(xT[:, c, :], bank, gain[:, c:c + 1], None, ALU.mult)
                        else:
                            last = nc.vector.tensor_copy(xT[:, c, :], bank)
                    last.then_inc(xT_ready, 1)
                    dve.wait_ge(logits_ready, t + 1)
                    if layer == 1:
                        s.link(nc.vector.tensor_tensor(logits[:], ps[:, LG, 0:E], bias[:], ALU.add), alone)
                        s.link(nc.vector.max(top[:], logits[:]), alone)
                        s.link(nc.vector.max_index(index[:], top[:], logits[:]))
                        nc.vector.tensor_scalar(w2[:, 0:2], top[:, 0:2], top[:, 0:1], None, ALU.subtract).then_inc(shifted, 1)
                        dve.wait_ge(exp_done, t + 1)
                        s.link(nc.vector.reciprocal(total[:, 1:2], total[:, 0:1]))
                        s.link(nc.vector.tensor_scalar(w2[:, 0:2], expd[:, 0:2], total[:, 1:2], None, ALU.mult))
                    else:
                        s.link(nc.vector.tensor_copy(logits[:], ps[:, LG, 0:E]))
                        s.link(nc.vector.tensor_reduce(total[:, 2:3], logits[:], AX_X, ALU.max))
                        nc.vector.tensor_scalar(w2[:], logits[:], total[:, 2:3], None, ALU.subtract).then_inc(shifted, 1)
                        dve.wait_ge(exp_done, t + 1)
                        s.link(nc.vector.reciprocal(total[:, 1:2], total[:, 0:1]))
                        s.link(nc.vector.tensor_scalar(logits[:], expd[:], total[:, 1:2], None, ALU.mult), alone)
                        s.link(nc.vector.max(top[:], logits[:]), alone)
                        s.link(nc.vector.max_index(index[:], top[:], logits[:]))
                        s.link(nc.vector.tensor_tensor(total[:, 3:4], top[:, 0:1], top[:, 1:2], ALU.add))
                        s.link(nc.vector.reciprocal(total[:, 3:4], total[:, 3:4]))
                        s.link(nc.vector.tensor_scalar(w2[:, 0:2], top[:, 0:2], total[:, 3:4], None, ALU.mult))
                    s.link(nc.vector.tensor_copy(where[:, 0:2], index[:, 0:2]))
                    s.link(nc.vector.tensor_scalar(comb[:], iota[:], where[:, 0:1], w2[:, 0:1], ALU.is_equal, ALU.mult))
                    s.link(nc.vector.tensor_scalar(other[:], iota[:], where[:, 1:2], w2[:, 1:2], ALU.is_equal, ALU.mult))
                    s.link(nc.vector.tensor_tensor(comb[:], comb[:], other[:], ALU.add))
                    s.link(nc.vector.tensor_copy(parts[:, 0:E], comb[:]))
                    s.link(nc.vector.tensor_tensor(rest[:], comb[:], parts[:, 0:E], ALU.subtract))
                    s.link(nc.vector.tensor_copy(parts[:, E:2 * E], rest[:]))
                    nc.vector.tensor_tensor(parts[:, 2 * E:K3], rest[:], parts[:, E:2 * E], ALU.subtract).then_inc(parts_ready, 1)
                    dve.wait_ge(combT_psum_ready, t + 1)
                    nc.vector.tensor_copy(combT[:, bass.ds(t * P, P)], combT_psum).then_inc(combT_ready, 1)
                    dve.wait_ge(xT_kept, t + 1)
                    assert s.n == per, s.n

        with ExitStack() as ctx:
            st = Stage(nc, ctx, f"ex{layer}")
            slots = st.sb("slots", [P, 2, 3 * D])
            parts = st.sb("parts", [P, 2, 2, 3 * D], F32R)
            sels = st.sb("sels", [K3, 2, P], BF16)
            act_out, h = st.sb("act_out", [P, 2, GROUP]), st.sb("h", [P, 2, GROUP])
            h_parts = st.sb("h_parts", [P, 2, 2, GROUP], F32R)
            high_split, weights_split, whole_ready, h_high_ready, waits_alone = (
                st.sem(n) for n in ("high_split", "weights_split", "whole_ready", "h_high_ready", "waits_alone"))
            slot_loaded = [st.sem(f"slot_loaded{n}") for n in range(2)]
            chunk_used, gate_up_ready, silu_done, gated, h_ready, y_ready, y_used = (st.sem(n) for n in (
                "chunk_used", "gate_up_ready", "silu_done", "gated", "h_ready", "y_ready", "y_used"))
            GATE, UP, SPREAD, Y = 0, 2, 4, 6
            tail = 1 if chunks % 2 else 2
            pairs = (chunks - tail) // 2
            block = st.block()

            def load(sp, c, slot):
                sp.dma_start(slots[:, slot, :], weights[bass.ds(c, 1)].rearrange("a p n -> p (a n)"))\
                    .then_inc(slot_loaded[slot], 16)
                sp.dma_start(sels[:, slot, :], selector[:, bass.ds(c * P, P)]).then_inc(slot_loaded[slot], 16)

            @block.sync
            def _(sp):
                for slot in range(2):
                    load(sp, slot, slot)
                with sp.Fori(1, pairs) as p:
                    for slot in range(2):
                        sp.wait_ge(chunk_used, 2 * p + slot - 1)
                        load(sp, 2 * p + slot, slot)
                for c in range(2 * pairs, chunks):
                    sp.wait_ge(chunk_used, c - 1)
                    load(sp, c, c % 2)

            @block.tensor
            def _(pe):
                def gate_up(c, slot, gr):
                    i = gr % 2
                    if gr == 0:
                        pe.wait_ge(slot_loaded[slot], 32 * (c // 2) + 32)
                        pe.wait_ge(weights_split, c + 1)
                    tokens = slice(gr * GROUP, (gr + 1) * GROUP)
                    for bank, w in ((GATE + i, 0), (UP + i, 1)):
                        for k in range(DC):
                            for left, right in PASSES:
                                nc.tensor.matmul(ps[:, bank, :], parts[:, slot, left, (DC * w + k) * P:(DC * w + k + 1) * P],
                                                 xT_all[:, right, k, tokens], start=(k + left + right == 0),
                                                 stop=((k, left, right) == (DC - 1, 0, 1)))
                    nc.tensor.matmul(ps[:, SPREAD + i, :], sels[:, slot, :], combT[:, tokens], start=True, stop=True)\
                        .then_inc(gate_up_ready, 1)

                def down(c, slot, gr, first=False):
                    unit = 4 * c + gr
                    pe.wait_ge(h_ready, unit + 1)
                    if not first:
                        pe.wait_ge(y_used, unit)
                    for j in range(TPG):
                        for left, right in PASSES:
                            last = nc.tensor.matmul(ps[:, Y + j // 2, (j % 2) * D:(j % 2 + 1) * D],
                                                    h_parts[:, gr % 2, left, j * P:(j + 1) * P],
                                                    parts[:, slot, right, 2 * DC * P:],
                                                    start=(left + right == 0), stop=(right == 1))
                    last.then_inc(y_ready, 1)

                def chunk(c, slot, more, first=False):
                    for gr in range(NG):
                        if gr < NG - 1:
                            gate_up(c, slot, gr + 1)
                        elif more:
                            gate_up(c + 1, 1 - slot, 0)
                        down(c, slot, gr, first and gr == 0)

                gate_up(0, 0, 0)
                chunk(0, 0, True, first=True)
                chunk(1, 1, True)
                with pe.Fori(1, pairs) as p:
                    chunk(2 * p, 0, True)
                    chunk(2 * p + 1, 1, True)
                for c in range(2 * pairs, chunks):
                    chunk(c, c % 2, c < chunks - 1)

            def over_chunks(eng, chunk):
                chunk(0, None)
                with eng.Fori(0, (chunks - 2) // 2) as p:
                    chunk(2 * p + 1, 0)
                    chunk(2 * p + 2, 1)
                for c in range(2 * ((chunks - 2) // 2) + 1, chunks):
                    chunk(c, (c + 1) % 2 if c + 1 < chunks else None)

            @block.gpsimd
            def _(pool):
                def low_weights(c, slot):
                    pool.wait_ge(high_split, c + 1)
                    nc.gpsimd.tensor_tensor(parts[:, slot, 1, :], slots[:, slot, :], parts[:, slot, 0, :].bitcast(F32),
                                            ALU.subtract).then_inc(weights_split, 1)

                def chunk(c, ahead):
                    for gr in range(NG):
                        pool.wait_ge(h_high_ready, NG * c + gr + 1)
                        nc.gpsimd.tensor_tensor(h_parts[:, gr % 2, 1, :], h[:, gr % 2, :], h_parts[:, gr % 2, 0, :].bitcast(F32),
                                                ALU.subtract).then_inc(h_ready, 1)
                        if gr == 1 and ahead is not None:
                            low_weights(c + 1, ahead)

                for slot in range(2):
                    low_weights(slot, slot)
                over_chunks(pool, chunk)

            @block.scalar
            def _(act):
                def high_weights(c, slot, reused):
                    act.wait_ge(slot_loaded[slot], 32 * (c // 2) + 32)
                    if reused:
                        act.wait_ge(chunk_used, c - 1)
                    nc.scalar.activation(parts[:, slot, 0, :], slots[:, slot, :], ACT.Copy).then_inc(high_split, 1)

                def chunk(c, ahead):
                    for gr in range(NG):
                        act.wait_ge(gate_up_ready, NG * c + gr + 1)
                        nc.scalar.activation(act_out[:, gr % 2, :], ps[:, GATE + gr % 2, :], ACT.Silu).then_inc(silu_done, 1)
                        if gr == 1 and ahead is not None:
                            high_weights(c + 1, ahead, True)

                for slot in range(2):
                    high_weights(slot, slot, False)
                over_chunks(act, chunk)

            @block.vector
            def _(dve):
                def hidden(u, i):
                    dve.wait_ge(silu_done, u + 1)
                    nc.vector.tensor_tensor(act_out[:, i, :], act_out[:, i, :], ps[:, UP + i, :], ALU.mult).then_inc(gated, 1)
                    dve.wait_ge(gated, u + 1)
                    nc.vector.tensor_tensor(h[:, i, :], act_out[:, i, :], ps[:, SPREAD + i, :], ALU.mult).then_inc(whole_ready, 1)
                    dve.wait_ge(whole_ready, u + 1)
                    nc.vector.tensor_copy(h_parts[:, i, 0, :], h[:, i, :]).then_inc(h_high_ready, 1)

                def add_up(u, gr):
                    dve.wait_ge(y_ready, u + 1)
                    part = acc[:, gr * TPG:(gr + 1) * TPG, :].rearrange("p t n -> p (t n)")
                    nc.vector.tensor_tensor(part, part, ps[:, Y:Y + 2, :].rearrange("p b n -> p (b n)"), ALU.add)\
                        .then_inc(y_used, 1)
                    if gr == NG - 1:
                        dve.sem_inc(chunk_used, 1)

                hidden(0, 0)
                with dve.Fori(0, chunks - 1) as c:
                    for gr in range(NG):
                        hidden(NG * c + gr + 1, (gr + 1) % 2)
                        add_up(NG * c + gr, gr)
                last = NG * (chunks - 1)
                for gr in range(NG):
                    if gr < NG - 1:
                        hidden(last + gr + 1, (gr + 1) % 2)
                    add_up(last + gr, gr)
                dve.wait_ge(y_used, chunks * NG)


def expert_layer_1(nc, g, dram):
    with ExitStack() as ctx:
        st = Stage(nc, ctx, "m1")
        acc = st.sb("acc", [P, TILES, D])
        mixture(nc, g, dram, 1, g.x, acc)
        add_gated(nc, g, acc, 1)


def add_gated(nc, g, acc, layer):
    with ExitStack() as ctx:
        st = Stage(nc, ctx, f"ag{layer}")
        added = st.sem("added")
        block = st.block()

        @block.vector
        def _(dve):
            at = GATE_FFN + layer
            nc.vector.scalar_tensor_tensor(out=g.x[:], in0=acc[:], scalar=g.gates[:, at:at + 1], in1=g.x[:],
                                           op0=ALU.mult, op1=ALU.add).then_inc(added, 1)
            dve.wait_ge(added, 1)


def product_key_experts(nc, g, dram):
    HEADS, KEYS, TOP = 8, 64, 16
    EXPERTS = KEYS * KEYS
    EC = EXPERTS // P
    SIDES = 2 * HEADS
    BLK = 1024
    BLOCKS = EXPERTS // BLK
    UNITS = [(head, q) for head in range(HEADS) for q in range(BLOCKS)]
    NU = len(UNITS)
    OWN = BLOCKS - 1
    POOL_ADDS = (HEADS - 1) * (BLOCKS - 1)
    KEPT = 3
    HB = EXPERTS // 512
    HIDDEN = {2 * k + 1: k for k in range(HB)}
    AHEAD_X, AHEAD_TURN, AHEAD_SIM = 12, 18, 22
    ps = g.ps
    with ExitStack() as ctx:
        st = Stage(nc, ctx, "pk")
        sim_w = st.sb("sim_w", [P, DC, SIDES * KEYS])
        spread = st.sb("spread", [P, EXPERTS], F32R)
        fold_product_keys(nc, g, dram, sim_w, spread)
        downT, up = st.sb("downT", [P, DC, EXPERTS]), st.sb("up", [P, EC, D])
        gain = st.sb("gain", [P, DC])
        norm, norm2 = Norm(nc, g, st), Norm(nc, g, st, "2")
        xn, xT = st.sb("xn", [P, D]), st.sb("xT", [P, DC, P])
        sims, rest = st.sb("sims", [P, SIDES, KEYS]), st.sb("rest", [P, SIDES, KEYS])
        simsT = st.sb("simsT", [P, 2, HEADS, P], F32R)
        best = st.sb("best", [P, SIDES, TOP])
        pairs = st.sb("pairs", [P, HEADS, TOP * TOP])
        top = st.sb("top", [P, HEADS, TOP])
        least = st.sb("least", [P, HEADS])
        sums, kept = st.sb("sums", [P, 2, BLK]), st.sb("kept", [P, KEPT, BLK])
        weight, hidden = st.sb("weight", [P, EXPERTS]), st.sb("hidden", [P, EXPERTS])
        hT = st.sb("hT", [P, 2, 4 * P])
        loaded, steps_done, alone = st.sem("loaded"), st.sem("steps_done"), st.sem("alone")
        xn_ready, xT_psum_ready, xT_ready, sims_psum_ready, sims_ready, simsT_psum_ready, simsT_high_ready, simsT_ready, \
            sums_psum_ready, sums_ready, kept_ready, pool_added, hid_psum_ready, gelu_done, hidden_ready, hT_psum_ready, hT_ready, \
            y_ready, tile_done = (st.sem(n) for n in (
                "xn_ready", "xT_psum_ready", "xT_ready", "sims_psum_ready", "sims_ready", "simsT_psum_ready",
                "simsT_high_ready", "simsT_ready", "sums_psum_ready", "sums_ready", "kept_ready", "pool_added", "hid_psum_ready",
                "gelu_done", "hidden_ready", "hT_psum_ready", "hT_ready", "y_ready", "tile_done"))
        SUMS, WORK, XT, Y = 0, 4, 6, 7
        block = st.block()

        def two_banks(first):
            return ps[:, first:first + 2, :].rearrange("p b n -> p (b n)")

        @block.sync
        def _(sp):
            sp.dma_start(gain[:], dram["L2_ffn_norm"]).then_inc(loaded, 16)
            sp.dma_start(downT[:], dram["L2_ffn_downT"].rearrange("(c p) e -> p c e", p=P)).then_inc(loaded, 16)
            sp.dma_start(up[:], dram["L2_ffn_expert_up"].rearrange("(c p) n -> p c n", p=P)).then_inc(loaded, 16)

        @block.tensor
        def _(pe):
            def turn_x(t):
                pe.wait_ge(xn_ready, t + 1)
                for c in range(DC):
                    last = nc.tensor.transpose(ps[:, XT, c * P:(c + 1) * P], xn[:, c * P:(c + 1) * P], g.ident[:])
                last.then_inc(xT_psum_ready, 1)

            def similarities(t):
                pe.wait_ge(xT_ready, t + 1)
                for j in range(2):
                    for c in range(DC):
                        last = nc.tensor.matmul(ps[:, WORK + j, :], xT[:, c, :], sim_w[:, c, j * 512:(j + 1) * 512],
                                                start=(c == 0), stop=(c == DC - 1))
                last.then_inc(sims_psum_ready, 1)

            def turn_similarities(t):
                pe.wait_ge(sims_ready, t + 1)
                for head in range(HEADS):
                    last = nc.tensor.transpose(ps[:, WORK + head // 4, (head % 4) * P:(head % 4 + 1) * P],
                                               sims[:, 2 * head:2 * head + 2, :].rearrange("p s k -> p (s k)"), g.ident[:])
                last.then_inc(simsT_psum_ready, 1)

            def hidden_units(t, k):
                if k >= 2:
                    pe.wait_ge(gelu_done, HB * t + k - 1)
                for c in range(DC):
                    last = nc.tensor.matmul(ps[:, WORK + k % 2, :], xT[:, c, :], downT[:, c, k * 512:(k + 1) * 512],
                                            start=(c == 0), stop=(c == DC - 1))
                last.then_inc(hid_psum_ready, 1)

            def project(t):
                def turn(k):
                    pe.wait_ge(hidden_ready, HB * t + k + 1)
                    if k >= 2:
                        pe.wait_ge(hT_ready, HB * t + k - 1)
                    first = 4 * (HB - 1 - k)
                    for i in range(4):
                        last = nc.tensor.transpose(ps[:, WORK + k % 2, i * P:(i + 1) * P],
                                                   hidden[:, (first + i) * P:(first + i + 1) * P], g.ident[:])
                    last.then_inc(hT_psum_ready, 1)

                turn(0)
                for k in range(HB):
                    if k < HB - 1:
                        turn(k + 1)
                    pe.wait_ge(hT_ready, HB * t + k + 1)
                    for i in range(4):
                        last = nc.tensor.matmul(ps[:, Y, 0:D], hT[:, k % 2, i * P:(i + 1) * P], up[:, 4 * (HB - 1 - k) + i, :],
                                                start=(k == 0 and i == 0), stop=(k == HB - 1 and i == 3))
                last.then_inc(y_ready, 1)

            def step(t, ahead=True):
                pe.wait_ge(simsT_ready, t + 1)
                for u, (head, q) in enumerate(UNITS):
                    if u >= 2:
                        pe.wait_ge(sums_ready, NU * t + u - 1)
                    for j in range(2):
                        for part in range(2):
                            last = nc.tensor.matmul(ps[:, SUMS + 2 * (u % 2) + j, :], simsT[:, part, head, :],
                                                    spread[:, q * BLK + j * 512:q * BLK + (j + 1) * 512],
                                                    start=(part == 0), stop=(part == 1))
                    last.then_inc(sums_psum_ready, 1)
                    if u in HIDDEN:
                        hidden_units(t, HIDDEN[u])
                    if ahead and u == AHEAD_TURN:
                        turn_x(t + 1)
                    if ahead and u == AHEAD_SIM:
                        pe.wait_ge(gelu_done, HB * t + HB)
                        similarities(t + 1)
                if ahead:
                    turn_similarities(t + 1)
                    pe.wait_ge(simsT_ready, t + 2)
                project(t)

            turn_x(0)
            similarities(0)
            turn_similarities(0)
            pe.wait_ge(loaded, 48)
            with pe.Fori(0, TILES - 1) as t:
                step(t)
            step(TILES - 1, ahead=False)

        @block.gpsimd
        def _(pool):
            def step(t, ahead=True):
                added = 0
                for u, (head, q) in enumerate(UNITS):
                    if head > 0 and q != OWN:
                        part = weight[:, q * BLK:(q + 1) * BLK]
                        pool.wait_ge(kept_ready, NU * t + u + 1)
                        if head > 1 or q > 0:
                            pool.wait_ge(pool_added, POOL_ADDS * t + added)
                        nc.gpsimd.tensor_tensor(part, part, kept[:, u % KEPT, :], ALU.add).then_inc(pool_added, 1)
                        added += 1
                    if ahead and u == AHEAD_X:
                        norm.gpsimd(pool, t + 1)
                        norm2.gpsimd(pool, t + 1)

            norm.gpsimd(pool, 0)
            norm2.gpsimd(pool, 0)
            with pool.Fori(0, TILES - 1) as t:
                step(t)
            step(TILES - 1, ahead=False)

        @block.scalar
        def _(act):
            def similarities(t):
                act.wait_ge(sims_psum_ready, t + 1)
                nc.scalar.activation(sims[:].rearrange("p s k -> p (s k)"), two_banks(WORK), ACT.Copy).then_inc(sims_ready, 1)

            def turned_similarities(t):
                act.wait_ge(simsT_psum_ready, t + 1)
                nc.scalar.activation(simsT[:, 0].rearrange("p h n -> p (h n)"), two_banks(WORK), ACT.Copy)\
                    .then_inc(simsT_high_ready, 1)

            def step(t, ahead=True):
                for u in range(NU):
                    act.wait_ge(sums_psum_ready, NU * t + u + 1)
                    if u >= 2:
                        act.wait_ge(kept_ready, NU * t + u - 1)
                    nc.scalar.activation(sums[:, u % 2, :], two_banks(SUMS + 2 * (u % 2)), ACT.Copy).then_inc(sums_ready, 1)
                    if u in HIDDEN:
                        k = HIDDEN[u]
                        act.wait_ge(hid_psum_ready, HB * t + k + 1)
                        nc.scalar.activation(hidden[:, k * 512:(k + 1) * 512], ps[:, WORK + k % 2, :], ACT.Gelu)\
                            .then_inc(gelu_done, 1)
                    if ahead and u == AHEAD_SIM + 1:
                        similarities(t + 1)
                if ahead:
                    turned_similarities(t + 1)
                for k in range(HB):
                    act.wait_ge(hT_psum_ready, HB * t + k + 1)
                    nc.scalar.activation(hT[:, k % 2, :], ps[:, WORK + k % 2, :], ACT.Copy).then_inc(hT_ready, 1)

            similarities(0)
            turned_similarities(0)
            with act.Fori(0, TILES - 1) as t:
                step(t)
            step(TILES - 1, ahead=False)

        @block.vector
        def _(dve):
            norm_links = NORM_LINKS["layer"] + NORM_LINKS["rms"] + 1
            top_links = 8
            own_links = HEADS - 1
            per = norm_links + top_links + own_links

            def normalised(t, s):
                s.link(norm.vector(dve, s, t, tile_of(g.x, t), xn[:], "layer"))
                norm2.vector(dve, s, t, xn[:], xn[:], "rms").then_inc(xn_ready, 1)

            def turned(t):
                dve.wait_ge(xT_psum_ready, t + 1)
                for c in range(DC):
                    last = nc.vector.tensor_scalar(xT[:, c, :], ps[:, XT, c * P:(c + 1) * P], gain[:, c:c + 1], None, ALU.mult)
                last.then_inc(xT_ready, 1)

            def low_part(t):
                dve.wait_ge(sims_ready, t + 1)
                dve.wait_ge(simsT_high_ready, t + 1)
                nc.vector.tensor_tensor(simsT[:, 1].rearrange("p h n -> p (h n)"), two_banks(WORK),
                                        simsT[:, 0].rearrange("p h n -> p (h n)").bitcast(F32), ALU.subtract)\
                    .then_inc(simsT_ready, 1)

            def bounds(t, s):
                for k in range(SIDES):
                    last = nc.vector.max(best[:, k, 0:8], sims[:, k, :])
                s.link(last, alone)
                for k in range(SIDES):
                    last = nc.vector.match_replace(rest[:, k, :], best[:, k, 0:8], sims[:, k, :], MASKED)
                s.link(last, alone)
                for k in range(SIDES):
                    last = nc.vector.max(best[:, k, 8:16], rest[:, k, :])
                s.link(last)
                for head in range(HEADS):
                    last = nc.vector.tensor_tensor(pairs[:, head, :].rearrange("p (i j) -> p i j", i=TOP),
                                                   best[:, 2 * head, :].unsqueeze(2).broadcast_to([P, TOP, TOP]),
                                                   best[:, 2 * head + 1, :].unsqueeze(1).broadcast_to([P, TOP, TOP]), ALU.add)
                s.link(last, alone)
                for head in range(HEADS):
                    last = nc.vector.max(top[:, head, 0:8], pairs[:, head, :])
                s.link(last, alone)
                for head in range(HEADS):
                    last = nc.vector.match_replace(pairs[:, head, :], top[:, head, 0:8], pairs[:, head, :], MASKED)
                s.link(last, alone)
                for head in range(HEADS):
                    last = nc.vector.max(top[:, head, 8:16], pairs[:, head, :])
                s.link(last)
                s.link(nc.vector.tensor_scalar(least[:], top[:, :, TOP - 1], 0.0, 1.0 - 2.0 ** -22, ALU.max, ALU.mult))

            def step(t, base, ahead=True):
                s = Steps(dve, steps_done, base)
                added = 0
                adds_before = {}
                for u, (head, q) in enumerate(UNITS):
                    adds_before[u] = added
                    added += head > 0 and q != OWN
                for u, (head, q) in enumerate(UNITS):
                    dve.wait_ge(sums_ready, NU * t + u + 1)
                    part = weight[:, q * BLK:(q + 1) * BLK]
                    if head > 0 and u >= KEPT and UNITS[u - KEPT][0] > 0 and UNITS[u - KEPT][1] != OWN:
                        dve.wait_ge(pool_added, POOL_ADDS * t + adds_before[u - KEPT] + 1)
                    dst = part if head == 0 else kept[:, u % KEPT, :]
                    unit = sums[:, u % 2, :]
                    nc.vector.scalar_tensor_tensor(out=dst, in0=unit, scalar=least[:, head:head + 1], in1=unit,
                                                   op0=ALU.is_ge, op1=ALU.mult).then_inc(kept_ready, 1)
                    if head > 0 and q == OWN:
                        dve.wait_ge(kept_ready, NU * t + u + 1)
                        s.link(nc.vector.tensor_tensor(part, part, kept[:, u % KEPT, :], ALU.add))
                    if ahead and u == AHEAD_X:
                        normalised(t + 1, s)
                    if ahead and u == AHEAD_TURN:
                        turned(t + 1)
                dve.wait_ge(gelu_done, HB * t + HB)
                for k in reversed(range(HB)):
                    if k == HB - BLK // 512 - 1:
                        if ahead:
                            low_part(t + 1)
                        dve.wait_ge(pool_added, POOL_ADDS * t + POOL_ADDS)
                    part = slice(k * 512, (k + 1) * 512)
                    nc.vector.tensor_tensor(hidden[:, part], hidden[:, part], weight[:, part], ALU.mult).then_inc(hidden_ready, 1)
                if ahead:
                    bounds(t + 1, s)
                x = tile_of(g.x, t)
                dve.wait_ge(y_ready, t + 1)
                nc.vector.scalar_tensor_tensor(out=x, in0=ps[:, Y, 0:D], scalar=g.gates[:, GATE_FFN + 2:GATE_FFN + 3], in1=x,
                                               op0=ALU.mult, op1=ALU.add).then_inc(tile_done, 1)

            dve.wait_ge(loaded, 48)
            s = Steps(dve, steps_done)
            normalised(0, s)
            turned(0)
            low_part(0)
            bounds(0, s)
            assert s.n == norm_links + top_links
            with dve.Fori(0, TILES - 1) as t:
                step(t, norm_links + top_links + per * t)
            step(TILES - 1, norm_links + top_links + per * (TILES - 1), ahead=False)
            dve.wait_ge(tile_done, TILES)


def fold_product_keys(nc, g, dram, sim_w, spread):
    SIDES, KEYS = dram["L2_ffn_keysT"].shape[1:]
    ps = g.ps
    with ExitStack() as ctx:
        st = Stage(nc, ctx, "fk")
        wqT, keysT = st.sb("wqT", [P, SIDES, D]), st.sb("keysT", [P, SIDES, KEYS])
        loaded, psum_ready, made, spread_made = (st.sem(n) for n in ("loaded", "psum_ready", "made", "spread_made"))
        block = st.block()

        @block.sync
        def _(sp):
            sp.dma_start(wqT[:], dram["L2_ffn_wqT"]).then_inc(loaded, 16)
            sp.dma_start(keysT[:], dram["L2_ffn_keysT"]).then_inc(loaded, 16)

        @block.tensor
        def _(pe):
            pe.wait_ge(loaded, 32)
            for c in range(DC):
                for k in range(SIDES):
                    last = nc.tensor.matmul(ps[:, 2 * c + k // 8, (k % 8) * KEYS:(k % 8 + 1) * KEYS],
                                            wqT[:, k, c * P:(c + 1) * P], keysT[:, k, :], start=True, stop=True)
                last.then_inc(psum_ready, 1)

        @block.vector
        def _(dve):
            for half in range(2):
                rows = slice(half * KEYS, (half + 1) * KEYS)
                own = g.ident[rows, rows]
                wide = own.unsqueeze(2) if half == 0 else own.unsqueeze(1)
                nc.vector.tensor_copy(spread[rows, :].rearrange("p (i j) -> p i j", i=KEYS),
                                      wide.broadcast_to([KEYS, KEYS, KEYS])).then_inc(spread_made, 1)
            for c in range(DC):
                dve.wait_ge(psum_ready, c + 1)
                nc.vector.tensor_copy(sim_w[:, c, :], ps[:, 2 * c:2 * c + 2, :].rearrange("p b n -> p (b n)"))\
                    .then_inc(made, 1)


def causal_attention_block(nc, g, dram, inner):
    for b in range(B):
        project_heads(nc, g, dram, b, inner)
        attend_heads(nc, g, dram, b, inner)


HEAD, NKV = 16, 4
QKV = (NH + 2 * NKV) * HEAD
QK = (NH + NKV) * HEAD


def project_heads(nc, g, dram, b, inner):
    HALF = HEAD // 2
    heads = NH + NKV
    ps = g.ps
    g.qkT = nc.dram_tensor(f"qkT{b}", (QK, S), F32).ap()
    g.values = nc.dram_tensor(f"values{b}", (NKV, P, TB, HEAD), F32).ap()
    with ExitStack() as ctx:
        st = Stage(nc, ctx, f"ph{b}")
        wqkv, gain = st.sb("wqkv", [P, DC, QKV]), st.sb("gain", [P, DC])
        cos, sin = st.sb("cos", [P, TB, HALF]), st.sb("sin", [P, TB, HALF])
        norm, norm2 = Norm(nc, g, st), Norm(nc, g, st, "2")
        xn, xT = st.sb("xn", [P, D]), st.sb("xT", [P, DC, P])
        qkv, turned = st.sb("qkv", [P, QKV]), st.sb("turned", [P, QK])
        prods = [st.sb(f"prod{n}", [P, heads, HALF]) for n in range(4)]
        qkT = st.sb("qkT", [P, 3, P])
        loaded, steps_done, prods_ready = st.sem("loaded"), st.sem("steps_done"), st.sem("prods_ready")
        xn_ready, xT_psum_ready, xT_ready, qkv_psum_ready, qkv_ready, turned_ready, qkT_psum_ready, qkT_ready, stored, \
            values_stored = (st.sem(n) for n in (
                "xn_ready", "xT_psum_ready", "xT_ready", "qkv_psum_ready", "qkv_ready", "turned_ready",
                "qkT_psum_ready", "qkT_ready", "stored", "values_stored"))
        XT, QP, TP = 0, 1, 2
        block = st.block()

        @block.sync
        def _(sp):
            sp.dma_start(wqkv[:], dram["L3_ffn_wqkvT"].rearrange("(c p) n -> p c n", p=P)).then_inc(loaded, 16)
            sp.dma_start(gain[:], dram["L3_ffn_ln1"]).then_inc(loaded, 16)
            sp.dma_start(cos[:], dram["rope_cos"].rearrange("(t p) n -> p t n", p=P)).then_inc(loaded, 16)
            sp.dma_start(sin[:], dram["rope_sin"].rearrange("(t p) n -> p t n", p=P)).then_inc(loaded, 16)
            with sp.Fori(0, TB) as t:
                sp.wait_ge(qkv_ready, t + 1)
                sp.dma_start(g.values[:, :, bass.ds(t, 1), :].rearrange("h p a n -> p h (a n)"),
                             qkv[:, QK:].rearrange("p (h n) -> p h n", h=NKV)).then_inc(values_stored, 16)
                sp.wait_ge(qkT_ready, t + 1)
                for c in range(3):
                    rows = min(P, QK - c * P)
                    sp.dma_start(g.qkT[c * P:c * P + rows, bass.ds(t * P, P)], qkT[0:rows, c, :]).then_inc(stored, 16)
            sp.wait_ge(stored, 48 * TB)
            sp.wait_ge(values_stored, 16 * TB)

        @block.tensor
        def _(pe):
            pe.wait_ge(loaded, 64)
            with pe.Fori(0, TB) as t:
                pe.wait_ge(xn_ready, t + 1)
                for c in range(DC):
                    last = nc.tensor.transpose(ps[:, XT, c * P:(c + 1) * P], xn[:, c * P:(c + 1) * P], g.ident[:])
                last.then_inc(xT_psum_ready, 1)
                pe.wait_ge(xT_ready, t + 1)
                for c in range(DC):
                    last = nc.tensor.matmul(ps[:, QP, 0:QKV], xT[:, c, :], wqkv[:, c, :], start=(c == 0), stop=(c == DC - 1))
                last.then_inc(qkv_psum_ready, 1)
                pe.wait_ge(turned_ready, t + 1)
                for c in range(3):
                    rows = min(P, QK - c * P)
                    last = nc.tensor.transpose(ps[0:rows, TP, c * P:(c + 1) * P], turned[:, c * P:c * P + rows], g.ident[:])
                last.then_inc(qkT_psum_ready, 1)

        @block.gpsimd
        def _(pool):
            with pool.Fori(0, TB) as t:
                norm.gpsimd(pool, t)
                norm2.gpsimd(pool, t)

        @block.vector
        def _(dve):
            per = NORM_LINKS["layer"] + NORM_LINKS["rms"] + 1
            dve.wait_ge(loaded, 64)
            with dve.Fori(0, TB) as t:
                s = Steps(dve, steps_done, t * per)
                own = tile_of(inner, b * TB + t)
                s.link(norm.vector(dve, s, t, tile_of(g.x, b * TB + t), own, "layer"), norm.waits_alone)
                norm2.vector(dve, s, t, own, xn[:], "rms").then_inc(xn_ready, 1)
                dve.wait_ge(xT_psum_ready, t + 1)
                for c in range(DC):
                    last = nc.vector.tensor_scalar(xT[:, c, :], ps[:, XT, c * P:(c + 1) * P], gain[:, c:c + 1], None, ALU.mult)
                last.then_inc(xT_ready, 1)
                dve.wait_ge(qkv_psum_ready, t + 1)
                nc.vector.tensor_copy(qkv[:], ps[:, QP, 0:QKV]).then_inc(qkv_ready, 1)
                dve.wait_ge(qkv_ready, t + 1)
                pair = qkv[:, 0:QK].rearrange("p (h s n) -> p s h n", s=2, n=HALF)
                out = turned[:].rearrange("p (h s n) -> p s h n", s=2, n=HALF)
                tables = [tab[:, bass.ds(t, 1), :].broadcast_to([P, heads, HALF]) for tab in (cos, sin)]
                for k, (half, table) in enumerate(((0, 0), (1, 1), (1, 0), (0, 1))):
                    last = nc.vector.tensor_tensor(prods[k][:], pair[:, half], tables[table], ALU.mult)
                last.then_inc(prods_ready, 1)
                dve.wait_ge(prods_ready, t + 1)
                nc.vector.tensor_tensor(out[:, 0], prods[0][:], prods[1][:], ALU.subtract)
                nc.vector.tensor_tensor(out[:, 1], prods[2][:], prods[3][:], ALU.add).then_inc(turned_ready, 1)
                dve.wait_ge(qkT_psum_ready, t + 1)
                nc.vector.tensor_scalar(qkT[:, 0:2, :], ps[:, TP, 0:2 * P].rearrange("p (c n) -> p c n", c=2),
                                        HEAD ** -0.5, None, ALU.mult)
                nc.vector.tensor_copy(qkT[0:QK - 2 * P, 2, :], ps[0:QK - 2 * P, TP, 2 * P:3 * P]).then_inc(qkT_ready, 1)
                dve.wait_ge(values_stored, 16 * t + 16)
                dve.wait_ge(stored, 48 * t + 48)


def attend_heads(nc, g, dram, b, inner):
    ps = g.ps
    with ExitStack() as ctx:
        st = Stage(nc, ctx, f"ah{b}")
        q, k, v = st.sb("q", [HEAD, 2, S]), st.sb("k", [HEAD, 2, S]), st.sb("v", [P, 2, TB, HEAD])
        probs, probsT = st.sb("probs", [P, 2, S]), st.sb("probsT", [P, 2, S])
        lowest, total, share = st.sb("lowest", [P, 2]), st.sb("total", [P, 2]), st.sb("share", [P, 2])
        attended = st.sb("attended", [P, TB, NH * HEAD])
        wo = st.sb("wo", [P, DC, D])
        row, rowT = st.sb("row", [P, D]), st.sb("rowT", [P, DC, P])
        head_loaded = [st.sem(f"head_loaded{n}") for n in range(2)]
        wo_loaded = st.sem("wo_loaded")
        scores_ready, masked, max_ready, exp_done, pT_psum_ready, pT_ready, o_ready, share_ready, unit_done, \
            row_ready, rowT_psum_ready, rowT_ready, y_ready, tile_done = (st.sem(n) for n in (
                "scores_ready", "masked", "max_ready", "exp_done", "pT_psum_ready", "pT_ready", "o_ready", "share_ready",
                "unit_done", "row_ready", "rowT_psum_ready", "rowT_ready", "y_ready", "tile_done"))
        SC, PT, O = 0, 4, 6
        UNITS = TB
        block = st.block()

        def banks(first, n):
            return ps[:, first:first + 2, :].rearrange("p b n -> p (b n)")[:, 0:n]

        @block.sync
        def _(sp):
            sp.dma_start(wo[:], dram["L3_ffn_woT"].rearrange("(c p) n -> p c n", p=P)).then_inc(wo_loaded, 16)

            def load(h, slot):
                for dst, src in ((q, g.qkT[bass.ds(h * HEAD, HEAD), :]),
                                 (k, g.qkT[bass.ds(NH * HEAD + (h // (NH // NKV)) * HEAD, HEAD), :])):
                    sp.dma_start(dst[:, slot, :], src).then_inc(head_loaded[slot], 16)
                sp.dma_start(v[:, slot], g.values[bass.ds(h // (NH // NKV), 1)].rearrange("a p t n -> p (a t) n"))\
                    .then_inc(head_loaded[slot], 16)

            load(0, 0)
            load(1, 1)
            with sp.Fori(1, NH // 2) as pair:
                for slot in range(2):
                    sp.wait_ge(unit_done, UNITS * (2 * pair + slot - 1))
                    load(2 * pair + slot, slot)

        @block.tensor
        def _(pe):
            def scores(u, slot, i):
                for j in range(0, i + 1, 4):
                    n = min(4, i + 1 - j) * P
                    last = nc.tensor.matmul(ps[:, SC + 2 * (i % 2) + j // 4, 0:n], q[:, slot, i * P:(i + 1) * P],
                                            k[:, slot, j * P:j * P + n], start=True, stop=True)
                last.then_inc(scores_ready, 1)

            with pe.Fori(0, NH // 2) as pair:
                for slot in range(2):
                    head = 2 * pair + slot
                    pe.wait_ge(head_loaded[slot], 48 * pair + 48)
                    for i in range(TB + 1):
                        if i < TB:
                            scores(UNITS * head + i, slot, i)
                        if i == 0:
                            continue
                        n, u = i, UNITS * head + i - 1
                        pe.wait_ge(exp_done, u + 1)
                        for j in range(n):
                            last = nc.tensor.transpose(ps[:, PT + j // 4, (j % 4) * P:(j % 4 + 1) * P],
                                                       probs[:, (n - 1) % 2, j * P:(j + 1) * P], g.ident[:])
                        last.then_inc(pT_psum_ready, 1)
                        pe.wait_ge(pT_ready, u + 1)
                        for j in range(n):
                            last = nc.tensor.matmul(ps[:, O + (n - 1) % 2, 0:HEAD], probsT[:, (n - 1) % 2, j * P:(j + 1) * P],
                                                    v[:, slot, j, :], start=(j == 0), stop=(j == n - 1))
                        last.then_inc(o_ready, 1)
            pe.wait_ge(wo_loaded, 16)
            with pe.Fori(0, TB) as t:
                pe.wait_ge(row_ready, t + 1)
                for c in range(DC):
                    last = nc.tensor.transpose(ps[:, PT, c * P:(c + 1) * P], row[:, c * P:(c + 1) * P], g.ident[:])
                last.then_inc(rowT_psum_ready, 1)
                pe.wait_ge(rowT_ready, t + 1)
                for c in range(DC):
                    last = nc.tensor.matmul(ps[:, SC, 0:D], rowT[:, c, :], wo[:, c, :], start=(c == 0), stop=(c == DC - 1))
                last.then_inc(y_ready, 1)

        @block.scalar
        def _(act):
            with act.Fori(0, NH // 2) as pair:
                for slot in range(2):
                    for i in range(TB):
                        u = UNITS * (2 * pair + slot) + i
                        act.wait_ge(max_ready, u + 1)
                        n = (i + 1) * P
                        nc.scalar.activation(probs[:, i % 2, 0:n], banks(SC + 2 * (i % 2), n), ACT.Exp,
                                             bias=lowest[:, i % 2:i % 2 + 1], accum_out=total[:, i % 2:i % 2 + 1])\
                            .then_inc(exp_done, 1)

        @block.vector
        def _(dve):
            def finish(u, slot, i, head):
                n = (i + 1) * P
                dve.wait_ge(pT_psum_ready, u + 1)
                nc.vector.tensor_copy(probsT[:, i % 2, 0:n], banks(PT, n)).then_inc(pT_ready, 1)
                dve.wait_ge(exp_done, u + 1)
                nc.vector.reciprocal(share[:, i % 2:i % 2 + 1], total[:, i % 2:i % 2 + 1]).then_inc(share_ready, 1)
                dve.wait_ge(share_ready, u + 1)
                dve.wait_ge(o_ready, u + 1)
                nc.vector.tensor_scalar(attended[:, i, bass.ds(head * HEAD, HEAD)], ps[:, O + i % 2, 0:HEAD],
                                        share[:, i % 2:i % 2 + 1], None, ALU.mult).then_inc(unit_done, 1)

            with dve.Fori(0, NH // 2) as pair:
                for slot in range(2):
                    head = 2 * pair + slot
                    for i in range(TB):
                        u = UNITS * head + i
                        n = (i + 1) * P
                        bank = banks(SC + 2 * (i % 2), n)
                        dve.wait_ge(scores_ready, u + 1)
                        nc.vector.tensor_tensor(bank[:, n - P:n], bank[:, n - P:n], g.causal[:], ALU.add).then_inc(masked, 1)
                        dve.wait_ge(masked, u + 1)
                        nc.vector.tensor_reduce(lowest[:, i % 2:i % 2 + 1], bank, AX_X, ALU.max, negate=True)\
                            .then_inc(max_ready, 1)
                        if i > 0:
                            finish(u - 1, slot, i - 1, head)
                    finish(UNITS * head + TB - 1, slot, TB - 1, head)
            with dve.Fori(0, TB) as t:
                nc.vector.tensor_copy(row[:], tile_of(attended, t)).then_inc(row_ready, 1)
                dve.wait_ge(rowT_psum_ready, t + 1)
                nc.vector.tensor_copy(rowT[:], ps[:, PT, 0:D].rearrange("p (c n) -> p c n", c=DC)).then_inc(rowT_ready, 1)
                dve.wait_ge(y_ready, t + 1)
                own = tile_of(inner, b * TB + t)
                nc.vector.tensor_tensor(own, own, ps[:, SC, 0:D], ALU.add).then_inc(tile_done, 1)
                dve.wait_ge(tile_done, t + 1)


def transformer_layer_3(nc, g, dram):
    with ExitStack() as ctx:
        st = Stage(nc, ctx, "m3")
        inner = st.sb("inner", [P, TILES, D])
        causal_attention_block(nc, g, dram, inner)
        mixture(nc, g, dram, 3, inner, inner)
        add_gated(nc, g, inner, 3)


class Shared:
    pass


def attention_layer(layer):
    def stage(nc, g, dram):
        cross_attention(nc, g, dram, layer)
    return stage


STAGES = [(1, linear_attention), (2, sign_network), (3, attention_layer(1)), (4, expert_layer_1), (5, attention_layer(2)), (6, product_key_experts), (7, attention_layer(3)),
          (8, transformer_layer_3)]


def build(nc, dram, out, upto=99):
    with ExitStack() as ctx:
        g = Shared()
        st = Stage(nc, ctx, "g")
        g.x = st.sb("x", [P, TILES, D])
        g.gates = st.sb("gates", [P, 16])
        g.ident = st.sb("ident", [P, P])
        g.identb = st.sb("identb", [P, P], BF16)
        g.minus_half = st.sb("minus_half", [P, 2])
        g.ones = st.sb("ones", [P, P])
        g.causal = st.sb("causal", [P, P])
        g.ps = ctx.enter_context(nc.psum_tensor("ps", [P, 8, 512], F32))
        load_stream(nc, g, dram)
        for n, stage in STAGES:
            if n <= upto:
                stage(nc, g, dram)
        store_stream(nc, g, out)


def expert_chunks(gate, up, down):
    n = gate.shape[1] // P
    left = [w.reshape(DC, P, n, P).transpose(2, 1, 0, 3).reshape(n, P, DC * P) for w in (gate, up)]
    return np.concatenate([*left, down.reshape(n, P, D)], axis=2)


def expert_selector(experts, hidden):
    return np.tile(np.kron(np.eye(experts), np.ones((1, hidden))), (3, 1)).astype(mybir.dt.np(BF16))


def lay_out(v):
    a = {k: np.asarray(x) for k, x in v.items()}
    a["ctxT"] = a["ctx_1024"].transpose(2, 0, 1).reshape(D, B * NKEY)
    a["L0_xattn_WqT"] = a["L0_xattn_Wq"].T
    a["maskT_ff1"] = a["mask_BxS2x1_ff1"][:, :, 0].T
    for n in (1, 2):
        a[f"L{n}_xattn_WqT"] = a[f"L{n}_xattn_Wq"].reshape(D, NH, D // NH).transpose(2, 1, 0)
        a[f"L{n}_xattn_bias"] = np.stack([a[f"L{n}_xattn_b{w}"].reshape(NH, D // NH) for w in "qkv"]).transpose(2, 0, 1)
    a["L3_xattn_WqT"] = a["L3_xattn_w_q"].reshape(D, NH, -1).transpose(2, 1, 0)
    a["L3_xattn_Wk"], a["L3_xattn_Wv"] = np.split(a["L3_xattn_w_kv"], 2, axis=1)
    a["L3_xattn_Wo"], a["L3_xattn_bo"] = a["L3_xattn_w_out"], a["L3_xattn_b_out"]
    a["L3_xattn_affine"] = np.stack([a["L3_xattn_ln_gamma"], a["L3_xattn_ln_beta"]]).reshape(2, DC, P).transpose(2, 0, 1)
    a["L1_xattn_mask"], a["L2_xattn_mask"] = a["mask_Bx1x1xS2_fk0"][:, 0, 0], a["mask_BxS2_ik0"]
    used = [f"L{n}_xattn_{w}" for n in (1, 2, 3) for w in ("WqT", "Wk", "Wv", "Wo", "bo")]
    used += ["L1_xattn_bias", "L2_xattn_bias", "L1_xattn_mask", "L2_xattn_mask", "L3_xattn_affine"]
    for n in range(3):
        a[f"L0_ffn_s{n}"] = a[f"L0_ffn_s{n}"].reshape(1)
        used += [f"L0_ffn_k{n}", f"L0_ffn_s{n}"]
    e, _, f = a["L1_ffn_Wg"].shape
    a["L1_moe_w"] = expert_chunks(a["L1_ffn_Wg"].transpose(1, 0, 2).reshape(D, e * f),
                                  a["L1_ffn_Wu"].transpose(1, 0, 2).reshape(D, e * f), a["L1_ffn_Wd"].reshape(e * f, D))
    a["L1_moe_sel"], a["L1_moe_router"] = expert_selector(e, f), a["L1_ffn_Ws"]
    f = a["L3_ffn_w2"].shape[2]
    gate, up = a["L3_ffn_w13"][:, :f], a["L3_ffn_w13"][:, f:]
    a["L3_moe_w"] = expert_chunks(gate.reshape(e * f, D).T, up.reshape(e * f, D).T,
                                  a["L3_ffn_w2"].transpose(0, 2, 1).reshape(e * f, D))
    a["L3_moe_sel"], a["L3_moe_router"] = expert_selector(e, f), a["L3_ffn_gate_w"].T
    a["L3_ffn_ln2"] = a["L3_ffn_ln2_w"].reshape(DC, P).T
    a["iota8"] = np.arange(8, dtype=np.float32)
    used += ["L1_moe_w", "L1_moe_sel", "L1_moe_router", "L1_ffn_bs", "L3_moe_w", "L3_moe_sel", "L3_moe_router",
             "L3_ffn_ln2", "iota8"]
    a["L2_ffn_wqT"] = a["L2_ffn_wq"].reshape(D, 16, P).transpose(2, 1, 0)
    a["L2_ffn_keysT"] = a["L2_ffn_keys"].transpose(3, 0, 2, 1).reshape(P, 16, 64)
    a["L2_ffn_downT"] = a["L2_ffn_expert_down"].T
    a["L2_ffn_norm"] = a["L2_ffn_norm_w"].reshape(DC, P).T
    used += ["L2_ffn_wqT", "L2_ffn_keysT", "L2_ffn_downT", "L2_ffn_norm", "L2_ffn_expert_up"]
    a["L3_ffn_wqkvT"], a["L3_ffn_woT"] = a["L3_ffn_wqkv"].T, a["L3_ffn_wo"].T
    a["L3_ffn_ln1"] = a["L3_ffn_ln1_w"].reshape(DC, P).T
    freq = np.float32(1.0) / np.float32(10000.0) ** (np.arange(0, HEAD, 2, dtype=np.float32) / np.float32(HEAD))
    angle = np.arange(S, dtype=np.float32)[:, None] * freq[None, :]
    a["rope_cos"], a["rope_sin"] = np.cos(angle), np.sin(angle)
    used += ["L3_ffn_wqkvT", "L3_ffn_woT", "L3_ffn_ln1", "rope_cos", "rope_sin"]
    used += ["x", "g_xattn", "g_ffn", "L3_xattn_gate", "ctxT", "maskT_ff1",
            "L0_xattn_Wk", "L0_xattn_Wv", "L0_xattn_Wo", "L0_xattn_WqT"]
    return {k: np.ascontiguousarray(a[k]) for k in used}


def kernel(**inputs):
    import concourse.bacc as bacc
    from concourse.bass_utils import run_bass_kernel_spmd

    nc = bacc.Bacc("TRN2", target_bir_lowering=False, num_devices=1)
    arrays = lay_out(inputs)
    dram = {k: nc.dram_tensor(f"in_{k}", a.shape, mybir.dt.from_np(a.dtype), kind="ExternalInput").ap()
            for k, a in arrays.items()}
    out = nc.dram_tensor("out_x", (B, S, D), F32, kind="ExternalOutput").ap()
    build(nc, dram, out)
    r = run_bass_kernel_spmd(nc, [{f"in_{k}": a for k, a in arrays.items()}], core_ids=[0])
    return r.results[0]["out_x"]
```

```python
from contextlib import ExitStack

import numpy as np

import concourse.bass as bass
from concourse import mybir

F32 = mybir.dt.float32
F32R = mybir.dt.float32r
BF16 = mybir.dt.bfloat16
I32 = mybir.dt.int32
U32 = mybir.dt.uint32
U8 = mybir.dt.uint8
ALU = mybir.AluOpType
ACT = mybir.ActivationFunctionType
AX_X = mybir.AxisListType.X

P = 128
B, S, D = 2, 1024, 256
TILES = B * S // P
TB = S // P
DC = D // P
NKEY = 77
NH = 16
HK = NH * NKEY
HKC = -(-HK // P)
HK_LAST = HK - (HKC - 1) * P
HPB = 512 // NKEY
GROUP = 512
NG = B * S // GROUP
TPG = GROUP // P
EPS = 1e-5
MASKED = -3.0e38
GATE_XATTN, GATE_FFN, GATE_L3 = 0, 4, 8

HEAD_BANKS = [(j, h0, min(HPB, NH - h0)) for j, h0 in enumerate(range(0, NH, HPB))]


class Steps:

    def __init__(self, eng, sem, base=0):
        self.eng, self.sem, self.base, self.n = eng, sem, base, 0

    def mark(self, ins):
        ins.then_inc(self.sem, 1)
        self.n += 1

    def link(self, ins, alone=None):
        self.mark(ins)
        self.eng.wait_ge(self.sem, self.base + self.n)
        if alone is not None:
            self.eng.sem_inc(alone, 1)


def flat(ap):
    return ap.rearrange("p a n -> p (a n)")


def tile_of(t3, t):
    return flat(t3[:, bass.ds(t, 1), :])


class Norm:

    def __init__(self, nc, g, st, name=""):
        self.nc, self.minus_half = nc, g.minus_half
        self.stats, self.agg = st.sb(f"stats{name}", [P, TILES, 6]), st.sb(f"agg{name}", [P, TILES, 2])
        self.power, self.rstd = st.sb(f"power{name}", [P, TILES]), st.sb(f"rstd{name}", [P, TILES])
        self.stats_ready, self.agg_ready, self.squared, self.var_ready, self.rstd_ready = (
            st.sem(f"{n}{name}") for n in ("stats_ready", "agg_ready", "squared", "var_ready", "rstd_ready"))

    def vector(self, dve, src, dst, kind, done):
        nc, tiles = self.nc, range(src.shape[1])
        mean, var = (self.agg[:, :, n] for n in range(2))
        for t in tiles:
            nc.vector.bn_stats(self.stats[:, t, :], src[:, t, :]).then_inc(self.stats_ready, 1)
        dve.wait_ge(self.stats_ready, len(tiles))
        for t in tiles:
            nc.vector.bn_aggr(self.agg[:, t, :], self.stats[:, t, :]).then_inc(self.agg_ready, 1)
        dve.wait_ge(self.agg_ready, len(tiles))
        if kind == "rms":
            nc.vector.tensor_tensor(self.power[:], mean, mean, ALU.mult).then_inc(self.squared, 1)
            dve.wait_ge(self.squared, 1)
            nc.vector.scalar_tensor_tensor(out=self.power[:], in0=self.power[:], scalar=EPS, in1=var,
                                           op0=ALU.add, op1=ALU.add).then_inc(self.var_ready, 1)
        else:
            nc.vector.tensor_scalar(self.power[:], var, EPS, None, ALU.add).then_inc(self.var_ready, 1)
        dve.wait_ge(self.rstd_ready, 1)
        for t in tiles:
            rstd = self.rstd[:, t:t + 1]
            if kind == "rms":
                nc.vector.tensor_scalar(dst[:, t, :], src[:, t, :], rstd, None, ALU.mult).then_inc(done, 1)
            else:
                nc.vector.tensor_scalar(dst[:, t, :], src[:, t, :], self.agg[:, t, 0:1], rstd, ALU.subtract, ALU.mult)\
                    .then_inc(done, 1)

    def gpsimd(self, pool):
        pool.wait_ge(self.var_ready, 1)
        self.nc.gpsimd.tensor_tensor(self.rstd[:], self.power[:], self.minus_half[:, 0:1].broadcast_to([P, TILES]), ALU.pow)\
            .then_inc(self.rstd_ready, 1)


class Stage:

    def __init__(self, nc, ctx, name):
        self.nc, self.ctx, self.name, self.sems = nc, ctx, name, []
        ctx.callback(self.clear)

    def clear(self):
        if self.sems:
            self.nc.clear_and_free_semaphores(self.sems)
            self.nc.all_engine_barrier()

    def sb(self, name, shape, dt=F32):
        return self.ctx.enter_context(self.nc.sbuf_tensor(f"{self.name}_{name}", shape, dt))

    def sem(self, name):
        self.sems.append(self.nc.alloc_semaphore(f"{self.name}_{name}"))
        return self.sems[-1]

    def block(self):
        return self.ctx.enter_context(self.nc.Block())


def load_stream(nc, g, dram):
    with ExitStack() as ctx:
        st = Stage(nc, ctx, "in")
        loaded, gates_loaded = st.sem("loaded"), st.sem("gates_loaded")
        zeroed, made, gates_done = st.sem("zeroed"), st.sem("made"), st.sem("gates_done")
        block = st.block()

        @block.sync
        def _(sp):
            sp.dma_start(g.x[:], dram["x"].rearrange("b (t p) d -> p (b t) d", p=P)).then_inc(loaded, 16)
            for src, at, n in (("g_xattn", GATE_XATTN, 4), ("g_ffn", GATE_FFN, 4), ("L3_xattn_gate", GATE_L3, 1)):
                sp.dma_start(g.gates[:, at:at + n], dram[src].partition_broadcast(P)).then_inc(gates_loaded, 16)
            sp.wait_ge(loaded, 16)

        @block.scalar
        def _(act):
            act.wait_ge(gates_loaded, 48)
            nc.scalar.activation(g.gates[:, 0:9], g.gates[:, 0:9], ACT.Tanh).then_inc(gates_done, 1)
            act.wait_ge(gates_done, 1)

        @block.gpsimd
        def _(pool):
            nc.gpsimd.memset(g.ident[:], 0.0).then_inc(zeroed, 1)
            nc.gpsimd.memset(g.identb[:], 0.0).then_inc(zeroed, 1)
            nc.gpsimd.memset(g.ones[:], 1.0).then_inc(made, 1)
            nc.gpsimd.memset(g.minus_half[:], -0.5).then_inc(made, 1)
            nc.gpsimd.memset(g.causal[:], 0.0).then_inc(zeroed, 1)
            pool.wait_ge(zeroed, 3)
            for m in (g.ident, g.identb):
                nc.gpsimd.affine_select(out=m[:], in_=m[:], compare_op=ALU.not_equal, fill=1.0, base=0,
                                        pattern=[[-1, P]], channel_multiplier=1).then_inc(made, 1)
            nc.gpsimd.affine_select(out=g.causal[:], in_=g.causal[:], compare_op=ALU.is_ge, fill=MASKED / 4, base=0,
                                    pattern=[[-1, P]], channel_multiplier=1).then_inc(made, 1)
            pool.wait_ge(made, 5)


def store_stream(nc, g, out):
    with ExitStack() as ctx:
        st = Stage(nc, ctx, "out")
        stored = st.sem("stored")
        block = st.block()

        @block.sync
        def _(sp):
            sp.dma_start(out.rearrange("b (t p) d -> p (b t) d", p=P), g.x[:]).then_inc(stored, 16)
            sp.wait_ge(stored, 16)


def linear_attention(nc, g, dram):
    with ExitStack() as ctx:
        st = Stage(nc, ctx, "la")
        ctxT = st.sb("ctxT", [P, DC, B * NKEY])
        wk, wv, wo, wqT = (st.sb(n, [P, DC, D]) for n in ("wk", "wv", "wo", "wqT"))
        mask = st.sb("mask", [P, B])
        pk, pv = (st.sb(n, [P, B, D]) for n in ("pk", "pv"))
        kvT, kvo, mat = (st.sb(n, [P, B, DC, D]) for n in ("kvT", "kvo", "mat"))
        norm = Norm(nc, g, st)
        xn = st.sb("xn", [P, TILES, D])
        xT = st.sb("xT", [P, 2, DC, P])
        loaded, keys_ready, kv_in_ready = st.sem("loaded"), st.sem("keys_ready"), st.sem("kv_in_ready")
        prod_ready, prod_used = st.sem("prod_ready"), st.sem("prod_used")
        xn_ready, xT_psum_ready, xT_ready, y_ready, tile_done = (
            st.sem(n) for n in ("xn_ready", "xT_psum_ready", "xT_ready", "y_ready", "tile_done"))
        ps = g.ps
        XT, Y = 0, 2
        block = st.block()

        @block.sync
        def _(sp):
            sp.dma_start(ctxT[:], dram["ctxT"].rearrange("(c p) k -> p c k", p=P)).then_inc(loaded, 16)
            for t, n in ((wk, "L0_xattn_Wk"), (wv, "L0_xattn_Wv"), (wo, "L0_xattn_Wo"), (wqT, "L0_xattn_WqT")):
                sp.dma_start(t[:], dram[n].rearrange("(c p) n -> p c n", p=P)).then_inc(loaded, 16)
            sp.dma_start(mask[0:NKEY, :], dram["maskT_ff1"]).then_inc(loaded, 16)

        @block.tensor
        def _(pe):
            pe.wait_ge(loaded, 96)
            for b in range(B):
                for w, bank in ((wk, 0), (wv, 1)):
                    for c in range(DC):
                        last = nc.tensor.matmul(ps[0:NKEY, 2 * b + bank, 0:D], ctxT[:, c, b * NKEY:(b + 1) * NKEY], w[:, c, :],
                                                start=(c == 0), stop=(c == DC - 1))
            last.then_inc(keys_ready, 1)
            pe.wait_ge(kv_in_ready, 2 * B)
            for b in range(B):
                for c in range(DC):
                    last = nc.tensor.matmul(ps[:, 4 + b, c * D:(c + 1) * D], pv[0:NKEY, b, c * P:(c + 1) * P],
                                            pk[0:NKEY, b, :], start=True, stop=True)
            last.then_inc(prod_ready, 1)
            for n, (lhs, rhs) in enumerate(((kvT, wo), (wqT, kvo))):
                pe.wait_ge(prod_used, n + 1)
                for b in range(B):
                    for m in range(DC):
                        for c in range(DC):
                            left = (lhs[:, b, c] if n == 0 else lhs[:, c])[:, m * P:(m + 1) * P]
                            right = rhs[:, c, :] if n == 0 else rhs[:, b, c, :]
                            last = nc.tensor.matmul(ps[:, 4 + b, m * D:(m + 1) * D], left, right,
                                                    start=(c == 0), stop=(c == DC - 1))
                last.then_inc(prod_ready, 1)
            def turn(t):
                pe.wait_ge(xn_ready, t + 1)
                if t >= 2:
                    pe.wait_ge(xT_ready, t - 1)
                for c in range(DC):
                    last = nc.tensor.transpose(ps[:, XT + t % 2, c * P:(c + 1) * P], xn[:, t, c * P:(c + 1) * P], g.ident[:])
                last.then_inc(xT_psum_ready, 1)

            turn(0)
            pe.wait_ge(prod_used, 3)
            for t in range(TILES):
                if t < TILES - 1:
                    turn(t + 1)
                pe.wait_ge(xT_ready, t + 1)
                if t >= 2:
                    pe.wait_ge(tile_done, t - 1)
                for c in range(DC):
                    last = nc.tensor.matmul(ps[:, Y + t % 2, 0:D], xT[:, t % 2, c, :], mat[:, t // TB, c, :],
                                            start=(c == 0), stop=(c == DC - 1))
                last.then_inc(y_ready, 1)

        @block.scalar
        def _(act):
            act.wait_ge(keys_ready, 1)
            for b in range(B):
                for dst, bank, fn in ((pk, 0, ACT.Silu), (pv, 1, ACT.Copy)):
                    nc.scalar.activation(dst[0:NKEY, b, :], ps[0:NKEY, 2 * b + bank, 0:D], fn, scale=mask[0:NKEY, b:b + 1])\
                        .then_inc(kv_in_ready, 1)
            for n, dst in enumerate((kvT, kvo, mat)):
                act.wait_ge(prod_ready, n + 1)
                for b in range(B):
                    scale = g.gates[:, GATE_XATTN:GATE_XATTN + 1] if n == 2 else 1.0
                    last = nc.scalar.activation(dst[:, b].rearrange("p c n -> p (c n)"), ps[:, 4 + b, :], ACT.Copy, scale=scale)
                last.then_inc(prod_used, 1)
            for t in range(TILES):
                act.wait_ge(xT_psum_ready, t + 1)
                if t >= 2:
                    act.wait_ge(y_ready, t - 1)
                nc.scalar.activation(xT[:, t % 2].rearrange("p c n -> p (c n)"), ps[:, XT + t % 2, 0:D], ACT.Copy)\
                    .then_inc(xT_ready, 1)

        @block.gpsimd
        def _(pool):
            norm.gpsimd(pool)

        @block.vector
        def _(dve):
            norm.vector(dve, g.x, xn, "layer", xn_ready)
            for t in range(TILES):
                dve.wait_ge(y_ready, t + 1)
                nc.vector.tensor_tensor(g.x[:, t, :], g.x[:, t, :], ps[:, Y + t % 2, 0:D], ALU.add).then_inc(tile_done, 1)


def split(nc, hi, lo, src):
    return nc.vector.tensor_copy(hi, src), lambda: nc.vector.tensor_tensor(lo, src, hi.bitcast(F32), ALU.subtract)


PASSES = ((0, 0), (1, 0), (0, 1))


def cross_attention(nc, g, dram, layer):
    full = layer == 3
    ps = g.ps
    with ExitStack() as ctx:
        st = Stage(nc, ctx, f"xa{layer}")
        scores_w = st.sb("scores_w", [P, 2, B, DC, HK], F32R)
        scores_b = st.sb("scores_b", [1, 2, B, 2 if full else HK], F32R)
        values_w = st.sb("values_w", [P, B, HKC, D])
        bo = st.sb("bo", [1, B, D])
        affine = st.sb("affine", [P, 2, DC])
        fold_context(nc, g, dram, layer, scores_w, scores_b, values_w, bo, affine)

        norm = Norm(nc, g, st)
        norm2 = Norm(nc, g, st, "2") if full else None
        centred_rows, row_ready = st.sem("centred_rows"), st.sem("row_ready")
        xn, row, xT = st.sb("xn", [P, TILES, D]), st.sb("row", [P, D]), st.sb("xT", [P, 2, DC, P], F32R)
        xT_whole = st.sb("xT_whole", [P, DC, P])
        probs = st.sb("probs", [P, NH, NKEY])
        probs_flat = probs[:].rearrange("p h k -> p (h k)")
        probsT = st.sb("probsT", [P, HKC, P])
        row_max, row_sum = st.sb("row_max", [P, NH]), st.sb("row_sum", [P, NH])
        ones = st.sb("ones", [1, P], F32R)
        steps_done, ones_ready = st.sem("steps_done"), st.sem("ones_ready")
        xn_ready, xT_psum_ready, xT_ready, scores_ready, centred, exp_done, probs_ready, pT_psum_ready, pT_ready, \
            y_ready, tile_done = (st.sem(n) for n in (
                "xn_ready", "xT_psum_ready", "xT_ready", "scores_ready", "centred", "exp_done", "probs_ready",
                "pT_psum_ready", "pT_ready", "y_ready", "tile_done"))
        SC, PT, XT, Y = 0, 3, 6, 7
        block = st.block()

        @block.tensor
        def _(pe):
            def turn_x(n):
                pe.wait_ge(row_ready, n + 1)
                for c in range(DC):
                    last = nc.tensor.transpose(ps[:, XT, c * P:(c + 1) * P], row[:, c * P:(c + 1) * P], g.ident[:])
                last.then_inc(xT_psum_ready, 1)

            def scores(n, b):
                for j, h0, heads in HEAD_BANKS:
                    cols = slice(h0 * NKEY, (h0 + heads) * NKEY)
                    out = ps[:, SC + j, 0:heads * NKEY]
                    for c in range(DC):
                        for left, right in PASSES:
                            last = nc.tensor.matmul(out, xT[:, left, c, :], scores_w[:, right, b, c, cols],
                                                    start=(c + left + right == 0),
                                                    stop=(full and (c, left, right) == (DC - 1, 0, 1)))
                    if not full:
                        for part in range(2):
                            last = nc.tensor.matmul(out, ones[0:1, :], scores_b[0:1, part, b, cols], start=False, stop=(part == 1))
                last.then_inc(scores_ready, 1)

            def step(n, b, b_next=None, turn=True, first=False):
                if b_next is not None:
                    pe.wait_ge(centred, n + 1)
                    pe.wait_ge(xT_ready, n + 2)
                    scores(n + 1, b_next)
                if turn:
                    turn_x(n + 2)
                pe.wait_ge(probs_ready, n + 1)
                for c in range(HKC):
                    w = P if c < HKC - 1 else HK_LAST
                    last = nc.tensor.transpose(ps[0:w, PT + c // 4, (c % 4) * P:(c % 4 + 1) * P],
                                               probs_flat[:, c * P:c * P + w], g.ident[:])
                last.then_inc(pT_psum_ready, 1)
                if not first:
                    pe.wait_ge(tile_done, n)
                pe.wait_ge(pT_ready, 4 * n + 4)
                for c in range(HKC):
                    w = P if c < HKC - 1 else HK_LAST
                    nc.tensor.matmul(ps[:, Y, 0:D], probsT[0:w, c, :], values_w[0:w, b, c, :], start=(c == 0), stop=False)
                nc.tensor.matmul(ps[:, Y, 0:D], g.ones[0:1, :], bo[0:1, b, :], start=False, stop=True).then_inc(y_ready, 1)

            turn_x(0)
            pe.wait_ge(ones_ready, 1)
            pe.wait_ge(xT_ready, 1)
            scores(0, 0)
            turn_x(1)
            step(0, 0, 0, first=True)
            with pe.Fori(1, TB - 1) as n:
                step(n, 0, 0)
            step(TB - 1, 0, 1)
            with pe.Fori(TB, TILES - 2) as n:
                step(n, 1, 1)
            step(TILES - 2, 1, 1, turn=False)
            step(TILES - 1, 1, turn=False)

        @block.gpsimd
        def _(pool):
            norm.gpsimd(pool)
            if full:
                norm2.gpsimd(pool)

        @block.scalar
        def _(act):
            def take_row(n):
                nc.scalar.activation(row[:], tile_of(xn, n), ACT.Copy).then_inc(row_ready, 1)

            def step(t, ahead=True):
                act.wait_ge(centred, t + 1)
                nc.scalar.activation(probs_flat, probs_flat, ACT.Exp).then_inc(exp_done, 1)
                if ahead:
                    act.wait_ge(xT_psum_ready, t + 2)
                    take_row(t + 2)
                act.wait_ge(pT_psum_ready, t + 1)
                for k in range(2):
                    nc.scalar.activation(probsT[:, 4 * k:4 * k + 4, :].rearrange("p c n -> p (c n)"), ps[:, PT + k, :],
                                         ACT.Copy).then_inc(pT_ready, 1)
                nc.scalar.activation(probsT[:, 8, :], ps[:, PT + 2, 0:P], ACT.Copy).then_inc(pT_ready, 1)
                nc.scalar.activation(probsT[0:HK_LAST, 9, :], ps[0:HK_LAST, PT + 2, P:2 * P], ACT.Copy)\
                    .then_inc(pT_ready, 1)

            act.wait_ge(xn_ready, TILES)
            take_row(0)
            act.wait_ge(xT_psum_ready, 1)
            take_row(1)
            with act.Fori(0, TILES - 2) as t:
                step(t)
            step(TILES - 2, ahead=False)
            step(TILES - 1, ahead=False)

        @block.vector
        def _(dve):
            per_turn = 2 if full else 1
            per = per_turn + 3

            def turned(n, s):
                dve.wait_ge(xT_psum_ready, n + 1)
                src = ps[:, XT, 0:D].rearrange("p (c n) -> p c n", c=DC)
                if full:
                    for c in range(DC):
                        last = nc.vector.tensor_scalar(xT_whole[:, c, :], src[:, c, :], affine[:, 0, c:c + 1],
                                                       affine[:, 1, c:c + 1], ALU.mult, ALU.add)
                    s.link(last)
                    src = xT_whole[:]
                high, low = split(nc, xT[:, 0], xT[:, 1], src)
                s.link(high)
                low().then_inc(xT_ready, 1)

            def add_up(n):
                x = tile_of(g.x, n)
                dve.wait_ge(y_ready, n + 1)
                nc.vector.tensor_tensor(x, x, ps[:, Y, 0:D], ALU.add).then_inc(tile_done, 1)

            def step(n, base, ahead=True, first=False):
                s = Steps(dve, steps_done, base)
                dve.wait_ge(scores_ready, n + 1)
                sc = [(j, slice(h0, h0 + k), k, ps[:, SC + j, 0:k * NKEY].rearrange("p (h k) -> p h k", h=k))
                      for j, h0, k in HEAD_BANKS]
                for j, heads, k, bank in sc:
                    last = nc.vector.tensor_reduce(row_max[:, heads], bank, AX_X, ALU.max)
                s.link(last)
                if not first:
                    dve.wait_ge(pT_psum_ready, n)
                for j, heads, k, bank in sc:
                    last = nc.vector.tensor_tensor(probs[:, heads, :], bank,
                                                   row_max[:, heads].unsqueeze(2).broadcast_to([P, k, NKEY]), ALU.subtract)
                last.then_inc(centred, 1)
                if not first:
                    add_up(n - 1)
                dve.wait_ge(exp_done, n + 1)
                s.link(nc.vector.tensor_reduce(row_sum[:], probs[:], AX_X, ALU.add))
                s.link(nc.vector.reciprocal(row_sum[:], row_sum[:]))
                nc.vector.tensor_tensor(probs[:], probs[:], row_sum[:].unsqueeze(2).broadcast_to([P, NH, NKEY]), ALU.mult)\
                    .then_inc(probs_ready, 1)
                if ahead:
                    turned(n + 2, s)

            nc.vector.memset(xT_whole[0:1, 0, :], 1.0).then_inc(steps_done, 1)
            dve.wait_ge(steps_done, 1)
            nc.vector.tensor_copy(ones[:], xT_whole[0:1, 0, :]).then_inc(ones_ready, 1)
            dve.wait_ge(ones_ready, 1)
            start = 1 + 2 * per_turn
            norm.vector(dve, g.x, xn, "layer", centred_rows if full else xn_ready)
            if full:
                dve.wait_ge(centred_rows, TILES)
                norm2.vector(dve, xn, xn, "layer", xn_ready)
            for n in range(2):
                s = Steps(dve, steps_done, 1 + n * per_turn)
                turned(n, s)
                assert s.n == per_turn
            step(0, start, first=True)
            with dve.Fori(1, TILES - 2) as n:
                step(n, start + per * n)
            step(TILES - 2, start + per * (TILES - 2), ahead=False)
            step(TILES - 1, start + per * (TILES - 2) + 3, ahead=False)
            add_up(TILES - 1)
            dve.wait_ge(tile_done, TILES)


def fold_context(nc, g, dram, layer, scores_w, scores_b, values_w, bo, affine):
    dh = dram[f"L{layer}_xattn_WqT"].shape[0]
    inner = NH * dh
    scale = dh ** -0.5
    full = layer == 3
    BK = B * NKEY
    HPF = 512 // BK
    FILLS = [(h0, min(HPF, NH - h0)) for h0 in range(0, NH, HPF)]
    RING = 6
    VALUE_FILLS = B * NH // 2
    ps = g.ps
    scratch = nc.dram_tensor(f"values_w{layer}", (B, HK, D), F32).ap()
    with ExitStack() as ctx:
        st = Stage(nc, ctx, f"fc{layer}")
        ctxT = st.sb("ctxT", [P, DC, BK])
        wk, wv = st.sb("wk", [P, DC, inner]), st.sb("wv", [P, DC, inner])
        wqT, wo = st.sb("wqT", [dh, NH, D]), st.sb("wo", [dh, NH, D])
        bias = st.sb("bias", [dh, 3, NH])
        mask_in = st.sb("mask_in", [P, B, NKEY], I32 if layer == 2 else F32)
        mask = st.sb("mask", [P, B, NKEY])
        gate = st.sb("gate", [P, B, 2])
        bo_in = st.sb("bo_in", [1, D])
        row = st.sb("row", [1, B, 2 if full else HK])
        kT, vT = st.sb("kT", [dh, NH, BK]), st.sb("vT", [dh, NH, BK])
        vwo = st.sb("vwo", [NKEY, B, NH, D])
        small_loaded, k_loaded, v_loaded, q_loaded, o_loaded = (
            st.sem(n) for n in ("small_loaded", "k_loaded", "v_loaded", "q_loaded", "o_loaded"))
        stored, reloaded = st.sem("stored"), st.sem("reloaded")
        filled, emptied, steps_done, gate_done = st.sem("filled"), st.sem("emptied"), st.sem("steps_done"), st.sem("gate_done")
        smalls = 3 if full else 4
        block = st.block()

        @block.sync
        def _(sp):
            sp.dma_start(ctxT[:], dram["ctxT"].rearrange("(c p) k -> p c k", p=P)).then_inc(small_loaded, 16)
            sp.dma_start(wk[:], dram[f"L{layer}_xattn_Wk"].rearrange("(c p) n -> p c n", p=P)).then_inc(k_loaded, 16)
            sp.dma_start(bo_in[:], dram[f"L{layer}_xattn_bo"].rearrange("(a n) -> a n", a=1)).then_inc(small_loaded, 16)
            if full:
                sp.dma_start(affine[:], dram["L3_xattn_affine"]).then_inc(small_loaded, 16)
            else:
                sp.dma_start(bias[:], dram[f"L{layer}_xattn_bias"]).then_inc(small_loaded, 16)
                sp.dma_start(mask_in[:], dram[f"L{layer}_xattn_mask"].partition_broadcast(P)).then_inc(small_loaded, 16)
            sp.dma_start(wv[:], dram[f"L{layer}_xattn_Wv"].rearrange("(c p) n -> p c n", p=P)).then_inc(v_loaded, 16)
            sp.dma_start(wqT[:], dram[f"L{layer}_xattn_WqT"]).then_inc(q_loaded, 16)
            sp.dma_start(wo[:], dram[f"L{layer}_xattn_Wo"].rearrange("(h p) n -> p h n", p=dh)).then_inc(o_loaded, 16)
            before = len(FILLS) * (4 if full else 5)
            for b in range(B):
                sp.wait_ge(emptied, before + (b + 1) * NH // 2)
                sp.dma_start(scratch[b].rearrange("(h k) n -> k h n", h=NH), vwo[:, b]).then_inc(stored, 16)
                sp.wait_ge(stored, 16 * b + 16)
                sp.dma_start(values_w[:, b, 0:HKC - 1, :], scratch[b, 0:(HKC - 1) * P, :].rearrange("(c p) n -> p c n", p=P))\
                    .then_inc(reloaded, 16)
                sp.dma_start(values_w[0:HK_LAST, b, HKC - 1, :], scratch[b, (HKC - 1) * P:HK, :]).then_inc(reloaded, 16)
            sp.wait_ge(reloaded, 32 * B)

        @block.tensor
        def _(pe):
            count = 0

            def bank():
                nonlocal count
                if count >= RING:
                    pe.wait_ge(emptied, count - RING + 1)
                count += 1
                return ps[:, (count - 1) % RING, :]

            pe.wait_ge(small_loaded, 16 * smalls)
            for w, loaded in ((wk, k_loaded), (wv, v_loaded)):
                pe.wait_ge(loaded, 16)
                for h0, heads in FILLS:
                    out = bank()
                    for h in range(heads):
                        for c in range(DC):
                            last = nc.tensor.matmul(out[0:dh, h * BK:(h + 1) * BK], w[:, c, (h0 + h) * dh:(h0 + h + 1) * dh],
                                                    ctxT[:, c, :], start=(c == 0), stop=(c == DC - 1))
                    last.then_inc(filled, 1)
            pe.wait_ge(q_loaded, 16)
            pe.wait_ge(emptied, len(FILLS))
            for m in range(DC if full else DC + 1):
                for h0, heads in FILLS:
                    out = bank()
                    for h in range(heads):
                        left = wqT[:, h0 + h, m * P:(m + 1) * P] if m < DC else bias[:, 0, h0 + h:h0 + h + 1]
                        last = nc.tensor.matmul(out[0:left.shape[1], h * BK:(h + 1) * BK], left, kT[:, h0 + h, :],
                                                start=True, stop=True)
                    last.then_inc(filled, 1)
            pe.wait_ge(o_loaded, 16)
            pe.wait_ge(emptied, 2 * len(FILLS))
            for b in range(B):
                for h0 in range(0, NH, 2):
                    out = bank()
                    for h in range(2):
                        last = nc.tensor.matmul(out[0:NKEY, h * D:(h + 1) * D], vT[:, h0 + h, b * NKEY:(b + 1) * NKEY],
                                                wo[:, h0 + h, :], start=True, stop=True)
                    last.then_inc(filled, 1)

        @block.vector
        def _(dve):
            count = 0

            def bank(rows, cols):
                nonlocal count
                dve.wait_ge(filled, count + 1)
                count += 1
                return ps[0:rows, (count - 1) % RING, 0:cols]

            s = Steps(dve, steps_done)
            dve.wait_ge(small_loaded, 16 * smalls)
            at = GATE_XATTN + layer
            own_gate = g.gates[:, at:at + 1]
            for b in range(B):
                if full:
                    s.link(nc.vector.tensor_tensor(gate[:, b, 0:1], own_gate, g.gates[:, GATE_L3:GATE_L3 + 1], ALU.mult))
                elif layer == 1:
                    s.link(nc.vector.tensor_copy(gate[:, b, 0:1], own_gate))
                    s.link(nc.vector.tensor_scalar(mask[:, b, :], mask_in[:, b, :], -1e9, None, ALU.mult))
                else:
                    s.link(nc.vector.tensor_scalar(mask[:, b, :], mask_in[:, b, :], 0.0, None, ALU.not_equal))
                    s.link(nc.vector.tensor_reduce(gate[:, b, 1:2], mask[:, b, :], AX_X, ALU.max))
                    s.link(nc.vector.reciprocal(gate[:, b, 1:2], gate[:, b, 1:2]))
                    s.link(nc.vector.scalar_tensor_tensor(out=gate[:, b, 0:1], in0=gate[:, b, 1:2], scalar=0.0,
                                                          in1=own_gate, op0=ALU.mult, op1=ALU.add))
                    s.link(nc.vector.tensor_scalar(mask[:, b, :], mask_in[:, b, :], 0.0, MASKED, ALU.is_equal, ALU.mult))
                s.link(nc.vector.tensor_scalar(bo[0:1, b, :], bo_in[:], gate[0:1, b, 0:1], None, ALU.mult))
            for dst, which in ((kT, 1), (vT, 2)):
                for h0, heads in FILLS:
                    src = bank(dh, heads * BK).rearrange("p (h k) -> p h k", h=heads)
                    if full:
                        last = nc.vector.tensor_copy(dst[:, h0:h0 + heads, :], src)
                    else:
                        last = nc.vector.tensor_tensor(dst[:, h0:h0 + heads, :], src, bias[:, which, h0:h0 + heads].unsqueeze(2)
                                                       .broadcast_to([dh, heads, BK]), ALU.add)
                    last.then_inc(emptied, 1)
            for m in range(DC):
                for h0, heads in FILLS:
                    src = bank(P, heads * BK).rearrange("p (h b k) -> p b h k", h=heads, b=B)
                    cols = slice(h0 * NKEY, (h0 + heads) * NKEY)
                    high, low = ([scores_w[:, part, b, m, cols].rearrange("p (h k) -> p h k", h=heads) for b in range(B)]
                                 for part in range(2))
                    for b in range(B):
                        last = nc.vector.tensor_scalar(high[b], src[:, b], scale, None, ALU.mult)
                    s.link(last)
                    for b in range(B):
                        last = nc.vector.scalar_tensor_tensor(out=low[b], in0=src[:, b], scalar=scale, in1=high[b].bitcast(F32),
                                                              op0=ALU.mult, op1=ALU.subtract)
                    last.then_inc(emptied, 1)
            if not full:
                for h0, heads in FILLS:
                    src = bank(1, heads * BK).rearrange("p (h b k) -> p b h k", h=heads, b=B)
                    for b in range(B):
                        last = nc.vector.scalar_tensor_tensor(
                            out=row[0:1, b, h0 * NKEY:(h0 + heads) * NKEY].rearrange("p (h k) -> p h k", h=heads),
                            in0=src[:, b], scalar=scale, in1=mask[0:1, b, :].unsqueeze(1).broadcast_to([1, heads, NKEY]),
                            op0=ALU.mult, op1=ALU.add)
                    last.then_inc(emptied, 1)
            for b in range(B):
                for h0 in range(0, NH, 2):
                    nc.vector.tensor_scalar(vwo[:, b, h0:h0 + 2, :], bank(NKEY, 2 * D).rearrange("p (h n) -> p h n", h=2),
                                            gate[0:NKEY, b, 0:1], None, ALU.mult).then_inc(emptied, 1)
            if not full:
                dve.wait_ge(emptied, 5 * len(FILLS))
                high, low = split(nc, scores_b[0:1, 0], scores_b[0:1, 1], row[:])
                s.link(high)
                s.link(low())


def sign_network(nc, g, dram):
    F = dram["L0_ffn_k1"].shape[0]
    FC = F // P
    ps = g.ps
    with ExitStack() as ctx:
        st = Stage(nc, ctx, "sn")
        w0, w1, w2 = (st.sb(n, shape, F32R) for n, shape in (("w0", [P, DC, F]), ("w1", [P, FC, F]), ("w2", [P, FC, D])))
        scales = st.sb("scales", [P, 4])
        prep_sign_weights(nc, g, dram, w0, w1, w2, scales)
        norm = Norm(nc, g, st)
        xn, rows, xT = st.sb("xn", [P, TILES, D]), st.sb("rows", [P, TPG, D]), st.sb("xT", [P, 2, DC, GROUP], F32R)
        h1, h2 = st.sb("h1", [P, 2, FC, GROUP], F32R), st.sb("h2", [P, 2, FC, GROUP], F32R)
        whole = st.sb("whole", [P, 2, GROUP])
        whole_ready, high_ready, high_x = st.sem("whole_ready"), st.sem("high_ready"), st.sem("high_x")
        rows_ready = st.sem("rows_ready")
        xn_ready, xT_psum_ready, xT_ready, h_psum_ready, h_ready, y_ready, y_used = (st.sem(n) for n in (
            "xn_ready", "xT_psum_ready", "xT_ready", "h_psum_ready", "h_ready", "y_ready", "y_used"))
        H_BANKS, XT, Y = 4, 4, 6
        block = st.block()

        @block.tensor
        def _(pe):
            with pe.Fori(0, NG) as gr:
                for j in range(TPG):
                    pe.wait_ge(rows_ready, gr + 1)
                    if j > 0:
                        pe.wait_ge(xT_ready, gr * TPG + j)
                    for c in range(DC):
                        last = nc.tensor.transpose(ps[:, XT, c * P:(c + 1) * P], rows[:, j, c * P:(c + 1) * P], g.ident[:])
                    last.then_inc(xT_psum_ready, 1)
                pe.wait_ge(xT_ready, gr * TPG + TPG)
                for m in range(2 * FC):
                    if m >= H_BANKS:
                        pe.wait_ge(h_ready, gr * (2 * FC) + m - H_BANKS + 1)
                    if m == FC:
                        pe.wait_ge(h_ready, gr * (2 * FC) + FC)
                    w, src, n = (w0, xT, DC) if m < FC else (w1, h1, FC)
                    for c in range(n):
                        for part in range(2):
                            last = nc.tensor.matmul(ps[:, m % H_BANKS, :], w[:, c, (m % FC) * P:(m % FC + 1) * P],
                                                    src[:, part, c, :], start=(c + part == 0), stop=(c + part == n))
                    last.then_inc(h_psum_ready, 1)
                pe.wait_ge(h_ready, gr * (2 * FC) + 2 * FC)
                for j in range(TPG):
                    if j >= 2:
                        pe.wait_ge(y_used, gr * TPG + j - 1)
                    for c in range(FC):
                        for part in range(2):
                            last = nc.tensor.matmul(ps[:, Y + j % 2, 0:D], h2[:, part, c, j * P:(j + 1) * P], w2[:, c, :],
                                                    start=(c + part == 0), stop=(c + part == FC))
                    last.then_inc(y_ready, 1)

        @block.gpsimd
        def _(pool):
            norm.gpsimd(pool)

        @block.scalar
        def _(act):
            act.wait_ge(xn_ready, TILES)
            with act.Fori(0, NG) as gr:
                nc.scalar.activation(rows[:], xn[:, bass.ds(gr * TPG, TPG), :], ACT.Copy).then_inc(rows_ready, 1)
                for m in range(2 * FC):
                    dst = h1 if m < FC else h2
                    act.wait_ge(whole_ready, gr * (2 * FC) + m + 1)
                    nc.scalar.activation(dst[:, 0, m % FC, :], whole[:, m % 2, :], ACT.Copy).then_inc(high_ready, 1)

        @block.vector
        def _(dve):
            norm.vector(dve, g.x, xn, "layer", xn_ready)
            with dve.Fori(0, NG) as gr:
                for j in range(TPG):
                    n = gr * TPG + j
                    dve.wait_ge(xT_psum_ready, n + 1)
                    src = ps[:, XT, 0:D].rearrange("p (c n) -> p c n", c=DC)
                    nc.vector.tensor_copy(xT[:, 0, :, j * P:(j + 1) * P], src).then_inc(high_x, 1)
                    dve.wait_ge(high_x, n + 1)
                    nc.vector.tensor_tensor(xT[:, 1, :, j * P:(j + 1) * P], src, xT[:, 0, :, j * P:(j + 1) * P].bitcast(F32),
                                            ALU.subtract).then_inc(xT_ready, 1)
                for m in range(2 * FC):
                    k = gr * (2 * FC) + m
                    dve.wait_ge(h_psum_ready, k + 1)
                    dst, scale = (h1, scales[:, 0:1]) if m < FC else (h2, scales[:, 1:2])
                    nc.vector.tensor_scalar(whole[:, m % 2, :], ps[:, m % H_BANKS, :], scale, 0.0, ALU.mult, ALU.max)\
                        .then_inc(whole_ready, 1)
                    dve.wait_ge(high_ready, k + 1)
                    nc.vector.tensor_tensor(dst[:, 1, m % FC, :], whole[:, m % 2, :], dst[:, 0, m % FC, :].bitcast(F32),
                                            ALU.subtract).then_inc(h_ready, 1)
                for j in range(TPG):
                    n = gr * TPG + j
                    dve.wait_ge(y_ready, n + 1)
                    nc.vector.scalar_tensor_tensor(out=tile_of(g.x, n), in0=ps[:, Y + j % 2, 0:D], scalar=scales[:, 2:3],
                                                   in1=tile_of(g.x, n), op0=ALU.mult, op1=ALU.add).then_inc(y_used, 1)
                    dve.wait_ge(y_used, n + 1)


def prep_sign_weights(nc, g, dram, w0, w1, w2, scales):
    F = dram["L0_ffn_k1"].shape[0]
    FC = F // P
    with ExitStack() as ctx:
        st = Stage(nc, ctx, "sp")
        b0, b1, b2 = st.sb("b0", [P, 2 * DC, F], U8), st.sb("b1", [P, FC, F], U8), st.sb("b2", [P, FC, D], U8)
        loaded, made = st.sem("loaded"), st.sem("made")
        diff_ready = st.sem("diff_ready")
        block = st.block()

        @block.sync
        def _(sp):
            for n, (t, name) in enumerate(((b0, "L0_ffn_k0"), (b2, "L0_ffn_k2"), (b1, "L0_ffn_k1"))):
                sp.dma_start(t[:], dram[name].rearrange("(c p) n -> p c n", p=P)).then_inc(loaded, 16)
            for n in range(3):
                sp.dma_start(scales[:, n:n + 1], dram[f"L0_ffn_s{n}"].partition_broadcast(P)).then_inc(loaded, 16)

        @block.vector
        def _(dve):
            dve.wait_ge(loaded, 96)
            nc.vector.tensor_tensor(w0[:], b0[:, 0:DC, :], b0[:, DC:2 * DC, :], ALU.subtract).then_inc(diff_ready, 1)
            nc.vector.tensor_scalar(w2[:], b2[:], 4.0, -2.0, ALU.mult, ALU.add)
            nc.vector.tensor_scalar(w1[:], b1[:], 8.0, -4.0, ALU.mult, ALU.add)
            nc.vector.tensor_tensor(scales[:, 2:3], scales[:, 2:3], g.gates[:, GATE_FFN:GATE_FFN + 1], ALU.mult)\
                .then_inc(made, 1)


def mixture(nc, g, dram, layer, src, acc):
    E = 8
    K3 = 3 * E
    weights = dram[f"L{layer}_moe_w"]
    selector = dram[f"L{layer}_moe_sel"]
    chunks = weights.shape[0]
    inner_norm = layer == 3
    ps = g.ps
    with ExitStack() as outer:
        combT = Stage(nc, outer, f"mx{layer}").sb("combT", [K3, B * S], BF16)
        xT_all = Stage(nc, outer, f"mx{layer}").sb("xT_all", [P, 2, DC, B * S], F32R)
        with ExitStack() as ctx:
            st = Stage(nc, ctx, f"rt{layer}")
            norm = Norm(nc, g, st)
            xn, xT = st.sb("xn", [P, TILES, D]), st.sb("xT", [P, 2, DC, P])
            router, gain = st.sb("router", [P, DC, E]), st.sb("gain", [P, DC])
            bias, iota = st.sb("bias", [P, E]), st.sb("iota", [P, E])
            logits, top, expd, shift, comb, other, rest = (st.sb(n, [P, TILES, E]) for n in (
                "logits", "top", "expd", "shift", "comb", "other", "rest"))
            w2, where, total = st.sb("w2", [P, TILES, 2]), st.sb("where", [P, TILES, 2]), st.sb("total", [P, TILES])
            index = st.sb("index", [P, TILES, E], U32)
            parts = st.sb("parts", [P, TILES, K3], BF16)
            loaded, steps_done, high_ready = st.sem("loaded"), st.sem("steps_done"), st.sem("high_ready")
            xn_ready, xT_psum_ready, xT_ready, low_ready, logits_ready, shifted, exp_done, parts_ready, \
                combT_psum_ready, combT_ready, cleared = (st.sem(n) for n in (
                    "xn_ready", "xT_psum_ready", "xT_ready", "low_ready", "logits_ready", "shifted", "exp_done",
                    "parts_ready", "combT_psum_ready", "combT_ready", "cleared"))
            XT, LG, CT = 0, 2, 3
            combT_psum = ps[0:K3, CT:CT + 2, :].rearrange("p b n -> p (b n)").bitcast(BF16)
            loads = 4 if layer == 1 else 3
            chosen = 2 if layer == 1 else E
            block = st.block()

            @block.sync
            def _(sp):
                sp.dma_start(router[:], dram[f"L{layer}_moe_router"].rearrange("(c p) e -> p c e", p=P)).then_inc(loaded, 16)
                sp.dma_start(iota[:], dram["iota8"].partition_broadcast(P)).then_inc(loaded, 16)
                if layer == 1:
                    sp.dma_start(bias[:], dram["L1_ffn_bs"].partition_broadcast(P)).then_inc(loaded, 16)
                sp.dma_start(gain[:], dram["L3_ffn_ln2"]).then_inc(loaded, 16)

            @block.tensor
            def _(pe):
                def turn(t):
                    pe.wait_ge(xn_ready, t + 1)
                    if t >= 2:
                        pe.wait_ge(xT_ready, t - 1)
                    for c in range(DC):
                        last = nc.tensor.transpose(ps[:, XT + t % 2, c * P:(c + 1) * P], xn[:, t, c * P:(c + 1) * P], g.ident[:])
                    last.then_inc(xT_psum_ready, 1)

                pe.wait_ge(loaded, 16 * loads)
                turn(0)
                for t in range(TILES):
                    if t < TILES - 1:
                        turn(t + 1)
                    pe.wait_ge(xT_ready, t + 1)
                    for c in range(DC):
                        last = nc.tensor.matmul(ps[:, LG, t * E:(t + 1) * E], xT[:, t % 2, c, :], router[:, c, :],
                                                start=(c == 0), stop=(c == DC - 1))
                    last.then_inc(logits_ready, 1)
                pe.wait_ge(parts_ready, 1)
                for t in range(TILES):
                    last = nc.tensor.transpose(combT_psum[:, t * P:(t + 1) * P], parts[:, t, :], g.identb[:])
                last.then_inc(combT_psum_ready, 1)

            @block.gpsimd
            def _(pool):
                norm.gpsimd(pool)
                for t in range(TILES):
                    pool.wait_ge(xT_ready, t + 1)
                    nc.gpsimd.tensor_copy(xT_all[:, 0, :, t * P:(t + 1) * P], xT[:, t % 2]).then_inc(high_ready, 1)
                if not inner_norm:
                    nc.gpsimd.memset(acc[:], 0.0).then_inc(cleared, 1)

            @block.scalar
            def _(act):
                for t in range(TILES):
                    act.wait_ge(xT_psum_ready, t + 1)
                    if t >= 2:
                        act.wait_ge(logits_ready, t - 1)
                        act.wait_ge(low_ready, t - 1)
                    for c in range(DC):
                        scale = gain[:, c:c + 1] if inner_norm else 1.0
                        last = nc.scalar.activation(xT[:, t % 2, c, :], ps[:, XT + t % 2, c * P:(c + 1) * P], ACT.Copy,
                                                    scale=scale)
                    last.then_inc(xT_ready, 1)
                act.wait_ge(shifted, 1)
                nc.scalar.activation(expd[:, :, 0:chosen], shift[:, :, 0:chosen], ACT.Exp).then_inc(exp_done, 1)

            @block.vector
            def _(dve):
                def wide(column, n):
                    return column.unsqueeze(2).broadcast_to([P, TILES, n])

                s = Steps(dve, steps_done)
                dve.wait_ge(loaded, 16 * loads)
                norm.vector(dve, src, xn, "rms" if inner_norm else "layer", xn_ready)
                for t in range(TILES):
                    dve.wait_ge(high_ready, t + 1)
                    nc.vector.tensor_tensor(xT_all[:, 1, :, t * P:(t + 1) * P], xT[:, t % 2],
                                            xT_all[:, 0, :, t * P:(t + 1) * P].bitcast(F32), ALU.subtract).then_inc(low_ready, 1)
                dve.wait_ge(logits_ready, TILES)
                logits_psum = ps[:, LG, 0:TILES * E].rearrange("p (t e) -> p t e", e=E)
                if layer == 1:
                    s.link(nc.vector.tensor_tensor(logits[:], logits_psum, bias[:].unsqueeze(1).broadcast_to([P, TILES, E]),
                                                   ALU.add))
                else:
                    s.link(nc.vector.tensor_copy(logits[:], logits_psum))
                    s.link(nc.vector.tensor_reduce(total[:], logits[:], AX_X, ALU.max))
                    nc.vector.tensor_tensor(shift[:], logits[:], wide(total[:], E), ALU.subtract).then_inc(shifted, 1)
                    dve.wait_ge(exp_done, 1)
                    s.link(nc.vector.tensor_reduce(total[:], expd[:], AX_X, ALU.add))
                    s.link(nc.vector.reciprocal(total[:], total[:]))
                    s.link(nc.vector.tensor_tensor(logits[:], expd[:], wide(total[:], E), ALU.mult))
                for t in range(TILES):
                    last = nc.vector.max(top[:, t, :], logits[:, t, :])
                s.link(last)
                for t in range(TILES):
                    last = nc.vector.max_index(index[:, t, :], top[:, t, :], logits[:, t, :])
                s.link(last)
                if layer == 1:
                    nc.vector.tensor_tensor(shift[:, :, 0:2], top[:, :, 0:2], wide(top[:, :, 0], 2), ALU.subtract)\
                        .then_inc(shifted, 1)
                    dve.wait_ge(exp_done, 1)
                    s.link(nc.vector.tensor_tensor(total[:], expd[:, :, 0], expd[:, :, 1], ALU.add))
                    pair = expd
                else:
                    s.link(nc.vector.tensor_tensor(total[:], top[:, :, 0], top[:, :, 1], ALU.add))
                    pair = top
                s.link(nc.vector.reciprocal(total[:], total[:]))
                s.link(nc.vector.tensor_tensor(w2[:], pair[:, :, 0:2], wide(total[:], 2), ALU.mult))
                s.link(nc.vector.tensor_copy(where[:], index[:, :, 0:2]))
                for n, one in enumerate((comb, other)):
                    s.link(nc.vector.tensor_tensor(one[:], iota[:].unsqueeze(1).broadcast_to([P, TILES, E]),
                                                   wide(where[:, :, n], E), ALU.is_equal))
                    s.link(nc.vector.tensor_tensor(one[:], one[:], wide(w2[:, :, n], E), ALU.mult))
                s.link(nc.vector.tensor_tensor(comb[:], comb[:], other[:], ALU.add))
                s.link(nc.vector.tensor_copy(parts[:, :, 0:E], comb[:]))
                s.link(nc.vector.tensor_tensor(rest[:], comb[:], parts[:, :, 0:E], ALU.subtract))
                s.link(nc.vector.tensor_copy(parts[:, :, E:2 * E], rest[:]))
                nc.vector.tensor_tensor(parts[:, :, 2 * E:K3], rest[:], parts[:, :, E:2 * E], ALU.subtract).then_inc(parts_ready, 1)
                dve.wait_ge(combT_psum_ready, 1)
                nc.vector.tensor_copy(combT[:], combT_psum).then_inc(combT_ready, 1)

        with ExitStack() as ctx:
            st = Stage(nc, ctx, f"ex{layer}")
            slots = st.sb("slots", [P, 2, 3 * D])
            parts = st.sb("parts", [P, 2, 2, 3 * D], F32R)
            sels = st.sb("sels", [K3, 2, P], BF16)
            act_out, h = st.sb("act_out", [P, 2, GROUP]), st.sb("h", [P, 2, GROUP])
            h_parts = st.sb("h_parts", [P, 2, 2, GROUP], F32R)
            high_split, weights_split, whole_ready, h_high_ready, waits_alone = (
                st.sem(n) for n in ("high_split", "weights_split", "whole_ready", "h_high_ready", "waits_alone"))
            slot_loaded = [st.sem(f"slot_loaded{n}") for n in range(2)]
            chunk_used, gate_up_ready, silu_done, gated, h_ready, y_ready, y_used = (st.sem(n) for n in (
                "chunk_used", "gate_up_ready", "silu_done", "gated", "h_ready", "y_ready", "y_used"))
            GATE, UP, SPREAD, Y = 0, 2, 4, 6
            tail = 1 if chunks % 2 else 2
            pairs = (chunks - tail) // 2
            block = st.block()

            def load(sp, c, slot):
                sp.dma_start(slots[:, slot, :], weights[bass.ds(c, 1)].rearrange("a p n -> p (a n)"))\
                    .then_inc(slot_loaded[slot], 16)
                sp.dma_start(sels[:, slot, :], selector[:, bass.ds(c * P, P)]).then_inc(slot_loaded[slot], 16)

            @block.sync
            def _(sp):
                for slot in range(2):
                    load(sp, slot, slot)
                with sp.Fori(1, pairs) as p:
                    for slot in range(2):
                        sp.wait_ge(chunk_used, 2 * p + slot - 1)
                        load(sp, 2 * p + slot, slot)
                for c in range(2 * pairs, chunks):
                    sp.wait_ge(chunk_used, c - 1)
                    load(sp, c, c % 2)

            @block.tensor
            def _(pe):
                def gate_up(c, slot, gr):
                    i = gr % 2
                    if gr == 0:
                        pe.wait_ge(slot_loaded[slot], 32 * (c // 2) + 32)
                        pe.wait_ge(weights_split, c + 1)
                    tokens = slice(gr * GROUP, (gr + 1) * GROUP)
                    for bank, w in ((GATE + i, 0), (UP + i, 1)):
                        for k in range(DC):
                            for left, right in PASSES:
                                nc.tensor.matmul(ps[:, bank, :], parts[:, slot, left, (DC * w + k) * P:(DC * w + k + 1) * P],
                                                 xT_all[:, right, k, tokens], start=(k + left + right == 0),
                                                 stop=((k, left, right) == (DC - 1, 0, 1)))
                    nc.tensor.matmul(ps[:, SPREAD + i, :], sels[:, slot, :], combT[:, tokens], start=True, stop=True)\
                        .then_inc(gate_up_ready, 1)

                def down(c, slot, gr, first=False):
                    unit = 4 * c + gr
                    pe.wait_ge(h_ready, unit + 1)
                    if not first:
                        pe.wait_ge(y_used, unit)
                    for j in range(TPG):
                        for left, right in PASSES:
                            last = nc.tensor.matmul(ps[:, Y + j // 2, (j % 2) * D:(j % 2 + 1) * D],
                                                    h_parts[:, gr % 2, left, j * P:(j + 1) * P],
                                                    parts[:, slot, right, 2 * DC * P:],
                                                    start=(left + right == 0), stop=(right == 1))
                    last.then_inc(y_ready, 1)

                def chunk(c, slot, more, first=False):
                    for gr in range(NG):
                        if gr < NG - 1:
                            gate_up(c, slot, gr + 1)
                        elif more:
                            gate_up(c + 1, 1 - slot, 0)
                        down(c, slot, gr, first and gr == 0)

                gate_up(0, 0, 0)
                chunk(0, 0, True, first=True)
                chunk(1, 1, True)
                with pe.Fori(1, pairs) as p:
                    chunk(2 * p, 0, True)
                    chunk(2 * p + 1, 1, True)
                for c in range(2 * pairs, chunks):
                    chunk(c, c % 2, c < chunks - 1)

            def over_chunks(eng, chunk):
                chunk(0, None)
                with eng.Fori(0, (chunks - 2) // 2) as p:
                    chunk(2 * p + 1, 0)
                    chunk(2 * p + 2, 1)
                for c in range(2 * ((chunks - 2) // 2) + 1, chunks):
                    chunk(c, (c + 1) % 2 if c + 1 < chunks else None)

            @block.gpsimd
            def _(pool):
                def low_weights(c, slot):
                    pool.wait_ge(high_split, c + 1)
                    nc.gpsimd.tensor_tensor(parts[:, slot, 1, :], slots[:, slot, :], parts[:, slot, 0, :].bitcast(F32),
                                            ALU.subtract).then_inc(weights_split, 1)

                def chunk(c, ahead):
                    for gr in range(NG):
                        pool.wait_ge(h_high_ready, NG * c + gr + 1)
                        nc.gpsimd.tensor_tensor(h_parts[:, gr % 2, 1, :], h[:, gr % 2, :], h_parts[:, gr % 2, 0, :].bitcast(F32),
                                                ALU.subtract).then_inc(h_ready, 1)
                        if gr == 1 and ahead is not None:
                            low_weights(c + 1, ahead)

                for slot in range(2):
                    low_weights(slot, slot)
                over_chunks(pool, chunk)

            @block.scalar
            def _(act):
                def high_weights(c, slot, reused):
                    act.wait_ge(slot_loaded[slot], 32 * (c // 2) + 32)
                    if reused:
                        act.wait_ge(chunk_used, c - 1)
                    nc.scalar.activation(parts[:, slot, 0, :], slots[:, slot, :], ACT.Copy).then_inc(high_split, 1)

                def chunk(c, ahead):
                    for gr in range(NG):
                        act.wait_ge(gate_up_ready, NG * c + gr + 1)
                        nc.scalar.activation(act_out[:, gr % 2, :], ps[:, GATE + gr % 2, :], ACT.Silu).then_inc(silu_done, 1)
                        if gr == 1 and ahead is not None:
                            high_weights(c + 1, ahead, True)

                for slot in range(2):
                    high_weights(slot, slot, False)
                over_chunks(act, chunk)

            @block.vector
            def _(dve):
                def hidden(u, i):
                    dve.wait_ge(silu_done, u + 1)
                    nc.vector.tensor_tensor(act_out[:, i, :], act_out[:, i, :], ps[:, UP + i, :], ALU.mult).then_inc(gated, 1)
                    dve.wait_ge(gated, u + 1)
                    nc.vector.tensor_tensor(h[:, i, :], act_out[:, i, :], ps[:, SPREAD + i, :], ALU.mult).then_inc(whole_ready, 1)
                    dve.wait_ge(whole_ready, u + 1)
                    nc.vector.tensor_copy(h_parts[:, i, 0, :], h[:, i, :]).then_inc(h_high_ready, 1)

                def add_up(u, gr):
                    dve.wait_ge(y_ready, u + 1)
                    part = acc[:, gr * TPG:(gr + 1) * TPG, :].rearrange("p t n -> p (t n)")
                    nc.vector.tensor_tensor(part, part, ps[:, Y:Y + 2, :].rearrange("p b n -> p (b n)"), ALU.add)\
                        .then_inc(y_used, 1)
                    if gr == NG - 1:
                        dve.sem_inc(chunk_used, 1)

                hidden(0, 0)
                with dve.Fori(0, chunks - 1) as c:
                    for gr in range(NG):
                        hidden(NG * c + gr + 1, (gr + 1) % 2)
                        add_up(NG * c + gr, gr)
                last = NG * (chunks - 1)
                for gr in range(NG):
                    if gr < NG - 1:
                        hidden(last + gr + 1, (gr + 1) % 2)
                    add_up(last + gr, gr)
                dve.wait_ge(y_used, chunks * NG)


def expert_layer_1(nc, g, dram):
    with ExitStack() as ctx:
        st = Stage(nc, ctx, "m1")
        acc = st.sb("acc", [P, TILES, D])
        mixture(nc, g, dram, 1, g.x, acc)
        add_gated(nc, g, acc, 1)


def add_gated(nc, g, acc, layer):
    with ExitStack() as ctx:
        st = Stage(nc, ctx, f"ag{layer}")
        added = st.sem("added")
        block = st.block()

        @block.vector
        def _(dve):
            at = GATE_FFN + layer
            nc.vector.scalar_tensor_tensor(out=g.x[:], in0=acc[:], scalar=g.gates[:, at:at + 1], in1=g.x[:],
                                           op0=ALU.mult, op1=ALU.add).then_inc(added, 1)
            dve.wait_ge(added, 1)


def product_key_experts(nc, g, dram):
    HEADS, KEYS, TOP = 8, 64, 16
    EXPERTS = KEYS * KEYS
    EC = EXPERTS // P
    SIDES = 2 * HEADS
    BLK = 1024
    BLOCKS = EXPERTS // BLK
    UNITS = [(head, q) for head in range(HEADS) for q in range(BLOCKS)]
    NU = len(UNITS)
    OWN = BLOCKS - 1
    POOL_ADDS = (HEADS - 1) * (BLOCKS - 1)
    KEPT = 3
    HB = EXPERTS // 512
    HIDDEN = {2 * k + 1: k for k in range(HB)}
    AHEAD_TURN, AHEAD_SIM = 18, 22
    ps = g.ps
    with ExitStack() as ctx:
        st = Stage(nc, ctx, "pk")
        sim_w = st.sb("sim_w", [P, DC, SIDES * KEYS])
        spread = st.sb("spread", [P, EXPERTS], F32R)
        fold_product_keys(nc, g, dram, sim_w, spread)
        downT, up = st.sb("downT", [P, DC, EXPERTS]), st.sb("up", [P, EC, D])
        gain = st.sb("gain", [P, DC])
        norm, norm2 = Norm(nc, g, st), Norm(nc, g, st, "2")
        xn, row, xT = st.sb("xn", [P, TILES, D]), st.sb("row", [P, D]), st.sb("xT", [P, DC, P])
        sims, rest = st.sb("sims", [P, SIDES, KEYS]), st.sb("rest", [P, SIDES, KEYS])
        simsT = st.sb("simsT", [P, 2, HEADS, P], F32R)
        best = st.sb("best", [P, SIDES, TOP])
        pairs = st.sb("pairs", [P, HEADS, TOP * TOP])
        top = st.sb("top", [P, HEADS, TOP])
        least = st.sb("least", [P, HEADS])
        sums, kept = st.sb("sums", [P, 2, BLK]), st.sb("kept", [P, KEPT, BLK])
        weight, hidden = st.sb("weight", [P, EXPERTS]), st.sb("hidden", [P, EXPERTS])
        hT = st.sb("hT", [P, 2, 4 * P])
        loaded, steps_done, alone, centred = (st.sem(n) for n in ("loaded", "steps_done", "alone", "centred"))
        row_ready = st.sem("row_ready")
        xn_ready, xT_psum_ready, xT_ready, sims_psum_ready, sims_ready, simsT_psum_ready, simsT_high_ready, simsT_ready, \
            sums_psum_ready, sums_ready, kept_ready, pool_added, hid_psum_ready, gelu_done, hidden_ready, hT_psum_ready, hT_ready, \
            y_ready, tile_done = (st.sem(n) for n in (
                "xn_ready", "xT_psum_ready", "xT_ready", "sims_psum_ready", "sims_ready", "simsT_psum_ready",
                "simsT_high_ready", "simsT_ready", "sums_psum_ready", "sums_ready", "kept_ready", "pool_added", "hid_psum_ready",
                "gelu_done", "hidden_ready", "hT_psum_ready", "hT_ready", "y_ready", "tile_done"))
        SUMS, WORK, XT, Y = 0, 4, 6, 7
        block = st.block()

        def two_banks(first):
            return ps[:, first:first + 2, :].rearrange("p b n -> p (b n)")

        @block.sync
        def _(sp):
            sp.dma_start(gain[:], dram["L2_ffn_norm"]).then_inc(loaded, 16)
            sp.dma_start(downT[:], dram["L2_ffn_downT"].rearrange("(c p) e -> p c e", p=P)).then_inc(loaded, 16)
            sp.dma_start(up[:], dram["L2_ffn_expert_up"].rearrange("(c p) n -> p c n", p=P)).then_inc(loaded, 16)

        @block.tensor
        def _(pe):
            def turn_x(t):
                pe.wait_ge(row_ready, t + 1)
                for c in range(DC):
                    last = nc.tensor.transpose(ps[:, XT, c * P:(c + 1) * P], row[:, c * P:(c + 1) * P], g.ident[:])
                last.then_inc(xT_psum_ready, 1)

            def similarities(t):
                pe.wait_ge(xT_ready, t + 1)
                for j in range(2):
                    for c in range(DC):
                        last = nc.tensor.matmul(ps[:, WORK + j, :], xT[:, c, :], sim_w[:, c, j * 512:(j + 1) * 512],
                                                start=(c == 0), stop=(c == DC - 1))
                last.then_inc(sims_psum_ready, 1)

            def turn_similarities(t):
                pe.wait_ge(sims_ready, t + 1)
                for head in range(HEADS):
                    last = nc.tensor.transpose(ps[:, WORK + head // 4, (head % 4) * P:(head % 4 + 1) * P],
                                               sims[:, 2 * head:2 * head + 2, :].rearrange("p s k -> p (s k)"), g.ident[:])
                last.then_inc(simsT_psum_ready, 1)

            def hidden_units(t, k):
                if k >= 2:
                    pe.wait_ge(gelu_done, HB * t + k - 1)
                for c in range(DC):
                    last = nc.tensor.matmul(ps[:, WORK + k % 2, :], xT[:, c, :], downT[:, c, k * 512:(k + 1) * 512],
                                            start=(c == 0), stop=(c == DC - 1))
                last.then_inc(hid_psum_ready, 1)

            def project(t):
                def turn(k):
                    pe.wait_ge(hidden_ready, HB * t + k + 1)
                    if k >= 2:
                        pe.wait_ge(hT_ready, HB * t + k - 1)
                    first = 4 * (HB - 1 - k)
                    for i in range(4):
                        last = nc.tensor.transpose(ps[:, WORK + k % 2, i * P:(i + 1) * P],
                                                   hidden[:, (first + i) * P:(first + i + 1) * P], g.ident[:])
                    last.then_inc(hT_psum_ready, 1)

                turn(0)
                for k in range(HB):
                    if k < HB - 1:
                        turn(k + 1)
                    pe.wait_ge(hT_ready, HB * t + k + 1)
                    for i in range(4):
                        last = nc.tensor.matmul(ps[:, Y, 0:D], hT[:, k % 2, i * P:(i + 1) * P], up[:, 4 * (HB - 1 - k) + i, :],
                                                start=(k == 0 and i == 0), stop=(k == HB - 1 and i == 3))
                last.then_inc(y_ready, 1)

            def step(t, ahead=True):
                pe.wait_ge(simsT_ready, t + 1)
                for u, (head, q) in enumerate(UNITS):
                    if u >= 2:
                        pe.wait_ge(sums_ready, NU * t + u - 1)
                    for j in range(2):
                        for part in range(2):
                            last = nc.tensor.matmul(ps[:, SUMS + 2 * (u % 2) + j, :], simsT[:, part, head, :],
                                                    spread[:, q * BLK + j * 512:q * BLK + (j + 1) * 512],
                                                    start=(part == 0), stop=(part == 1))
                    last.then_inc(sums_psum_ready, 1)
                    if u in HIDDEN:
                        hidden_units(t, HIDDEN[u])
                    if ahead and u == AHEAD_TURN:
                        turn_x(t + 1)
                    if ahead and u == AHEAD_SIM:
                        pe.wait_ge(gelu_done, HB * t + HB)
                        similarities(t + 1)
                if ahead:
                    turn_similarities(t + 1)
                    pe.wait_ge(simsT_ready, t + 2)
                project(t)

            turn_x(0)
            similarities(0)
            turn_similarities(0)
            pe.wait_ge(loaded, 48)
            with pe.Fori(0, TILES - 1) as t:
                step(t)
            step(TILES - 1, ahead=False)

        @block.gpsimd
        def _(pool):
            def step(t, ahead=True):
                added = 0
                for u, (head, q) in enumerate(UNITS):
                    if head > 0 and q != OWN:
                        part = weight[:, q * BLK:(q + 1) * BLK]
                        pool.wait_ge(kept_ready, NU * t + u + 1)
                        if head > 1 or q > 0:
                            pool.wait_ge(pool_added, POOL_ADDS * t + added)
                        nc.gpsimd.tensor_tensor(part, part, kept[:, u % KEPT, :], ALU.add).then_inc(pool_added, 1)
                        added += 1

            norm.gpsimd(pool)
            norm2.gpsimd(pool)
            with pool.Fori(0, TILES - 1) as t:
                step(t)
            step(TILES - 1, ahead=False)

        @block.scalar
        def _(act):
            def similarities(t):
                act.wait_ge(sims_psum_ready, t + 1)
                nc.scalar.activation(sims[:].rearrange("p s k -> p (s k)"), two_banks(WORK), ACT.Copy).then_inc(sims_ready, 1)

            def take_row(t):
                nc.scalar.activation(row[:], tile_of(xn, t), ACT.Copy).then_inc(row_ready, 1)

            def turned_similarities(t):
                act.wait_ge(simsT_psum_ready, t + 1)
                nc.scalar.activation(simsT[:, 0].rearrange("p h n -> p (h n)"), two_banks(WORK), ACT.Copy)\
                    .then_inc(simsT_high_ready, 1)

            def step(t, ahead=True):
                for u in range(NU):
                    act.wait_ge(sums_psum_ready, NU * t + u + 1)
                    if u >= 2:
                        act.wait_ge(kept_ready, NU * t + u - 1)
                    nc.scalar.activation(sums[:, u % 2, :], two_banks(SUMS + 2 * (u % 2)), ACT.Copy).then_inc(sums_ready, 1)
                    if u in HIDDEN:
                        k = HIDDEN[u]
                        act.wait_ge(hid_psum_ready, HB * t + k + 1)
                        nc.scalar.activation(hidden[:, k * 512:(k + 1) * 512], ps[:, WORK + k % 2, :], ACT.Gelu)\
                            .then_inc(gelu_done, 1)
                    if ahead and u == AHEAD_TURN - 2:
                        act.wait_ge(xT_psum_ready, t + 1)
                        take_row(t + 1)
                    if ahead and u == AHEAD_SIM + 1:
                        similarities(t + 1)
                if ahead:
                    turned_similarities(t + 1)
                for k in range(HB):
                    act.wait_ge(hT_psum_ready, HB * t + k + 1)
                    nc.scalar.activation(hT[:, k % 2, :], ps[:, WORK + k % 2, :], ACT.Copy).then_inc(hT_ready, 1)

            act.wait_ge(xn_ready, TILES)
            take_row(0)
            similarities(0)
            turned_similarities(0)
            with act.Fori(0, TILES - 1) as t:
                step(t)
            step(TILES - 1, ahead=False)

        @block.vector
        def _(dve):
            top_links = 8
            own_links = HEADS - 1
            per = top_links + own_links

            def turned(t):
                dve.wait_ge(xT_psum_ready, t + 1)
                for c in range(DC):
                    last = nc.vector.tensor_scalar(xT[:, c, :], ps[:, XT, c * P:(c + 1) * P], gain[:, c:c + 1], None, ALU.mult)
                last.then_inc(xT_ready, 1)

            def low_part(t):
                dve.wait_ge(sims_ready, t + 1)
                dve.wait_ge(simsT_high_ready, t + 1)
                nc.vector.tensor_tensor(simsT[:, 1].rearrange("p h n -> p (h n)"), two_banks(WORK),
                                        simsT[:, 0].rearrange("p h n -> p (h n)").bitcast(F32), ALU.subtract)\
                    .then_inc(simsT_ready, 1)

            def bounds(t, s):
                for k in range(SIDES):
                    last = nc.vector.max(best[:, k, 0:8], sims[:, k, :])
                s.link(last, alone)
                for k in range(SIDES):
                    last = nc.vector.match_replace(rest[:, k, :], best[:, k, 0:8], sims[:, k, :], MASKED)
                s.link(last, alone)
                for k in range(SIDES):
                    last = nc.vector.max(best[:, k, 8:16], rest[:, k, :])
                s.link(last)
                for head in range(HEADS):
                    last = nc.vector.tensor_tensor(pairs[:, head, :].rearrange("p (i j) -> p i j", i=TOP),
                                                   best[:, 2 * head, :].unsqueeze(2).broadcast_to([P, TOP, TOP]),
                                                   best[:, 2 * head + 1, :].unsqueeze(1).broadcast_to([P, TOP, TOP]), ALU.add)
                s.link(last, alone)
                for head in range(HEADS):
                    last = nc.vector.max(top[:, head, 0:8], pairs[:, head, :])
                s.link(last, alone)
                for head in range(HEADS):
                    last = nc.vector.match_replace(pairs[:, head, :], top[:, head, 0:8], pairs[:, head, :], MASKED)
                s.link(last, alone)
                for head in range(HEADS):
                    last = nc.vector.max(top[:, head, 8:16], pairs[:, head, :])
                s.link(last)
                s.link(nc.vector.tensor_scalar(least[:], top[:, :, TOP - 1], 0.0, 1.0 - 2.0 ** -22, ALU.max, ALU.mult))

            def step(t, base, ahead=True):
                s = Steps(dve, steps_done, base)
                added = 0
                adds_before = {}
                for u, (head, q) in enumerate(UNITS):
                    adds_before[u] = added
                    added += head > 0 and q != OWN
                for u, (head, q) in enumerate(UNITS):
                    dve.wait_ge(sums_ready, NU * t + u + 1)
                    part = weight[:, q * BLK:(q + 1) * BLK]
                    if head > 0 and u >= KEPT and UNITS[u - KEPT][0] > 0 and UNITS[u - KEPT][1] != OWN:
                        dve.wait_ge(pool_added, POOL_ADDS * t + adds_before[u - KEPT] + 1)
                    dst = part if head == 0 else kept[:, u % KEPT, :]
                    unit = sums[:, u % 2, :]
                    nc.vector.scalar_tensor_tensor(out=dst, in0=unit, scalar=least[:, head:head + 1], in1=unit,
                                                   op0=ALU.is_ge, op1=ALU.mult).then_inc(kept_ready, 1)
                    if head > 0 and q == OWN:
                        dve.wait_ge(kept_ready, NU * t + u + 1)
                        s.link(nc.vector.tensor_tensor(part, part, kept[:, u % KEPT, :], ALU.add))
                    if ahead and u == AHEAD_TURN:
                        turned(t + 1)
                dve.wait_ge(gelu_done, HB * t + HB)
                for k in reversed(range(HB)):
                    if k == HB - BLK // 512 - 1:
                        if ahead:
                            low_part(t + 1)
                        dve.wait_ge(pool_added, POOL_ADDS * t + POOL_ADDS)
                    part = slice(k * 512, (k + 1) * 512)
                    nc.vector.tensor_tensor(hidden[:, part], hidden[:, part], weight[:, part], ALU.mult).then_inc(hidden_ready, 1)
                if ahead:
                    bounds(t + 1, s)
                x = tile_of(g.x, t)
                dve.wait_ge(y_ready, t + 1)
                nc.vector.scalar_tensor_tensor(out=x, in0=ps[:, Y, 0:D], scalar=g.gates[:, GATE_FFN + 2:GATE_FFN + 3], in1=x,
                                               op0=ALU.mult, op1=ALU.add).then_inc(tile_done, 1)

            s = Steps(dve, steps_done)
            norm.vector(dve, g.x, xn, "layer", centred)
            dve.wait_ge(centred, TILES)
            norm2.vector(dve, xn, xn, "rms", xn_ready)
            dve.wait_ge(loaded, 48)
            turned(0)
            low_part(0)
            bounds(0, s)
            assert s.n == top_links
            with dve.Fori(0, TILES - 1) as t:
                step(t, top_links + per * t)
            step(TILES - 1, top_links + per * (TILES - 1), ahead=False)
            dve.wait_ge(tile_done, TILES)


def fold_product_keys(nc, g, dram, sim_w, spread):
    SIDES, KEYS = dram["L2_ffn_keysT"].shape[1:]
    ps = g.ps
    with ExitStack() as ctx:
        st = Stage(nc, ctx, "fk")
        wqT, keysT = st.sb("wqT", [P, SIDES, D]), st.sb("keysT", [P, SIDES, KEYS])
        loaded, psum_ready, made, spread_made = (st.sem(n) for n in ("loaded", "psum_ready", "made", "spread_made"))
        block = st.block()

        @block.sync
        def _(sp):
            sp.dma_start(wqT[:], dram["L2_ffn_wqT"]).then_inc(loaded, 16)
            sp.dma_start(keysT[:], dram["L2_ffn_keysT"]).then_inc(loaded, 16)

        @block.tensor
        def _(pe):
            pe.wait_ge(loaded, 32)
            for c in range(DC):
                for k in range(SIDES):
                    last = nc.tensor.matmul(ps[:, 2 * c + k // 8, (k % 8) * KEYS:(k % 8 + 1) * KEYS],
                                            wqT[:, k, c * P:(c + 1) * P], keysT[:, k, :], start=True, stop=True)
                last.then_inc(psum_ready, 1)

        @block.vector
        def _(dve):
            for half in range(2):
                rows = slice(half * KEYS, (half + 1) * KEYS)
                own = g.ident[rows, rows]
                wide = own.unsqueeze(2) if half == 0 else own.unsqueeze(1)
                nc.vector.tensor_copy(spread[rows, :].rearrange("p (i j) -> p i j", i=KEYS),
                                      wide.broadcast_to([KEYS, KEYS, KEYS])).then_inc(spread_made, 1)
            for c in range(DC):
                dve.wait_ge(psum_ready, c + 1)
                nc.vector.tensor_copy(sim_w[:, c, :], ps[:, 2 * c:2 * c + 2, :].rearrange("p b n -> p (b n)"))\
                    .then_inc(made, 1)


def causal_attention_block(nc, g, dram, inner):
    GROUPS = B * NKV
    g.q_parts = nc.dram_tensor("q_parts", (PARTS, B * NH * HEAD, S), F32).ap()
    g.k_parts = nc.dram_tensor("k_parts", (PARTS, GROUPS * HEAD, S), F32).ap()
    with ExitStack() as ctx:
        st = Stage(nc, ctx, "cb")
        values = st.sb("values", [P, GROUPS, TB, HEAD + 1])
        attended = st.sb("attended", [P, B * NH, TB, HEAD])
        project_heads(nc, g, dram, inner, values)
        attend_heads(nc, g, dram, values, attended)
        project_attended(nc, g, dram, inner, attended)


HEAD, NKV = 16, 4
QKV = (NH + 2 * NKV) * HEAD
QK = (NH + NKV) * HEAD
PARTS = 3
STACK = 2 + PARTS * HEAD


def project_heads(nc, g, dram, inner, values):
    HALF = HEAD // 2
    heads = NH + NKV
    QC = NH * HEAD // P
    KROWS = NKV * HEAD
    STORES = 2 * PARTS
    ps = g.ps
    with ExitStack() as ctx:
        st = Stage(nc, ctx, "ph")
        wqkv, gain = st.sb("wqkv", [P, DC, QKV]), st.sb("gain", [P, DC])
        cos, sin = st.sb("cos", [P, TB, HALF]), st.sb("sin", [P, TB, HALF])
        norm, norm2 = Norm(nc, g, st), Norm(nc, g, st, "2")
        xn, xT = st.sb("xn", [P, TILES, D]), st.sb("xT", [P, 2, DC, P])
        qkv, turned = st.sb("qkv", [P, 2, QKV]), st.sb("turned", [P, 2, QK])
        prods = [st.sb(f"prod{n}", [P, heads, HALF]) for n in range(4)]
        qkT = st.sb("qkT", [P, 2, 2, QC + 1, GROUP], F32R)
        loaded, inner_ready, prods_ready = (
            st.sem(n) for n in ("loaded", "inner_ready", "prods_ready"))
        xn_ready, xT_psum_ready, xT_ready, qkv_psum_ready, qkv_ready, values_ready, turned_ready, qkT_psum_ready, \
            high_ready, qkT_ready, ones_ready = (st.sem(n) for n in (
                "xn_ready", "xT_psum_ready", "xT_ready", "qkv_psum_ready", "qkv_ready", "values_ready", "turned_ready",
                "qkT_psum_ready", "high_ready", "qkT_ready", "ones_ready"))
        stored = [st.sem(f"stored{n}") for n in range(2)]
        XT, QP, TP = 0, 2, 4
        pieces = [(P, slice(0, QC)), (KROWS, slice(QC, QC + 1))]
        block = st.block()

        def qkT_psum(t):
            return ps[:, TP + t % 2, 0:(QC + 1) * P].rearrange("p (c n) -> p c n", n=P)

        @block.sync
        def _(sp):
            sp.dma_start(wqkv[:], dram["L3_ffn_wqkvT"].rearrange("(c p) n -> p c n", p=P)).then_inc(loaded, 16)
            sp.dma_start(gain[:], dram["L3_ffn_ln1"]).then_inc(loaded, 16)
            sp.dma_start(cos[:], dram["rope_cos"].rearrange("(t p) n -> p t n", p=P)).then_inc(loaded, 16)
            sp.dma_start(sin[:], dram["rope_sin"].rearrange("(t p) n -> p t n", p=P)).then_inc(loaded, 16)
            for group in range(NG):
                b, slot, first = group * TPG // TB, group % 2, group * TPG % TB
                tokens = slice(first * P, (first + TPG) * P)
                sp.wait_ge(qkT_ready, (group + 1) * TPG)
                for row, (q_part, k_part) in enumerate(((0, 0), (0, 1), (1, 0))):
                    sp.dma_start(g.q_parts[row, b * QC * P:(b + 1) * QC * P, tokens].rearrange("(c p) n -> p c n", p=P),
                                 qkT[:, slot, q_part, 0:QC, :].bitcast(F32)).then_inc(stored[slot], 16)
                    sp.dma_start(g.k_parts[row, b * KROWS:(b + 1) * KROWS, tokens],
                                 qkT[0:KROWS, slot, k_part, QC, :].bitcast(F32)).then_inc(stored[slot], 16)
            for slot in range(2):
                sp.wait_ge(stored[slot], 16 * STORES * (NG // 2))

        @block.tensor
        def _(pe):
            def turn_x(t):
                pe.wait_ge(xn_ready, t + 1)
                if t >= 2:
                    pe.wait_ge(xT_ready, t - 1)
                for c in range(DC):
                    last = nc.tensor.transpose(ps[:, XT + t % 2, c * P:(c + 1) * P], xn[:, t, c * P:(c + 1) * P], g.ident[:])
                last.then_inc(xT_psum_ready, 1)

            def turn_heads(t):
                pe.wait_ge(turned_ready, t + 1)
                if t >= 2:
                    pe.wait_ge(qkT_ready, t - 1)
                for c in range(QC + 1):
                    rows = min(P, QK - c * P)
                    last = nc.tensor.transpose(qkT_psum(t)[0:rows, c], turned[:, t % 2, c * P:c * P + rows], g.ident[:])
                last.then_inc(qkT_psum_ready, 1)

            pe.wait_ge(loaded, 64)
            turn_x(0)
            for t in range(TILES):
                if t < TILES - 1:
                    turn_x(t + 1)
                pe.wait_ge(xT_ready, t + 1)
                if t >= 2:
                    pe.wait_ge(qkv_ready, t - 1)
                for c in range(DC):
                    last = nc.tensor.matmul(ps[:, QP + t % 2, 0:QKV], xT[:, t % 2, c, :], wqkv[:, c, :],
                                            start=(c == 0), stop=(c == DC - 1))
                last.then_inc(qkv_psum_ready, 1)
                if t >= 1:
                    turn_heads(t - 1)
            turn_heads(TILES - 1)

        @block.gpsimd
        def _(pool):
            nc.gpsimd.memset(values[:], 1.0).then_inc(ones_ready, 1)
            norm.gpsimd(pool)
            norm2.gpsimd(pool)

        @block.scalar
        def _(act):
            def high_part(t):
                act.wait_ge(qkT_psum_ready, t + 1)
                group, cols = t // TPG, slice(t % TPG * P, (t % TPG + 1) * P)
                if group >= 2:
                    act.wait_ge(stored[group % 2], 16 * STORES * (group // 2))
                for rows, c in pieces:
                    last = nc.scalar.activation(qkT[0:rows, group % 2, 0, c, cols], qkT_psum(t)[0:rows, c], ACT.Copy,
                                                scale=HEAD ** -0.25)
                last.then_inc(high_ready, 1)

            act.wait_ge(loaded, 64)
            for t in range(TILES):
                act.wait_ge(xT_psum_ready, t + 1)
                if t >= 2:
                    act.wait_ge(qkv_psum_ready, t - 1)
                for c in range(DC):
                    last = nc.scalar.activation(xT[:, t % 2, c, :], ps[:, XT + t % 2, c * P:(c + 1) * P], ACT.Copy,
                                                scale=gain[:, c:c + 1])
                last.then_inc(xT_ready, 1)
                act.wait_ge(qkv_psum_ready, t + 1)
                if t >= 2:
                    act.wait_ge(values_ready, t - 1)
                nc.scalar.activation(qkv[:, t % 2, :], ps[:, QP + t % 2, 0:QKV], ACT.Copy).then_inc(qkv_ready, 1)
                if t >= 1:
                    high_part(t - 1)
            high_part(TILES - 1)

        @block.vector
        def _(dve):
            def low_part(t):
                group, cols = t // TPG, slice(t % TPG * P, (t % TPG + 1) * P)
                dve.wait_ge(high_ready, t + 1)
                for rows, c in pieces:
                    last = nc.vector.scalar_tensor_tensor(out=qkT[0:rows, group % 2, 1, c, cols], in0=qkT_psum(t)[0:rows, c],
                                                          scalar=HEAD ** -0.25, in1=qkT[0:rows, group % 2, 0, c, cols].bitcast(F32),
                                                          op0=ALU.mult, op1=ALU.subtract)
                last.then_inc(qkT_ready, 1)

            norm.vector(dve, g.x, inner, "layer", inner_ready)
            dve.wait_ge(inner_ready, TILES)
            norm2.vector(dve, inner, xn, "rms", xn_ready)
            dve.wait_ge(loaded, 64)
            dve.wait_ge(ones_ready, 1)
            for t in range(TILES):
                b, own = t // TB, t % TB
                if t >= 1:
                    dve.wait_ge(turned_ready, t)
                dve.wait_ge(qkv_ready, t + 1)
                pair = qkv[:, t % 2, 0:QK].rearrange("p (h s n) -> p s h n", s=2, n=HALF)
                out = turned[:, t % 2, :].rearrange("p (h s n) -> p s h n", s=2, n=HALF)
                tables = [tab[:, own:own + 1, :].broadcast_to([P, heads, HALF]) for tab in (cos, sin)]
                for k, (half, table) in enumerate(((0, 0), (1, 1), (1, 0), (0, 1))):
                    last = nc.vector.tensor_tensor(prods[k][:], pair[:, half], tables[table], ALU.mult)
                last.then_inc(prods_ready, 1)
                nc.vector.tensor_copy(values[:, b * NKV:(b + 1) * NKV, own, 0:HEAD],
                                      qkv[:, t % 2, QK:].rearrange("p (h n) -> p h n", h=NKV)).then_inc(values_ready, 1)
                dve.wait_ge(prods_ready, t + 1)
                if t >= 2:
                    dve.wait_ge(qkT_psum_ready, t - 1)
                nc.vector.tensor_tensor(out[:, 0], prods[0][:], prods[1][:], ALU.subtract)
                nc.vector.tensor_tensor(out[:, 1], prods[2][:], prods[3][:], ALU.add).then_inc(turned_ready, 1)
                if t >= 1:
                    low_part(t - 1)
            low_part(TILES - 1)


def attend_heads(nc, g, dram, values, attended):
    HEADS, LEAD = B * NH, 4
    PAIRS = HEADS // 2
    ps = g.ps
    with ExitStack() as ctx:
        st = Stage(nc, ctx, "ah")
        max_q, max_k, q, k = (st.sb(n, [STACK, 2, S], F32R) for n in ("max_q", "max_k", "q", "k"))
        v = st.sb("v", [P, 2, TB, HEAD + 1])
        zeros = st.sb("zeros", [2, 2, S])
        lowest = st.sb("lowest", [P, 2, TB])
        lowestT = st.sb("lowestT", [TB, 2, 2, P], F32R)
        probs = st.sb("probs", [P, 2, S])
        out = st.sb("out", [HEAD + 1, S])
        share = st.sb("share", [P, TB])
        max_loaded = [st.sem(f"max_loaded{n}") for n in range(2)]
        head_loaded = [st.sem(f"head_loaded{n}") for n in range(2)]
        zeroed, rows_set, alone, pe_alone = (st.sem(n) for n in ("zeroed", "rows_set", "alone", "pe_alone"))
        max_scores_ready, max_done, lowest_psum_ready, lowest_high_ready, lowest_ready, v_ready, scores_ready, exp_done, \
            out_psum_ready, out_ready, turned_out_ready, share_ready, head_done = (st.sem(n) for n in (
                "max_scores_ready", "max_done", "lowest_psum_ready", "lowest_high_ready", "lowest_ready", "v_ready",
                "scores_ready", "exp_done", "out_psum_ready", "out_ready", "turned_out_ready", "share_ready", "head_done"))
        MX, TURN, SC, O = 0, 1, 2, 6
        FINISH_AT, TURN_AT = 4, 6
        block = st.block()

        def two_banks(first, rows=P):
            return ps[0:rows, first:first + 2, :].rearrange("p b n -> p (b n)")

        @block.tensor
        def _(pe):
            def max_scores(slot, i):
                for j in range(0, i + 1, 4):
                    cols = min(4, i + 1 - j) * P
                    diagonal = j + 4 > i
                    last = nc.tensor.matmul(ps[:, MX + j // 4, 0:cols], max_q[:, slot, i * P:(i + 1) * P],
                                            max_k[:, slot, j * P:j * P + cols], start=True, stop=not diagonal)
                    if diagonal:
                        last = nc.tensor.matmul(ps[:, MX + j // 4, cols - P:cols], g.identb[:], g.causal[:],
                                                start=False, stop=True)
                last.then_inc(max_scores_ready, 1)

            def scores(slot, j):
                for first, end in ([(j, 4), (4, TB)] if j < 4 else [(j, TB)]):
                    last = nc.tensor.matmul(two_banks(SC + 2 * (j % 2))[:, first * P:end * P], k[:, slot, j * P:(j + 1) * P],
                                            q[:, slot, first * P:end * P], start=True, stop=first != j)
                    if first == j:
                        last = nc.tensor.matmul(two_banks(SC + 2 * (j % 2))[:, j * P:(j + 1) * P], g.causal[:], g.identb[:],
                                                start=False, stop=True)
                last.then_inc(scores_ready, 1)

            def weigh(slot, j):
                for first, end in ([(j, 4), (4, TB)] if j < 4 else [(j, TB)]):
                    last = nc.tensor.matmul(two_banks(O, HEAD + 1)[:, first * P:end * P], v[:, slot, j, :],
                                            probs[:, j % 2, first * P:end * P], start=(j == 0), stop=(j == min(end, TB) - 1))
                return last

            def turn_lowest(n, slot):
                pe.wait_ge(max_done, TB * (n + 1))
                nc.tensor.transpose(ps[0:TB, TURN, 0:P], lowest[:, slot, :], g.ident[:]).then_inc(lowest_psum_ready, 1)

            def turn_out(h):
                pe.wait_ge(out_ready, h + 1)
                pe.sem_inc(pe_alone, 1)
                for i in range(TB):
                    last = nc.tensor.transpose(ps[:, TURN, i * (HEAD + 1):(i + 1) * (HEAD + 1)], out[:, i * P:(i + 1) * P],
                                               g.ident[0:HEAD + 1, 0:HEAD + 1])
                last.then_inc(turned_out_ready, 1)

            def weights_head(pair, slot, maxima=True, lowest_ahead=True, before=True, after=True):
                h = 2 * pair + slot
                for j in range(TB):
                    if j < TB - 1:
                        scores(slot, j + 1)
                    elif after:
                        pe.wait_ge(head_loaded[1 - slot], 64 * (pair + slot) + 64)
                        pe.wait_ge(exp_done, TB * h + TB - 1)
                        scores(1 - slot, 0)
                    if maxima:
                        if j == 0:
                            pe.wait_ge(max_loaded[slot], 32 * (pair + LEAD // 2) + 32)
                            pe.wait_ge(lowest_ready, h + LEAD - 1)
                        pe.wait_ge(max_done, TB * (h + LEAD) + j)
                        max_scores(slot, TB - 1 - j)
                    if before and j == FINISH_AT:
                        if not maxima:
                            pe.wait_ge(lowest_ready, min(h + LEAD - 1, HEADS))
                            pe.wait_ge(head_done, h - 1)
                        turn_out(h - 1)
                    if lowest_ahead and j == TURN_AT:
                        if before:
                            pe.wait_ge(head_done, h)
                        turn_lowest(h + LEAD - 1, 1 - slot)
                    pe.wait_ge(exp_done, TB * h + j + 1)
                    if j == 0:
                        pe.wait_ge(v_ready, h + 1)
                        if before:
                            pe.wait_ge(out_ready, h)
                    last = weigh(slot, j)
                last.then_inc(out_psum_ready, 1)

            pe.wait_ge(rows_set, 2)
            for h in range(LEAD):
                pe.wait_ge(max_loaded[h % 2], 32 * (h // 2) + 32)
                for n in range(TB):
                    if h or n:
                        pe.wait_ge(max_done, TB * h + n)
                    max_scores(h % 2, TB - 1 - n)
                    if h >= 1 and n == TURN_AT:
                        turn_lowest(h - 1, (h - 1) % 2)
            pe.wait_ge(rows_set, 3)
            pe.wait_ge(head_loaded[0], 64)
            scores(0, 0)
            weights_head(0, 0, before=False)
            weights_head(0, 1)
            with pe.Fori(1, PAIRS - 2) as pair:
                weights_head(pair, 0)
                weights_head(pair, 1)
            weights_head(PAIRS - 2, 0, maxima=False)
            weights_head(PAIRS - 2, 1, maxima=False, lowest_ahead=False)
            weights_head(PAIRS - 1, 0, maxima=False, lowest_ahead=False)
            weights_head(PAIRS - 1, 1, maxima=False, lowest_ahead=False, after=False)
            pe.wait_ge(head_done, HEADS - 1)
            turn_out(HEADS - 1)

        @block.gpsimd
        def _(pool):
            def load_for_max(h, slot):
                for stack, parts, n in ((max_q, g.q_parts, h), (max_k, g.k_parts, h // (NH // NKV))):
                    pool.dma_start(stack[2:, slot, :], parts[:, bass.ds(n * HEAD, HEAD), :])\
                        .then_inc(max_loaded[slot], 16)

            def load_for_weights(h, slot):
                for stack, parts, n in ((q, g.q_parts, h), (k, g.k_parts, h // (NH // NKV))):
                    pool.dma_start(stack[2:, slot, :], parts[:, bass.ds(n * HEAD, HEAD), :])\
                        .then_inc(head_loaded[slot], 16)

            def load_lowest(slot):
                for part in range(2):
                    pool.dma_start(q[part:part + 1, slot, :].rearrange("a (t n) -> a t n", n=P),
                                   lowestT[:, slot, part, :]).then_inc(head_loaded[slot], 16)

            def copy_values(h, slot):
                pool.sem_inc(alone, 1)
                nc.gpsimd.tensor_copy(v[:, slot].rearrange("p t n -> p (t n)"),
                                      values[:, bass.ds(h // (NH // NKV), 1)].rearrange("p a t n -> p (a t n)"))\
                    .then_inc(v_ready, 1)

            def body(pair, max_ahead=True):
                for slot in range(2):
                    pool.wait_ge(out_psum_ready, 2 * pair + slot + 1)
                    copy_values(2 * pair + slot + 2, slot)
                    load_for_weights(2 * pair + slot + 2, slot)
                    pool.wait_ge(lowest_ready, 2 * pair + slot + 3)
                    pool.sem_inc(alone, 1)
                    load_lowest(slot)
                    if max_ahead:
                        load_for_max(2 * pair + slot + LEAD + 2, slot)

            for slot in range(2):
                load_for_max(slot, slot)
            for slot in range(2):
                load_for_weights(slot, slot)
                copy_values(slot, slot)
            for h in range(2, LEAD + 2):
                pool.wait_ge(max_done, TB * (h - 1))
                load_for_max(h, h % 2)
                if h in (3, 4):
                    pool.wait_ge(lowest_ready, h - 2)
                    load_lowest(h - 3)
            with pool.Fori(0, PAIRS - 3) as pair:
                body(pair)
            body(PAIRS - 3, max_ahead=False)
            body(PAIRS - 2, max_ahead=False)

        @block.scalar
        def _(act):
            def high_part(n, slot, uses):
                act.wait_ge(lowest_psum_ready, n + 1)
                if uses is not None:
                    act.wait_ge(head_loaded[slot], 64 * uses)
                nc.scalar.activation(lowestT[:, slot, 0, :], ps[0:TB, TURN, 0:P], ACT.Copy).then_inc(lowest_high_ready, 1)

            def leave(h):
                act.wait_ge(out_psum_ready, h + 1)
                nc.scalar.activation(out[:], two_banks(O, HEAD + 1), ACT.Copy).then_inc(out_ready, 1)

            def weights_head(pair, slot, lowest_ahead=True, before=True):
                h = 2 * pair + slot
                for j in range(TB):
                    act.wait_ge(scores_ready, TB * h + j + 1)
                    nc.scalar.activation(probs[:, j % 2, j * P:], two_banks(SC + 2 * (j % 2))[:, j * P:], ACT.Exp)\
                        .then_inc(exp_done, 1)
                    if before and j == 0:
                        leave(h - 1)
                    if lowest_ahead and j == TURN_AT:
                        high_part(h + LEAD - 1, 1 - slot, pair + 1 + slot)

            for n in range(LEAD - 1):
                high_part(n, n % 2, 1 if n == 2 else None)
            weights_head(0, 0, before=False)
            weights_head(0, 1)
            with act.Fori(1, PAIRS - 2) as pair:
                weights_head(pair, 0)
                weights_head(pair, 1)
            weights_head(PAIRS - 2, 0)
            for h in range(HEADS - 3, HEADS):
                weights_head(h // 2, h % 2, lowest_ahead=False)
            leave(HEADS - 1)

        @block.vector
        def _(dve):
            def maximum(h, n, slot, i):
                dve.wait_ge(max_scores_ready, TB * h + n + 1)
                nc.vector.tensor_reduce(lowest[:, slot, i:i + 1], two_banks(MX)[:, 0:(i + 1) * P], AX_X, ALU.max, negate=True)\
                    .then_inc(max_done, 1)

            def low_part(n, slot):
                dve.wait_ge(lowest_high_ready, n + 1)
                nc.vector.tensor_tensor(lowestT[:, slot, 1, :], ps[0:TB, TURN, 0:P], lowestT[:, slot, 0, :].bitcast(F32), ALU.subtract)\
                    .then_inc(lowest_ready, 1)

            def finish(h):
                turned = ps[:, TURN, 0:TB * (HEAD + 1)].rearrange("p (t n) -> p t n", t=TB)
                dve.wait_ge(turned_out_ready, h + 1)
                nc.vector.reciprocal(share[:].unsqueeze(2), turned[:, :, HEAD:HEAD + 1]).then_inc(share_ready, 1)
                dve.wait_ge(share_ready, h + 1)
                nc.vector.tensor_tensor(attended[:, bass.ds(h, 1)].rearrange("p a t n -> p (a t) n"), turned[:, :, 0:HEAD],
                                        share[:].unsqueeze(2).broadcast_to([P, TB, HEAD]), ALU.mult).then_inc(head_done, 1)

            def weights_head(pair, slot, maxima=True, lowest_ahead=True, before=True):
                h = 2 * pair + slot
                for j in range(TB):
                    if maxima:
                        maximum(h + LEAD, j, slot, TB - 1 - j)
                    if before and j == FINISH_AT:
                        finish(h - 1)
                    if lowest_ahead and j == TURN_AT:
                        low_part(h + LEAD - 1, 1 - slot)

            nc.vector.memset(zeros[:], 0.0).then_inc(zeroed, 1)
            dve.wait_ge(zeroed, 1)
            for rows, value in ((max_q, 0.0), (max_k, 1.0), (k, 1.0)):
                nc.vector.tensor_scalar(rows[0:2], zeros[:], value, None, ALU.add).then_inc(rows_set, 1)
            for h in range(LEAD):
                for n in range(TB):
                    maximum(h, n, h % 2, TB - 1 - n)
                    if h >= 1 and n == TURN_AT:
                        low_part(h - 1, (h - 1) % 2)
            weights_head(0, 0, before=False)
            weights_head(0, 1)
            with dve.Fori(1, PAIRS - 2) as pair:
                weights_head(pair, 0)
                weights_head(pair, 1)
            weights_head(PAIRS - 2, 0, maxima=False)
            for h in range(HEADS - 3, HEADS):
                weights_head(h // 2, h % 2, maxima=False, lowest_ahead=False)
            finish(HEADS - 1)


def project_attended(nc, g, dram, inner, attended):
    ps = g.ps
    with ExitStack() as ctx:
        st = Stage(nc, ctx, "pa")
        wo = st.sb("wo", [P, DC, D])
        row, rowT = st.sb("row", [P, 2, D]), st.sb("rowT", [P, 2, DC, P])
        wo_loaded, row_ready, rowT_psum_ready, rowT_ready, y_ready, tile_done = (st.sem(n) for n in (
            "wo_loaded", "row_ready", "rowT_psum_ready", "rowT_ready", "y_ready", "tile_done"))
        RT, Y = 0, 2
        block = st.block()

        @block.sync
        def _(sp):
            sp.dma_start(wo[:], dram["L3_ffn_woT"].rearrange("(c p) n -> p c n", p=P)).then_inc(wo_loaded, 16)

        @block.gpsimd
        def _(pool):
            for t in range(TILES):
                b, own = t // TB, t % TB
                if t >= 2:
                    pool.wait_ge(rowT_psum_ready, t - 1)
                nc.gpsimd.tensor_copy(row[:, t % 2, :].rearrange("p (h n) -> p h n", n=HEAD),
                                      attended[:, b * NH:(b + 1) * NH, own, :]).then_inc(row_ready, 1)

        @block.tensor
        def _(pe):
            def turn(t):
                pe.wait_ge(row_ready, t + 1)
                for c in range(DC):
                    last = nc.tensor.transpose(ps[:, RT + t % 2, c * P:(c + 1) * P], row[:, t % 2, c * P:(c + 1) * P], g.ident[:])
                last.then_inc(rowT_psum_ready, 1)

            pe.wait_ge(wo_loaded, 16)
            turn(0)
            for t in range(TILES):
                if t < TILES - 1:
                    turn(t + 1)
                pe.wait_ge(rowT_ready, t + 1)
                if t >= 2:
                    pe.wait_ge(tile_done, t - 1)
                for c in range(DC):
                    last = nc.tensor.matmul(ps[:, Y + t % 2, 0:D], rowT[:, t % 2, c, :], wo[:, c, :],
                                            start=(c == 0), stop=(c == DC - 1))
                last.then_inc(y_ready, 1)

        @block.scalar
        def _(act):
            for t in range(TILES):
                act.wait_ge(rowT_psum_ready, t + 1)
                if t >= 2:
                    act.wait_ge(y_ready, t - 1)
                nc.scalar.activation(rowT[:, t % 2].rearrange("p c n -> p (c n)"), ps[:, RT + t % 2, 0:D], ACT.Copy)\
                    .then_inc(rowT_ready, 1)

        @block.vector
        def _(dve):
            for t in range(TILES):
                dve.wait_ge(y_ready, t + 1)
                nc.vector.tensor_tensor(inner[:, t, :], inner[:, t, :], ps[:, Y + t % 2, 0:D], ALU.add).then_inc(tile_done, 1)


def transformer_layer_3(nc, g, dram):
    with ExitStack() as ctx:
        st = Stage(nc, ctx, "m3")
        inner = st.sb("inner", [P, TILES, D])
        causal_attention_block(nc, g, dram, inner)
        mixture(nc, g, dram, 3, inner, inner)
        add_gated(nc, g, inner, 3)


class Shared:
    pass


def attention_layer(layer):
    def stage(nc, g, dram):
        cross_attention(nc, g, dram, layer)
    return stage


STAGES = [(1, linear_attention), (2, sign_network), (3, attention_layer(1)), (4, expert_layer_1), (5, attention_layer(2)), (6, product_key_experts), (7, attention_layer(3)),
          (8, transformer_layer_3)]


def build(nc, dram, out, upto=99):
    with ExitStack() as ctx:
        g = Shared()
        st = Stage(nc, ctx, "g")
        g.x = st.sb("x", [P, TILES, D])
        g.gates = st.sb("gates", [P, 16])
        g.ident = st.sb("ident", [P, P])
        g.identb = st.sb("identb", [P, P], BF16)
        g.minus_half = st.sb("minus_half", [P, 2])
        g.ones = st.sb("ones", [P, P])
        g.causal = st.sb("causal", [P, P], BF16)
        g.ps = ctx.enter_context(nc.psum_tensor("ps", [P, 8, 512], F32))
        load_stream(nc, g, dram)
        for n, stage in STAGES:
            if n <= upto:
                stage(nc, g, dram)
        store_stream(nc, g, out)


def expert_chunks(gate, up, down):
    n = gate.shape[1] // P
    left = [w.reshape(DC, P, n, P).transpose(2, 1, 0, 3).reshape(n, P, DC * P) for w in (gate, up)]
    return np.concatenate([*left, down.reshape(n, P, D)], axis=2)


def expert_selector(experts, hidden):
    return np.tile(np.kron(np.eye(experts), np.ones((1, hidden))), (3, 1)).astype(mybir.dt.np(BF16))


def lay_out(v):
    a = {k: np.asarray(x) for k, x in v.items()}
    a["ctxT"] = a["ctx_1024"].transpose(2, 0, 1).reshape(D, B * NKEY)
    a["L0_xattn_WqT"] = a["L0_xattn_Wq"].T
    a["maskT_ff1"] = a["mask_BxS2x1_ff1"][:, :, 0].T
    for n in (1, 2):
        a[f"L{n}_xattn_WqT"] = a[f"L{n}_xattn_Wq"].reshape(D, NH, D // NH).transpose(2, 1, 0)
        a[f"L{n}_xattn_bias"] = np.stack([a[f"L{n}_xattn_b{w}"].reshape(NH, D // NH) for w in "qkv"]).transpose(2, 0, 1)
    a["L3_xattn_WqT"] = a["L3_xattn_w_q"].reshape(D, NH, -1).transpose(2, 1, 0)
    a["L3_xattn_Wk"], a["L3_xattn_Wv"] = np.split(a["L3_xattn_w_kv"], 2, axis=1)
    a["L3_xattn_Wo"], a["L3_xattn_bo"] = a["L3_xattn_w_out"], a["L3_xattn_b_out"]
    a["L3_xattn_affine"] = np.stack([a["L3_xattn_ln_gamma"], a["L3_xattn_ln_beta"]]).reshape(2, DC, P).transpose(2, 0, 1)
    a["L1_xattn_mask"], a["L2_xattn_mask"] = a["mask_Bx1x1xS2_fk0"][:, 0, 0], a["mask_BxS2_ik0"]
    used = [f"L{n}_xattn_{w}" for n in (1, 2, 3) for w in ("WqT", "Wk", "Wv", "Wo", "bo")]
    used += ["L1_xattn_bias", "L2_xattn_bias", "L1_xattn_mask", "L2_xattn_mask", "L3_xattn_affine"]
    for n in range(3):
        a[f"L0_ffn_s{n}"] = a[f"L0_ffn_s{n}"].reshape(1)
        used += [f"L0_ffn_k{n}", f"L0_ffn_s{n}"]
    e, _, f = a["L1_ffn_Wg"].shape
    a["L1_moe_w"] = expert_chunks(a["L1_ffn_Wg"].transpose(1, 0, 2).reshape(D, e * f),
                                  a["L1_ffn_Wu"].transpose(1, 0, 2).reshape(D, e * f), a["L1_ffn_Wd"].reshape(e * f, D))
    a["L1_moe_sel"], a["L1_moe_router"] = expert_selector(e, f), a["L1_ffn_Ws"]
    f = a["L3_ffn_w2"].shape[2]
    gate, up = a["L3_ffn_w13"][:, :f], a["L3_ffn_w13"][:, f:]
    a["L3_moe_w"] = expert_chunks(gate.reshape(e * f, D).T, up.reshape(e * f, D).T,
                                  a["L3_ffn_w2"].transpose(0, 2, 1).reshape(e * f, D))
    a["L3_moe_sel"], a["L3_moe_router"] = expert_selector(e, f), a["L3_ffn_gate_w"].T
    a["L3_ffn_ln2"] = a["L3_ffn_ln2_w"].reshape(DC, P).T
    a["iota8"] = np.arange(8, dtype=np.float32)
    used += ["L1_moe_w", "L1_moe_sel", "L1_moe_router", "L1_ffn_bs", "L3_moe_w", "L3_moe_sel", "L3_moe_router",
             "L3_ffn_ln2", "iota8"]
    a["L2_ffn_wqT"] = a["L2_ffn_wq"].reshape(D, 16, P).transpose(2, 1, 0)
    a["L2_ffn_keysT"] = a["L2_ffn_keys"].transpose(3, 0, 2, 1).reshape(P, 16, 64)
    a["L2_ffn_downT"] = a["L2_ffn_expert_down"].T
    a["L2_ffn_norm"] = a["L2_ffn_norm_w"].reshape(DC, P).T
    used += ["L2_ffn_wqT", "L2_ffn_keysT", "L2_ffn_downT", "L2_ffn_norm", "L2_ffn_expert_up"]
    a["L3_ffn_wqkvT"], a["L3_ffn_woT"] = a["L3_ffn_wqkv"].T, a["L3_ffn_wo"].T
    a["L3_ffn_ln1"] = a["L3_ffn_ln1_w"].reshape(DC, P).T
    freq = np.float32(1.0) / np.float32(10000.0) ** (np.arange(0, HEAD, 2, dtype=np.float32) / np.float32(HEAD))
    angle = np.arange(S, dtype=np.float32)[:, None] * freq[None, :]
    a["rope_cos"], a["rope_sin"] = np.cos(angle), np.sin(angle)
    used += ["L3_ffn_wqkvT", "L3_ffn_woT", "L3_ffn_ln1", "rope_cos", "rope_sin"]
    used += ["x", "g_xattn", "g_ffn", "L3_xattn_gate", "ctxT", "maskT_ff1",
            "L0_xattn_Wk", "L0_xattn_Wv", "L0_xattn_Wo", "L0_xattn_WqT"]
    return {k: np.ascontiguousarray(a[k]) for k in used}


def kernel(**inputs):
    import concourse.bacc as bacc
    from concourse.bass_utils import run_bass_kernel_spmd

    nc = bacc.Bacc("TRN2", target_bir_lowering=False, num_devices=1)
    arrays = lay_out(inputs)
    dram = {k: nc.dram_tensor(f"in_{k}", a.shape, mybir.dt.from_np(a.dtype), kind="ExternalInput").ap()
            for k, a in arrays.items()}
    out = nc.dram_tensor("out_x", (B, S, D), F32, kind="ExternalOutput").ap()
    build(nc, dram, out)
    r = run_bass_kernel_spmd(nc, [{f"in_{k}": a for k, a in arrays.items()}], core_ids=[0])
    return r.results[0]["out_x"]
```
